# Optimizing a Trainium2 kernel written in Bass

```python
import numpy as np
import jax
import jax.numpy as jnp

def _softmax(x, axis=-1):
    return jax.nn.softmax(x, axis=axis)

def _gelu(x):
    return jax.nn.gelu(x, approximate=True)

def _silu(x):
    return jax.nn.silu(x)

def _sigmoid(x):
    return jax.nn.sigmoid(x)

def _layernorm(x, axis=-1, eps=1e-05):
    m = jnp.mean(x, axis=axis, keepdims=True)
    v = jnp.var(x, axis=axis, keepdims=True)
    return (x - m) / jnp.sqrt(v + eps)

def _scatter_add(tgt, idx, src, axis=0):
    return tgt.at[idx].add(src)

def _segment_sum(src, seg, n):
    return jax.ops.segment_sum(src, seg, n)
kernel_name = 'mk_xattn_ffn_d2_seqx_r4_f47372'

def setup_inputs(seed: int=0):
    np.random.seed(seed)
    _w = jnp.asarray

    def _rec_inputs():
        import jax
        import jax.numpy as jnp
        _rk = jax.random.key(seed)
        x = 7.22e-05 + 1 * jax.random.normal(jax.random.fold_in(_rk, 1), (4, 512, 512), jnp.float32)
        _lenS = 512 - jax.random.randint(jax.random.fold_in(_rk, 7), (4,), 0, max(1, 512 // 4) + 1, jnp.int32)
        _lenS2 = 512 - jax.random.randint(jax.random.fold_in(_rk, 8), (4,), 0, max(1, 512 // 4) + 1, jnp.int32)
        _ctx_1024P = jax.random.normal(jax.random.fold_in(_rk, 11), (4, 16, 256), jnp.float32)
        _ctx_1024c = jax.random.dirichlet(jax.random.fold_in(_rk, 511), 0.3 * jnp.ones((16,), jnp.float32), (4, 512))
        _ctx_1024t = jnp.einsum('bsk,bkd->bsd', _ctx_1024c, _ctx_1024P)
        _ctx_1024t = _ctx_1024t * jax.lax.rsqrt(jnp.mean(jnp.square(_ctx_1024t)) + 1e-12) * 0.953939
        ctx_1024 = 2.81802e-05 + 1.00001 * (_ctx_1024t + 0.3 * jax.random.normal(jax.random.fold_in(_rk, 611), (4, 512, 256), jnp.float32))
        _validS = jnp.arange(512)[None, :] < _lenS[:, None]
        _validS2 = jnp.arange(512)[None, :] < _lenS2[:, None]
        _causal = jnp.tril(jnp.ones((512, 512), dtype=bool))
        mask_BxS2_bf1 = jnp.ones((4, 512), dtype=bool)
        return (x, ctx_1024, mask_BxS2_bf1)
    x, ctx_1024, mask_BxS2_bf1 = _rec_inputs()

    def _L0_xattn_setup():
        import jax, jax.numpy as jnp
        import numpy as np
        key = jax.random.key(seed)
        ks = jax.random.split(key, 6)
        B, L, N, C, D = (8, 128, 512, 256, 128)
        return {'teacher_logits': jax.random.normal(ks[0], (B, L, N), dtype=jnp.float32), 'teacher_features': jax.random.normal(ks[1], (B, N, C), dtype=jnp.float32), 'Wq': jax.random.normal(ks[2], (D, C), dtype=jnp.float32) * (1.0 / np.sqrt(C)), 'bq': jnp.zeros((D,), dtype=jnp.float32), 'Wk': jax.random.normal(ks[3], (D, C), dtype=jnp.float32) * (1.0 / np.sqrt(C)), 'bk': jnp.zeros((D,), dtype=jnp.float32)}
    _L0_xattn_all = _L0_xattn_setup()
    _L0_xattn_in = {k: v for k, v in _L0_xattn_all.items() if k in ('Wq', 'bq', 'Wk', 'bk')}
    del _L0_xattn_all

    def _L0_ffn_setup():
        import jax, jax.numpy as jnp
        import numpy as np
        B, T, C = (2, 256, 512)
        E, TOPK = (8, 2)
        F_MOE = 352
        F_SHARED = 1408
        key = jax.random.key(seed)
        ks = jax.random.split(key, 9)
        s = 0.02
        return {'x': jax.random.normal(ks[0], (B, T, C), dtype=jnp.float32), 'gate_w': jax.random.normal(ks[1], (E, C), dtype=jnp.float32) * s, 'expert_fc1': jax.random.normal(ks[2], (E, F_MOE, C), dtype=jnp.float32) * s, 'expert_fc2': jax.random.normal(ks[3], (E, F_MOE, C), dtype=jnp.float32) * s, 'expert_proj': jax.random.normal(ks[4], (E, C, F_MOE), dtype=jnp.float32) * s, 'shared_fc1': jax.random.normal(ks[5], (F_SHARED, C), dtype=jnp.float32) * s, 'shared_fc2': jax.random.normal(ks[6], (F_SHARED, C), dtype=jnp.float32) * s, 'shared_proj': jax.random.normal(ks[7], (C, F_SHARED), dtype=jnp.float32) * s, 'shared_gate_w': jax.random.normal(ks[8], (1, C), dtype=jnp.float32) * s}
    _L0_ffn_all = _L0_ffn_setup()
    _L0_ffn_in = {k: v for k, v in _L0_ffn_all.items() if k in ('gate_w', 'expert_fc1', 'expert_fc2', 'expert_proj', 'shared_fc1', 'shared_fc2', 'shared_proj', 'shared_gate_w')}
    del _L0_ffn_all

    def _L1_xattn_setup():
        import jax, jax.numpy as jnp
        import numpy as np
        N_HEADS = 16
        N_KV_HEADS = 8
        HEAD_DIM = 128
        D_TEXT = 512
        D_VISION = 256
        GROUPS = N_HEADS // N_KV_HEADS
        key = jax.random.key(seed)
        ks = jax.random.split(key, 6)
        B, T_text, T_vis = (4, 512, 144)
        text_hidden = jax.random.normal(ks[0], (B, T_text, D_TEXT), dtype=jnp.float32)
        vision_tokens = jax.random.normal(ks[1], (B, T_vis, D_VISION), dtype=jnp.float32)
        vision_mask = jnp.ones((B, T_vis), dtype=bool)
        s = 0.02
        Wq = jax.random.normal(ks[2], (D_TEXT, N_HEADS * HEAD_DIM), dtype=jnp.float32) * s
        Wk = jax.random.normal(ks[3], (D_VISION, N_KV_HEADS * HEAD_DIM), dtype=jnp.float32) * s
        Wv = jax.random.normal(ks[4], (D_VISION, N_KV_HEADS * HEAD_DIM), dtype=jnp.float32) * s
        Wo = jax.random.normal(ks[5], (N_HEADS * HEAD_DIM, D_TEXT), dtype=jnp.float32) * s
        return {'text_hidden': text_hidden, 'vision_tokens': vision_tokens, 'vision_mask': vision_mask, 'Wq': Wq, 'Wk': Wk, 'Wv': Wv, 'Wo': Wo}
    _L1_xattn_all = _L1_xattn_setup()
    _L1_xattn_in = {k: v for k, v in _L1_xattn_all.items() if k in ('Wq', 'Wk', 'Wv', 'Wo')}
    del _L1_xattn_all

    def _L1_ffn_setup():
        import jax, jax.numpy as jnp
        import numpy as np
        HIDDEN = 512
        INTER = 2048
        SCALE = 64.0

        def fwht(x):
            orig_shape = x.shape
            n = orig_shape[-1]
            x = x.reshape(-1, n)
            h = 1
            while h < n:
                x = x.reshape(-1, n // (2 * h), 2, h)
                a, b = (x[:, :, 0, :], x[:, :, 1, :])
                x = jnp.stack([a + b, a - b], axis=2).reshape(-1, n)
                h *= 2
            return (x / jnp.sqrt(jnp.asarray(n, x.dtype))).reshape(orig_shape)
        key = jax.random.key(seed)
        ks = jax.random.split(key, 8)
        inp = jax.random.normal(ks[0], (4, 512, HIDDEN), dtype=jnp.float32)
        SU_ug = jnp.where(jax.random.bernoulli(ks[1], 0.5, (HIDDEN,)), 1.0, -1.0).astype(jnp.float32)
        SU_dp = jnp.where(jax.random.bernoulli(ks[2], 0.5, (INTER,)), 1.0, -1.0).astype(jnp.float32)
        Wscale_ug = jax.random.uniform(ks[3], (2 * INTER,), jnp.float32, 0.5, 1.5)
        Wscale_dp = jax.random.uniform(ks[4], (HIDDEN,), jnp.float32, 0.5, 1.5)
        W_up = jax.random.normal(ks[5], (INTER, HIDDEN), dtype=jnp.float32) * 0.02
        W_gate = jax.random.normal(ks[6], (INTER, HIDDEN), dtype=jnp.float32) * 0.02
        W_down = jax.random.normal(ks[7], (HIDDEN, INTER), dtype=jnp.float32) * 0.02
        return {'input': inp, 'SU_ug': SU_ug, 'SU_dp': SU_dp, 'Wscale_ug': Wscale_ug, 'Wscale_dp': Wscale_dp, 'W_up': W_up, 'W_gate': W_gate, 'W_down': W_down}
    _L1_ffn_all = _L1_ffn_setup()
    _L1_ffn_in = {k: v for k, v in _L1_ffn_all.items() if k in ('SU_ug', 'SU_dp', 'Wscale_ug', 'Wscale_dp', 'W_up', 'W_gate', 'W_down')}
    del _L1_ffn_all
    return {'x': x, 'ctx_1024': ctx_1024, 'mask_BxS2_bf1': mask_BxS2_bf1, 'L0_xattn_Wq': _L0_xattn_in['Wq'], 'L0_xattn_bq': _L0_xattn_in['bq'], 'L0_xattn_Wk': _L0_xattn_in['Wk'], 'L0_xattn_bk': _L0_xattn_in['bk'], 'L0_ffn_gate_w': _L0_ffn_in['gate_w'], 'L0_ffn_expert_fc1': _L0_ffn_in['expert_fc1'], 'L0_ffn_expert_fc2': _L0_ffn_in['expert_fc2'], 'L0_ffn_expert_proj': _L0_ffn_in['expert_proj'], 'L0_ffn_shared_fc1': _L0_ffn_in['shared_fc1'], 'L0_ffn_shared_fc2': _L0_ffn_in['shared_fc2'], 'L0_ffn_shared_proj': _L0_ffn_in['shared_proj'], 'L0_ffn_shared_gate_w': _L0_ffn_in['shared_gate_w'], 'L1_xattn_Wq': _L1_xattn_in['Wq'], 'L1_xattn_Wk': _L1_xattn_in['Wk'], 'L1_xattn_Wv': _L1_xattn_in['Wv'], 'L1_xattn_Wo': _L1_xattn_in['Wo'], 'L1_ffn_SU_ug': _L1_ffn_in['SU_ug'], 'L1_ffn_SU_dp': _L1_ffn_in['SU_dp'], 'L1_ffn_Wscale_ug': _L1_ffn_in['Wscale_ug'], 'L1_ffn_Wscale_dp': _L1_ffn_in['Wscale_dp'], 'L1_ffn_W_up': _L1_ffn_in['W_up'], 'L1_ffn_W_gate': _L1_ffn_in['W_gate'], 'L1_ffn_W_down': _L1_ffn_in['W_down']}

def reference(x, ctx_1024, mask_BxS2_bf1, L0_xattn_Wq, L0_xattn_bq, L0_xattn_Wk, L0_xattn_bk, L0_ffn_gate_w, L0_ffn_expert_fc1, L0_ffn_expert_fc2, L0_ffn_expert_proj, L0_ffn_shared_fc1, L0_ffn_shared_fc2, L0_ffn_shared_proj, L0_ffn_shared_gate_w, L1_xattn_Wq, L1_xattn_Wk, L1_xattn_Wv, L1_xattn_Wo, L1_ffn_SU_ug, L1_ffn_SU_dp, L1_ffn_Wscale_ug, L1_ffn_Wscale_dp, L1_ffn_W_up, L1_ffn_W_gate, L1_ffn_W_down):
    import jax
    import jax.numpy as jnp

    def _L0_xattn_ref(teacher_logits, teacher_features, Wq, bq, Wk, bk):
        import jax, jax.numpy as jnp
        import numpy as np
        query = jnp.einsum('bnc,dc->bnd', teacher_features, Wq) + bq
        key = jnp.einsum('bnc,dc->bnd', teacher_features, Wk) + bk
        energy = jnp.einsum('bnd,bmd->bnm', query, key)
        attention = jax.nn.softmax(energy, axis=-1)
        x_m = jnp.einsum('bln,bmn->blm', teacher_logits, attention)
        return x_m

    def _L0_ffn_ref(x, gate_w, expert_fc1, expert_fc2, expert_proj, shared_fc1, shared_fc2, shared_proj, shared_gate_w):
        import jax, jax.numpy as jnp
        import numpy as np
        B, T, C = (2, 256, 512)
        E, TOPK = (8, 2)
        F_MOE = 352
        F_SHARED = 1408
        b, t, c = x.shape
        xf = x.reshape(-1, c)
        n = xf.shape[0]
        router = xf @ gate_w.T
        probs = jax.nn.softmax(router.astype(jnp.float32), axis=1).astype(x.dtype)
        top_p, top_i = jax.lax.top_k(probs, TOPK)
        combine = jnp.zeros((n, E), dtype=x.dtype).at[jnp.arange(n)[:, None], top_i].set(top_p)
        h1 = jnp.einsum('nc,efc->enf', xf, expert_fc1)
        h2 = jnp.einsum('nc,efc->enf', xf, expert_fc2)
        h = jax.nn.silu(h1) * h2
        out_e = jnp.einsum('enf,ecf->enc', h, expert_proj)
        y = jnp.einsum('ne,enc->nc', combine, out_e)
        s1 = xf @ shared_fc1.T
        s2 = xf @ shared_fc2.T
        shared = jax.nn.silu(s1) * s2 @ shared_proj.T
        y = y + jax.nn.sigmoid(xf @ shared_gate_w.T) * shared
        return y.reshape(b, t, c)

    def _L1_xattn_ref(text_hidden, vision_tokens, vision_mask, Wq, Wk, Wv, Wo):
        import jax, jax.numpy as jnp
        import numpy as np
        N_HEADS = 16
        N_KV_HEADS = 8
        HEAD_DIM = 128
        D_TEXT = 512
        D_VISION = 256
        GROUPS = N_HEADS // N_KV_HEADS
        B, T_text, _ = text_hidden.shape
        T_vis = vision_tokens.shape[1]
        scale = jnp.float32(np.sqrt(HEAD_DIM))
        q = (text_hidden @ Wq).reshape(B, T_text, N_HEADS, HEAD_DIM).transpose(0, 2, 1, 3)
        k = (vision_tokens @ Wk).reshape(B, T_vis, N_KV_HEADS, HEAD_DIM).transpose(0, 2, 1, 3)
        v = (vision_tokens @ Wv).reshape(B, T_vis, N_KV_HEADS, HEAD_DIM).transpose(0, 2, 1, 3)
        k = jnp.repeat(k, GROUPS, axis=1)
        v = jnp.repeat(v, GROUPS, axis=1)
        scores = jnp.einsum('bhtd,bhsd->bhts', q, k) / scale
        mask = vision_mask[:, None, None, :]
        scores = jnp.where(mask, scores, -jnp.inf)
        attn = jax.nn.softmax(scores, axis=-1)
        attn = jnp.nan_to_num(attn, nan=0.0)
        out = jnp.einsum('bhts,bhsd->bhtd', attn, v)
        out = out.transpose(0, 2, 1, 3).reshape(B, T_text, N_HEADS * HEAD_DIM)
        return out @ Wo

    def _L1_ffn_ref(input, SU_ug, SU_dp, Wscale_ug, Wscale_dp, W_up, W_gate, W_down):
        import jax, jax.numpy as jnp
        import numpy as np
        HIDDEN = 512
        INTER = 2048
        SCALE = 64.0

        def fwht(x):
            orig_shape = x.shape
            n = orig_shape[-1]
            x = x.reshape(-1, n)
            h = 1
            while h < n:
                x = x.reshape(-1, n // (2 * h), 2, h)
                a, b = (x[:, :, 0, :], x[:, :, 1, :])
                x = jnp.stack([a + b, a - b], axis=2).reshape(-1, n)
                h *= 2
            return (x / jnp.sqrt(jnp.asarray(n, x.dtype))).reshape(orig_shape)
        n = SU_ug.shape[0]
        x = input.reshape(-1, n)
        x = fwht(x * SU_ug) / SCALE
        x_up = x @ W_up.T * (Wscale_ug[:INTER] * SCALE)
        x_gate = x @ W_gate.T * (Wscale_ug[INTER:] * SCALE)
        x = jax.nn.silu(x_gate) * x_up
        x = fwht(x * SU_dp) / SCALE
        x = x @ W_down.T * (Wscale_dp * SCALE)
        return x.reshape(input.shape)
    x = x + _L0_xattn_ref(_layernorm(x, axis=-1), ctx_1024, L0_xattn_Wq, L0_xattn_bq, L0_xattn_Wk, L0_xattn_bk)
    x = x + _L0_ffn_ref(_layernorm(x, axis=-1), L0_ffn_gate_w, L0_ffn_expert_fc1, L0_ffn_expert_fc2, L0_ffn_expert_proj, L0_ffn_shared_fc1, L0_ffn_shared_fc2, L0_ffn_shared_proj, L0_ffn_shared_gate_w)
    x = x + _L1_xattn_ref(_layernorm(x, axis=-1), ctx_1024, mask_BxS2_bf1, L1_xattn_Wq, L1_xattn_Wk, L1_xattn_Wv, L1_xattn_Wo)
    x = x + _L1_ffn_ref(_layernorm(x, axis=-1), L1_ffn_SU_ug, L1_ffn_SU_dp, L1_ffn_Wscale_ug, L1_ffn_Wscale_dp, L1_ffn_W_up, L1_ffn_W_gate, L1_ffn_W_down)
    return x

_drawn_inputs = setup_inputs


def setup_inputs(seed=0):
    import zlib

    import numpy as np

    out = dict(_drawn_inputs(seed))
    spreads = {'L0_xattn_bq': (0.0, 0.1), 'L0_xattn_bk': (0.0, 0.1)}
    factors = {}
    for name, (base, spread) in spreads.items():
        noise = np.random.default_rng([zlib.crc32(name.encode()), seed]).standard_normal(out[name].shape)
        drawn = base * np.exp(spread * noise) if base else spread * noise
        out[name] = jnp.asarray(drawn.astype(out[name].dtype))
    for name, factor in factors.items():
        out[name] = (out[name] * factor).astype(out[name].dtype)
    return out
```

```python
from contextlib import ExitStack

import numpy as np

import concourse.bass as bass
from concourse import mybir

F32 = mybir.dt.float32
F32R = mybir.dt.float32r
U8 = mybir.dt.uint8
ALU = mybir.AluOpType
ACT = mybir.ActivationFunctionType
AX = mybir.AxisListType

P = 128
B, S, C = 4, 512, 512
CV = 256
TOK = B * S
NT = TOK // P
TT = S // P
KC = C // P
KV = CV // P
D = 128
E, F_MOE, F_SHARED = 8, 352, 1408
RG = E + 2
GROUPS, HPG = 8, 2
INTER = 2048
NF = INTER // P
EPS = 1e-5
MASKED = 3.0e38
WSLICE = 3 * C


class Chain:

    def __init__(self, eng, sem):
        self.eng, self.sem, self.n = eng, sem, 0

    def link(self, ins):
        ins.then_inc(self.sem, 1)
        self.n += 1
        self.eng.wait_ge(self.sem, self.n)


class Bag:
    pass


class Place:

    def __init__(self, n, bank):
        self.n, self.bank = n, bank


def f32(ap):
    return ap.bitcast(F32)


def product(pe, out, lhs, rhs, start, stop):
    (lh, ll), (rh, rl) = lhs, rhs
    pe.matmul(out, lh, rh, start=start, stop=False)
    pe.matmul(out, lh, rl, start=False, stop=False)
    return pe.matmul(out, ll, rh, start=False, stop=stop)


def ln_buffers(sb, ps, sem, xn=None):
    R = Bag()
    R.stats = sb("ln_stats", [P, NT, 6], F32)
    R.mv = sb("ln_mean_var", [P, NT, 2], F32)
    R.veps = sb("ln_var_eps", [P, NT], F32)
    R.rstd = sb("ln_rstd", [P, NT], F32)
    R.mhalf = sb("ln_minus_half", [P, TT], F32)
    R.xn = xn or [sb(f"ln_xn{i}", [P, C], F32) for i in range(2)]
    R.psT = [ps(f"ps_xnT{i}") for i in range(2)]
    R.chain = sem("ln_chain")
    R.stats_done = sem("ln_stats_done")
    R.pool_chain = sem("ln_pool_chain")
    R.rstd_ready = sem("ln_rstd_ready")
    R.xn_ready = sem("ln_xn_ready")
    R.xn_turned = sem("ln_xn_turned")
    R.hi_ready = sem("ln_hi_ready")
    R.xT_ready = sem("ln_xT_ready")
    return R


def ln_gpsimd(pool, R):
    ch = Chain(pool, R.pool_chain)
    ch.link(pool.memset(R.mhalf[:], -0.5))
    for b in range(B):
        t = slice(TT * b, TT * b + TT)
        pool.wait_ge(R.stats_done, b + 1)
        ch.link(pool.tensor_scalar(R.veps[:, t], R.mv[:, t, 1], EPS, None, ALU.add))
        pool.tensor_tensor(R.rstd[:, t], R.veps[:, t], R.mhalf[:], ALU.pow).then_inc(R.rstd_ready, 1)


def ln_vector(dve, R, x, dst, x_loaded=None, col_scale=None, after_lo=None):
    ch = Chain(dve, R.chain)

    def low(t):
        dve.wait_ge(R.hi_ready, t + 1)
        hi, lo = dst(t)
        dve.tensor_tensor(lo, R.psT[t % 2][:].rearrange("p (k n) -> p k n", k=KC), f32(hi),
                          ALU.subtract).then_inc(R.xT_ready, 1)
        if after_lo is not None:
            after_lo(t)

    for b in range(B + 1):
        if b < B:
            if x_loaded is not None:
                dve.wait_ge(x_loaded[b], 16)
            for t in range(TT * b, TT * b + TT):
                last = dve.bn_stats(R.stats[:, t, :], x[:, t, :])
                if t < TT * b + TT - 1:
                    last.then_inc(R.chain, 1)
                    ch.n += 1
            ch.link(last)
            for t in range(TT * b, TT * b + TT):
                last = dve.bn_aggr(R.mv[:, t, :], R.stats[:, t, :])
                last.then_inc(R.chain, 1)
                ch.n += 1
            dve.wait_ge(R.chain, ch.n)
            dve.sem_inc(R.stats_done, 1)
        if b >= 1:
            dve.wait_ge(R.rstd_ready, b)
            for t in range(TT * b - TT, TT * b):
                if t >= 2:
                    dve.wait_ge(R.xn_turned, t - 1)
                norm = dve.tensor_scalar(R.xn[t % 2][:], x[:, t, :], R.mv[:, t, 0:1], R.rstd[:, t:t + 1],
                                         ALU.subtract, ALU.mult)
                if col_scale is not None:
                    ch.link(norm)
                    norm = dve.tensor_tensor(R.xn[t % 2][:], R.xn[t % 2][:], col_scale, ALU.mult)
                norm.then_inc(R.xn_ready, 1)
                if t >= 1:
                    low(t - 1)
    low(NT - 1)


def ln_tensor(pe, R, ident, after=None):
    for t in range(NT):
        pe.wait_ge(R.xn_ready, t + 1)
        if t >= 2:
            pe.wait_ge(R.xT_ready, t - 1)
        for k in range(KC):
            last = pe.transpose(R.psT[t % 2][:, k * P:(k + 1) * P], R.xn[t % 2][:, k * P:(k + 1) * P], ident)
        last.then_inc(R.xn_turned, 1)
        if after is not None:
            after(t)


def ln_scalar(act, R, dst, before=None, after=None):
    for t in range(NT):
        if before is not None:
            before(t)
        act.wait_ge(R.xn_turned, t + 1)
        act.activation(dst(t)[0], R.psT[t % 2][:].rearrange("p (k n) -> p k n", k=KC),
                       ACT.Copy).then_inc(R.hi_ready, 1)
        if after is not None:
            after(t)


def program(nc, io):
    out = io["out"]
    had_dram = nc.dram_tensor("wd_h128", (NF, P, C), F32, kind="Internal").ap()
    fold_dram = nc.dram_tensor("wd_folded", (NF, P, C), F32, kind="Internal").ap()
    with ExitStack() as top:
        x = top.enter_context(nc.sbuf_tensor("x", [P, NT, C], F32))
        xTh = top.enter_context(nc.sbuf_tensor("xT_hi", [P, KC, TOK], F32R))
        xTl = top.enter_context(nc.sbuf_tensor("xT_lo", [P, KC, TOK], F32R))
        ident = top.enter_context(nc.sbuf_tensor("ident", [P, P], F32))
        G = Bag()
        G.x, G.xTh, G.xTl, G.ident, G.ident_t = x, xTh, xTl, ident[:], ident
        G.had_dram, G.fold_dram = had_dram, fold_dram
        channel_attention(nc, io, G)
        moe = dict(name="moe", GC=3, NG=11, weights=io["moe_w"], down=None)
        gated_ffn(nc, io, G, **moe)
        cross_attention(nc, io, G)
        ffn = dict(name="ffn", GC=4, NG=4, weights=io["ffn_w"], down=fold_dram)
        gated_ffn(nc, io, G, **ffn)


def scope(nc, ctx, name):
    def sb(n, shape, dt):
        return ctx.enter_context(nc.sbuf_tensor(f"{name}_{n}", shape, dt))

    def ps(n, cols=512):
        return ctx.enter_context(nc.psum_tensor(f"{name}_{n}", [P, cols], F32))

    def sem(n):
        return ctx.enter_context(nc.semaphore(f"{name}_{n}"))

    return sb, ps, sem


def xT_tile(G):
    return lambda t: (G.xTh[:, :, t * P:(t + 1) * P], G.xTl[:, :, t * P:(t + 1) * P])


def channel_attention(nc, io, G):
    with ExitStack() as ctx:
        sb, ps, sem = scope(nc, ctx, "ca")
        R = ln_buffers(sb, ps, sem)
        x, ident = G.x, G.ident
        ctxr = sb("ctx", [P, B, KV, S], F32)
        ctxh, ctxl = sb("ctx_hi", [P, B, KV, S], F32R), sb("ctx_lo", [P, B, KV, S], F32R)
        wr = sb("wqk", [P, 2, KV, D], F32)
        wh, wl = sb("wqk_hi", [P, 2, KV, D], F32R), sb("wqk_lo", [P, 2, KV, D], F32R)
        bias = sb("bqk", [P, 2], F32)
        qkh, qkl = sb("qk_hi", [P, 2, S], F32R), sb("qk_lo", [P, 2, S], F32R)
        prob = [sb(f"prob{i}", [P, S], F32) for i in range(4)]
        mx = sb("max", [P, NT], F32)
        nmx = sb("minus_max", [P, NT], F32)
        tot = sb("total", [P, NT], F32)
        inv = sb("inverse", [P, NT], F32)
        Ah, Al = sb("attnT_hi", [P, TT, S], F32R), sb("attnT_lo", [P, TT, S], F32R)
        had = sb("h128", [P, P], F32)
        hadr = sb("h128_r", [P, P], F32R)
        wdp = sb("wscale_dp", [P, C], F32)
        wdr = [sb(f"wd_raw{i}", [P, C], F32) for i in range(2)]
        wds = [sb(f"wd_scaled{i}", [P, C], F32) for i in range(2)]
        wdh = [sb(f"wd_hi{i}", [P, C], F32R) for i in range(2)]
        wdl = [sb(f"wd_lo{i}", [P, C], F32R) for i in range(2)]
        wdz = R.xn
        psS = [ps(f"ps_s{i}") for i in range(2)]
        psQ = [ps(f"ps_q{i}") for i in range(2)]
        psX = [ps(f"ps_x{i}") for i in range(2)]
        psA = R.psT
        x_loaded = [sem(f"x_loaded{b}") for b in range(B)]
        M = Bag()
        M.small_loaded = sem("small_loaded")
        M.ctx_loaded = sem("ctx_loaded")
        M.const_loaded = sem("const_loaded")
        M.wd_loaded0 = sem("wd_loaded0")
        M.wd_loaded1 = sem("wd_loaded1")
        M.wd_stored0 = sem("wd_stored0")
        M.wd_stored1 = sem("wd_stored1")
        M.w_hi = sem("w_hi")
        M.w_ready = sem("w_ready")
        M.ctx_hi = sem("ctx_hi")
        M.ctx_ready = sem("ctx_ready")
        M.had_ready = sem("had_ready")
        M.qk_done = sem("qk_done")
        M.qk_hi = sem("qk_hi")
        M.qk_ready = sem("qk_ready")
        M.s_done = sem("s_done")
        M.max_ready = sem("max_ready")
        M.exp_done = sem("exp_done")
        M.norm_ready = sem("norm_ready")
        M.a_turned = sem("a_turned")
        M.a_hi = sem("a_hi")
        M.a_ready = sem("a_ready")
        M.x_done = sem("x_done")
        M.x_added = sem("x_added")
        M.chain = sem("chain")
        M.wd_scaled = sem("wd_scaled")
        M.wd_hi = sem("wd_hi")
        M.wd_ready = sem("wd_ready")
        M.wd_done = sem("wd_done")
        M.wd_out = sem("wd_out")
        wd_loaded, wd_stored = [M.wd_loaded0, M.wd_loaded1], [M.wd_stored0, M.wd_stored1]

        with nc.Block() as block:

            @block.sync
            def _(sp):
                sp.dma_start(G.ident_t[:], io["ident"]).then_inc(M.const_loaded, 16)
                for b in range(B):
                    sp.dma_start(x[:, TT * b:TT * b + TT, :],
                                 io["x"][b].rearrange("(t p) c -> p t c", p=P)).then_inc(x_loaded[b], 16)
                sp.dma_start(wr[:], io["ca_w"]).then_inc(M.small_loaded, 16)
                sp.dma_start(bias[:], io["ca_b"]).then_inc(M.small_loaded, 16)
                sp.dma_start(ctxr[:], io["ctxT"].rearrange("b p k s -> p b k s")).then_inc(M.ctx_loaded, 16)
                sp.dma_start(had[:], io["h128"]).then_inc(M.const_loaded, 16)
                sp.dma_start(wdp[:], io["wscale_dp"].partition_broadcast(P)).then_inc(M.const_loaded, 16)
                for n in range(NF):
                    if n >= 2:
                        sp.wait_ge(M.wd_scaled, n - 1)
                    sp.dma_start(wdr[n % 2][:], io["wdT"][n]).then_inc(wd_loaded[n % 2], 16)
                    if n >= 1:
                        sp.wait_ge(M.wd_out, n)
                        sp.dma_start(G.had_dram[n - 1], wdz[(n - 1) % 2][:]).then_inc(wd_stored[(n - 1) % 2], 16)
                sp.wait_ge(M.wd_out, NF)
                sp.dma_start(G.had_dram[NF - 1], wdz[(NF - 1) % 2][:]).then_inc(wd_stored[(NF - 1) % 2], 16)
                for i in range(2):
                    sp.wait_ge(wd_stored[i], 16 * (NF // 2))

            @block.gpsimd
            def _(pool):
                ln_gpsimd(pool, R)
                for n in range(NF):
                    pool.wait_ge(M.wd_hi, n + 1)
                    if n >= 2:
                        pool.wait_ge(M.wd_done, n - 1)
                    pool.tensor_tensor(wdl[n % 2][:], wds[n % 2][:], f32(wdh[n % 2][:]),
                                       ALU.subtract).then_inc(M.wd_ready, 1)

            def quarters():
                return range(NT)

            @block.scalar
            def _(act):
                act.wait_ge(M.small_loaded, 32)
                act.activation(wh[:], wr[:], ACT.Copy).then_inc(M.w_hi, 1)
                act.wait_ge(M.ctx_loaded, 16)
                act.activation(ctxh[:], ctxr[:], ACT.Copy).then_inc(M.ctx_hi, 1)
                ln_scalar(act, R, xT_tile(G))
                act.wait_ge(M.const_loaded, 48)
                act.activation(hadr[:], had[:], ACT.Copy).then_inc(M.had_ready, 1)

                def qk_high(b):
                    for j in range(2):
                        act.wait_ge(M.qk_done, 2 * b + j + 1)
                        act.activation(qkh[:, j, :], psQ[j][:], ACT.Identity,
                                       bias=bias[:, j:j + 1]).then_inc(M.qk_hi, 1)

                def exp(i):
                    act.wait_ge(M.max_ready, i + 1)
                    if i >= 4:
                        act.wait_ge(M.a_turned, i - 3)
                    act.activation(prob[i % 4][:], psS[i % 2][:], ACT.Exp, bias=nmx[:, i:i + 1],
                                   accum_out=tot[:, i:i + 1]).then_inc(M.exp_done, 1)

                def wd_high(n):
                    act.wait_ge(M.wd_scaled, n + 1)
                    if n >= 2:
                        act.wait_ge(M.wd_done, n - 1)
                    act.activation(wdh[n % 2][:], wds[n % 2][:], ACT.Copy).then_inc(M.wd_hi, 1)

                def wd_out(n):
                    act.wait_ge(M.wd_done, n + 1)
                    if n >= 2:
                        act.wait_ge(wd_stored[n % 2], 16 * (n // 2))
                    act.activation(wdz[n % 2][:], psX[n % 2][:], ACT.Copy).then_inc(M.wd_out, 1)

                qk_high(0)
                exp(0)
                exp(1)
                for i in quarters():
                    b, tt = divmod(i, TT)
                    wd_high(i)
                    act.wait_ge(M.a_turned, i + 1)
                    if tt == 0 and b >= 1:
                        act.wait_ge(M.x_done, TT * b)
                    act.activation(Ah[:, :, tt * P:(tt + 1) * P], psA[i % 2][:].rearrange("p (k n) -> p k n", k=TT),
                                   ACT.Copy).then_inc(M.a_hi, 1)
                    if tt < 2:
                        exp(i + 2)
                    wd_out(i)
                    if tt == 3 and b + 1 < B:
                        qk_high(b + 1)
                        exp(i + 1)
                        exp(i + 2)

            @block.vector
            def _(dve):
                dve.wait_ge(M.w_hi, 1)
                dve.tensor_tensor(wl[:], wr[:], f32(wh[:]), ALU.subtract).then_inc(M.w_ready, 1)
                ln_vector(dve, R, x, xT_tile(G), x_loaded=x_loaded)
                dve.wait_ge(M.ctx_hi, 1)
                dve.tensor_tensor(ctxl[:], ctxr[:], f32(ctxh[:]), ALU.subtract).then_inc(M.ctx_ready, 1)
                dve.wait_ge(M.const_loaded, 48)
                ch = Chain(dve, M.chain)

                def qk_low(b):
                    for j in range(2):
                        dve.wait_ge(M.qk_hi, 2 * b + j + 1)
                        dve.scalar_tensor_tensor(out=qkl[:, j, :], in0=psQ[j][:], scalar=bias[:, j:j + 1],
                                                 in1=f32(qkh[:, j, :]), op0=ALU.add,
                                                 op1=ALU.subtract).then_inc(M.qk_ready, 1)

                def row_max(i):
                    dve.wait_ge(M.s_done, i + 1)
                    ch.link(dve.reduce_max(mx[:, i:i + 1], psS[i % 2][:], axis=AX.X))
                    dve.tensor_scalar(nmx[:, i:i + 1], mx[:, i:i + 1], -1.0, None, ALU.mult).then_inc(M.max_ready, 1)

                def normalise(i):
                    dve.wait_ge(M.exp_done, i + 1)
                    ch.link(dve.reciprocal(inv[:, i:i + 1], tot[:, i:i + 1]))
                    dve.tensor_scalar(prob[i % 4][:], prob[i % 4][:], inv[:, i:i + 1], None,
                                      ALU.mult).then_inc(M.norm_ready, 1)

                def attn_low(i):
                    tt = i % TT
                    dve.wait_ge(M.a_hi, i + 1)
                    dve.tensor_tensor(Al[:, :, tt * P:(tt + 1) * P], psA[i % 2][:].rearrange("p (k n) -> p k n", k=TT),
                                      f32(Ah[:, :, tt * P:(tt + 1) * P]), ALU.subtract).then_inc(M.a_ready, 1)

                def scale_wd(n):
                    dve.wait_ge(wd_loaded[n % 2], 16 * (n // 2 + 1))
                    if n >= 2:
                        dve.wait_ge(M.wd_ready, n - 1)
                    dve.tensor_tensor(wds[n % 2][:], wdr[n % 2][:], wdp[:], ALU.mult).then_inc(M.wd_scaled, 1)

                def add_x(b):
                    for lt in range(TT):
                        t = TT * b + lt
                        dve.wait_ge(M.x_done, t + 1)
                        dve.tensor_tensor(x[:, t, :], psX[lt % 2][:], x[:, t, :], ALU.add).then_inc(M.x_added, 1)

                qk_low(0)
                row_max(0)
                row_max(1)
                for i in quarters():
                    b, tt = divmod(i, TT)
                    scale_wd(i)
                    normalise(i)
                    attn_low(i)
                    if tt < 2:
                        row_max(i + 2)
                    if tt == 3:
                        if b + 1 < B:
                            qk_low(b + 1)
                            row_max(i + 1)
                            row_max(i + 2)
                        add_x(b)

            @block.tensor
            def _(pe):
                pe.wait_ge(M.const_loaded, 48)
                ln_tensor(pe, R, ident)
                pe.wait_ge(M.w_ready, 1)
                pe.wait_ge(M.ctx_ready, 1)

                def qk(b):
                    if b >= 1:
                        pe.wait_ge(M.qk_ready, 2 * b)
                    for j in range(2):
                        for k in range(KV):
                            last = product(pe, psQ[j][:], (wh[:, j, k, :], wl[:, j, k, :]),
                                           (ctxh[:, b, k, :], ctxl[:, b, k, :]), k == 0, k == KV - 1)
                        last.then_inc(M.qk_done, 1)

                def scores(i):
                    b, mt = divmod(i, TT)
                    pe.wait_ge(M.qk_ready, 2 * b + 2)
                    if i >= 2:
                        pe.wait_ge(M.exp_done, i - 1)
                    m = slice(mt * P, (mt + 1) * P)
                    product(pe, psS[i % 2][:], (qkh[:, 0, m], qkl[:, 0, m]), (qkh[:, 1, :], qkl[:, 1, :]),
                            True, True).then_inc(M.s_done, 1)

                def turn(i):
                    pe.wait_ge(M.norm_ready, i + 1)
                    pe.wait_ge(R.xT_ready, NT)
                    if i >= 2:
                        pe.wait_ge(M.a_ready, i - 1)
                    for k in range(TT):
                        last = pe.transpose(psA[i % 2][:, k * P:(k + 1) * P], prob[i % 4][:, k * P:(k + 1) * P], ident)
                    last.then_inc(M.a_turned, 1)

                def wd(n):
                    pe.wait_ge(M.had_ready, 1)
                    pe.wait_ge(M.wd_ready, n + 1)
                    if n >= 2:
                        pe.wait_ge(M.wd_out, n - 1)
                    if n >= TT:
                        pe.wait_ge(M.x_added, TT * (n // TT))
                    pe.matmul(psX[n % 2][:], hadr[:], wdh[n % 2][:], start=True, stop=False)
                    pe.matmul(psX[n % 2][:], hadr[:], wdl[n % 2][:], start=False, stop=True).then_inc(M.wd_done, 1)

                def weighted(b):
                    pe.wait_ge(M.a_ready, TT * b + TT)
                    pe.wait_ge(M.wd_out, TT * b + TT)
                    for lt in range(TT):
                        t = TT * b + lt
                        if lt >= 2:
                            pe.wait_ge(M.x_added, t - 1)
                        for k in range(KC):
                            last = product(pe, psX[lt % 2][:], (G.xTh[:, k, t * P:(t + 1) * P], G.xTl[:, k, t * P:(t + 1) * P]),
                                           (Ah[:, k, :], Al[:, k, :]), k == 0, k == KC - 1)
                        last.then_inc(M.x_done, 1)

                qk(0)
                scores(0)
                scores(1)
                for i in quarters():
                    b, tt = divmod(i, TT)
                    turn(i)
                    if tt < 2:
                        scores(i + 2)
                    wd(i)
                    if tt == 3:
                        if b + 1 < B:
                            qk(b + 1)
                            scores(i + 1)
                            scores(i + 2)
                        weighted(b)


def gated_ffn(nc, io, G, name, GC, NG, weights, down):
    moe = name == "moe"
    STEPS = B * GC
    LINKS = 3 if moe else 2
    with ExitStack() as ctx:
        sb, ps, sem = scope(nc, ctx, name)
        x, ident = G.x, G.ident
        lnctx = ExitStack()
        raw = [sb(f"w_raw{j}", [P, WSLICE], F32) for j in range(GC)]
        whi = [sb(f"w_hi{j}", [P, WSLICE], F32R) for j in range(GC)]
        wlo = [sb(f"w_lo{j}", [P, WSLICE], F32R) for j in range(GC)]
        act_out = [sb(f"silu{i}", [P, S], F32) for i in range(2)]
        hhi = [sb(f"hidden_hi{i}", [P, S], F32R) for i in range(2)]
        hlo = [sb(f"hidden_lo{i}", [P, S], F32R) for i in range(2)]
        psG = [ps(f"ps_gate{i}") for i in range(2)]
        psU = [ps(f"ps_up{i}") for i in range(2)]
        psY = [ps(f"ps_y{i}") for i in range(TT)]
        banks = iter((psY[0], psY[1]))
        R = ln_buffers(sb, lambda n: next(banks), sem)
        prod, hidden = R.xn[0], [R.xn[1]] * 2
        if not moe:
            hidden = R.xn
        M = Bag()
        M.w_hi = sem("w_hi")
        M.w_ready = sem("w_ready")
        M.gate_done = sem("gate_done")
        M.up_done = sem("up_done")
        M.silu_done = sem("silu_done")
        M.hidden_steps = sem("hidden_steps")
        M.hidden_ready = sem("hidden_ready")
        M.hidden_free = sem("hidden_free")
        M.y_added = sem("y_added")
        M.const_loaded = sem("const_loaded")
        M.stored = sem("stored")
        M.prep = sem("prep")
        M.prep_pool = sem("prep_pool")
        M.prep_pe = sem("prep_pe")
        M.prep_act = sem("prep_act")
        M.fold_loaded = sem("fold_loaded")
        M.fold_stored = sem("fold_stored")
        M.now_ready = sem("now_ready")
        raw_loaded = [sem(f"raw_loaded{j}") for j in range(GC)]
        raw_parts = 1 if down is None else 2
        if moe:
            gr = sb("router", [P, KC, RG], F32)
            grh, grl = sb("router_hi", [P, KC, RG], F32R), sb("router_lo", [P, KC, RG], F32R)
            lower = sb("lower", [P, E, E], F32)
            lg = sb("logits", [P, NT, RG], F32)
            pr = sb("probs", [P, NT, E], F32)
            sc1 = sb("row_scratch", [P, NT], F32)
            sig = sb("shared_gate", [P, NT], F32)
            beats = sb("beats", [P, NT // 4, E, E], F32)
            ties = sb("ties", [P, NT // 4, E, E], F32)
            rank = sb("rank", [P, NT, E], F32)
            comb = sb("combine", [P, NT, E], F32)
            rep = [sb(f"replicated{i}", [P, 2, P], F32) for i in range(2)]
            row_scale = [sb("expert_scale", [P, TOK], F32), sb("shared_scale", [P, TOK], F32)]
            FOLD = 64
            fold = [sb(f"fold{i}", [P, NF, FOLD], F32) for i in range(2)]
        else:
            had = sb("h128", [P, P], F32)
            hadr = sb("h128_r", [P, 2, P], F32R)
            su_ug = sb("su_ug", [P, C], F32)
            tabs = sb("tables", [P, 3, NF], F32)
            scales = sb("scales", [P, 2, NF], F32)
            now = sb("scales_now", [P, 2, GC], F32)
            uTh, uTl = sb("uT_hi", [P, KC, S], F32R), sb("uT_lo", [P, KC, S], F32R)

        def u_tile(t):
            tt = t % TT
            return uTh[:, :, tt * P:(tt + 1) * P], uTl[:, :, tt * P:(tt + 1) * P]

        ln_dst = xT_tile(G) if moe else u_tile

        def groups(eng, body):
            with eng.Fori(0, NG - 1) as g:
                body(g, False)
            body(NG - 1, True)

        with nc.Block() as block:

            @block.sync
            def _(sp):
                if moe:
                    sp.dma_start(gr[:], io["router"]).then_inc(M.const_loaded, 16)
                    sp.dma_start(lower[:], io["lower"].partition_broadcast(P)).then_inc(M.const_loaded, 16)
                else:
                    sp.dma_start(had[:], io["h128"]).then_inc(M.const_loaded, 16)
                    sp.dma_start(su_ug[:], io["su_ug"].partition_broadcast(P)).then_inc(M.const_loaded, 16)
                    sp.dma_start(tabs[:], io["ffn_tables"]).then_inc(M.const_loaded, 16)

                def load(g, j):
                    if down is None:
                        sp.dma_start(raw[j][:], weights[g * GC + j]).then_inc(raw_loaded[j], 16)
                    else:
                        sp.dma_start(raw[j][:, 0:2 * C], weights[g * GC + j]).then_inc(raw_loaded[j], 16)
                        sp.dma_start(raw[j][:, 2 * C:], down[g * GC + j]).then_inc(raw_loaded[j], 16)

                for j in range(GC):
                    load(0, j)
                with sp.Fori(1, NG) as g:
                    for j in range(GC):
                        sp.wait_ge(M.w_ready, ((g - 1) * GC + j + 1) * 3)
                        load(g, j)
                if not moe:
                    for t in range(NT):
                        sp.wait_ge(M.y_added, NT * (NG - 1) + t + 1)
                        sp.dma_start(io["out"][t // TT, (t % TT) * P:(t % TT + 1) * P, :], x[:, t, :]).then_inc(M.stored, 16)
                    sp.wait_ge(M.stored, 16 * NT)

            @block.gpsimd
            def _(pool):
                ln_gpsimd(pool, R)
                if moe:
                    ch = Chain(pool, M.prep_pool)
                    had_v, fold_v = (d.rearrange("n p c -> p n c") for d in (G.had_dram, G.fold_dram))
                    for k in range(C // FOLD):
                        c = slice(k * FOLD, (k + 1) * FOLD)
                        if k >= 1:
                            pool.wait_ge(M.fold_stored, 16 * k)
                        pool.dma_start(fold[0][:], had_v[:, :, c]).then_inc(M.fold_loaded, 16)
                        pool.wait_ge(M.fold_loaded, 16 * (k + 1))
                        for st in range(4):
                            src = fold[st % 2][:].rearrange("p (a two b) c -> p a two (b c)", two=2, b=1 << st)
                            dst = fold[1 - st % 2][:].rearrange("p (a two b) c -> p a two (b c)", two=2, b=1 << st)
                            pool.tensor_tensor(dst[:, :, 0, :], src[:, :, 0, :], src[:, :, 1, :], ALU.add).then_inc(M.prep_pool, 1)
                            ch.n += 1
                            ch.link(pool.tensor_tensor(dst[:, :, 1, :], src[:, :, 0, :], src[:, :, 1, :], ALU.subtract))
                        pool.dma_start(fold_v[:, :, c], fold[0][:]).then_inc(M.fold_stored, 16)
                    pool.wait_ge(M.fold_stored, 16 * (C // FOLD))

            @block.scalar
            def _(act):
                def split_hi(g, j):
                    act.wait_ge(raw_loaded[j], 16 * raw_parts * (g + 1))
                    for part in range(3):
                        c = slice(part * C, (part + 1) * C)
                        act.activation(whi[j][:, c], raw[j][:, c], ACT.Copy).then_inc(M.w_hi, 1)

                if moe:
                    act.wait_ge(M.const_loaded, 32)
                    act.activation(grh[:], gr[:], ACT.Copy).then_inc(M.prep_act, 1)
                    ln_scalar(act, R, ln_dst)
                    act.wait_ge(M.prep_pe, 1)
                    act.activation(lg[:], psG[0][:, 0:NT * RG].rearrange("p (t e) -> p t e", t=NT), ACT.Copy).then_inc(M.prep_act, 1)
                    act.wait_ge(M.prep, 3)
                    act.activation(pr[:], pr[:], ACT.Exp).then_inc(M.prep_act, 1)
                    act.activation(sig[:], lg[:, :, E], ACT.Sigmoid).then_inc(M.prep_act, 1)
                    for t in range(NT):
                        act.wait_ge(M.prep_pe, t + 2)
                        for i in range(2):
                            last = act.activation(row_scale[i][:, t * P:(t + 1) * P], psU[t % 2][:, i * P:(i + 1) * P], ACT.Copy)
                            if i == 0:
                                last.then_inc(M.prep_act, 1)
                        last.then_inc(M.prep_act, 1)
                else:
                    act.wait_ge(M.const_loaded, 48)
                    act.activation(hadr[:, 0, :], had[:], ACT.Copy).then_inc(M.prep_act, 1)
                    act.activation(hadr[:, 1, :], had[:], ACT.Copy, scale=-1.0).then_inc(M.prep_act, 1)

                    def rotated(t):
                        if t % TT == TT - 1:
                            b = t // TT
                            for m in range(KC):
                                act.wait_ge(M.prep_pe, KC * b + m + 1)
                                act.activation(G.xTh[:, m, b * S:(b + 1) * S], psG[m % 2][:], ACT.Copy).then_inc(M.prep_act, 1)

                    def uT_free(t):
                        if t % TT == 0 and t:
                            act.wait_ge(M.prep_pe, KC * (t // TT))
                    ln_scalar(act, R, ln_dst, before=uT_free, after=rotated)

                for j in range(GC - 2):
                    split_hi(0, j)

                def body(g, last):
                    for s in range(STEPS):
                        b, j = divmod(s, GC)
                        if s < 2:
                            act.wait_ge(M.hidden_free, g * STEPS + s + 1)
                            split_hi(g, GC - 2 + s)
                        if b == B - 1 and j >= 2 and not last:
                            act.wait_ge(M.hidden_free, g * STEPS + s + 1)
                            split_hi(g + 1, j - 2)
                        act.wait_ge(M.gate_done, g * STEPS + s + 1)
                        act.wait_ge(M.hidden_steps, (g * STEPS + s) * LINKS + 1)
                        if moe:
                            ins = act.activation(act_out[s % 2][:], psG[s % 2][:], ACT.Silu)
                        else:
                            if s == 0:
                                act.wait_ge(M.now_ready, g + 1)
                            ins = act.activation(act_out[s % 2][:], psG[s % 2][:], ACT.Silu,
                                                 scale=now[:, 1, j:j + 1])
                        ins.then_inc(M.silu_done, 1)

                groups(act, body)

            @block.vector
            def _(dve):
                def split_lo(g, j):
                    for part in range(3):
                        c = slice(part * C, (part + 1) * C)
                        dve.wait_ge(M.w_hi, (g * GC + j) * 3 + part + 1)
                        last = dve.tensor_tensor(wlo[j][:, c], raw[j][:, c], f32(whi[j][:, c]), ALU.subtract)
                        last.then_inc(M.w_ready, 1)

                if moe:
                    dve.wait_ge(M.prep_act, 1)
                    dve.tensor_tensor(grl[:], gr[:], f32(grh[:]), ALU.subtract).then_inc(M.prep, 1)
                    ln_vector(dve, R, x, ln_dst)
                    ch = Chain(dve, M.prep)
                    ch.n = 1
                    dve.wait_ge(M.prep_act, 2)
                    ch.link(dve.reduce_max(sc1[:], lg[:, :, 0:E], axis=AX.X))
                    ch.link(dve.tensor_tensor(pr[:], lg[:, :, 0:E], sc1[:].unsqueeze(2).broadcast_to([P, NT, E]), ALU.subtract))
                    dve.wait_ge(M.prep_act, 4)
                    ch.link(dve.reduce_sum(sc1[:], pr[:], axis=AX.X))
                    ch.link(dve.reciprocal(sc1[:], sc1[:]))
                    ch.link(dve.tensor_tensor(pr[:], pr[:], sc1[:].unsqueeze(2).broadcast_to([P, NT, E]), ALU.mult))
                    for q in range(4):
                        t = slice(4 * q, 4 * q + 4)
                        own = pr[:, t, :].unsqueeze(3).broadcast_to([P, 4, E, E])
                        other = pr[:, t, :].unsqueeze(2).broadcast_to([P, 4, E, E])
                        ch.link(dve.tensor_tensor(beats[:], other, own, ALU.is_gt))
                        ch.link(dve.tensor_tensor(ties[:], other, own, ALU.is_equal))
                        ch.link(dve.tensor_tensor(ties[:], ties[:], lower[:].unsqueeze(1).broadcast_to([P, 4, E, E]), ALU.mult))
                        ch.link(dve.tensor_tensor(beats[:], beats[:], ties[:], ALU.add))
                        ch.link(dve.reduce_sum(rank[:, t, :], beats[:], axis=AX.X))
                    ch.link(dve.tensor_scalar(rank[:], rank[:], 1.5, None, ALU.is_lt))
                    ch.link(dve.tensor_tensor(comb[:], pr[:], rank[:], ALU.mult))
                    for t in range(NT):
                        if t >= 2:
                            dve.wait_ge(M.prep_pe, t)
                        dve.tensor_copy(rep[t % 2][:, 0, :].rearrange("p (e r) -> p e r", e=E),
                                        comb[:, t, :].unsqueeze(2).broadcast_to([P, E, P // E])).then_inc(M.prep, 1)
                        dve.tensor_copy(rep[t % 2][:, 1, :], sig[:, t:t + 1].broadcast_to([P, P])).then_inc(M.prep, 1)
                    dve.wait_ge(M.prep_act, 4 + 2 * NT)
                else:
                    dve.wait_ge(M.const_loaded, 48)
                    ch = Chain(dve, M.prep)
                    up_s, gate_s = scales[:, 0, :], scales[:, 1, :]
                    ch.link(dve.tensor_tensor(up_s, tabs[:, 0, :], tabs[:, 2, :], ALU.mult))
                    ch.link(dve.tensor_scalar(up_s, up_s, float((C * INTER) ** -0.5), None, ALU.mult))
                    ch.link(dve.tensor_scalar(gate_s, tabs[:, 1, :], float(C ** -0.5), None, ALU.mult))
                    dve.tensor_copy(now[:], scales[:, :, 0:GC]).then_inc(M.now_ready, 1)

                    def rotated(t):
                        if t % TT == TT - 1:
                            b = t // TT
                            for m in range(KC):
                                dve.wait_ge(M.prep_act, 2 + KC * b + m + 1)
                                dve.tensor_tensor(G.xTl[:, m, b * S:(b + 1) * S], psG[m % 2][:],
                                                  f32(G.xTh[:, m, b * S:(b + 1) * S]), ALU.subtract).then_inc(M.prep, 1)
                    ln_vector(dve, R, x, ln_dst, col_scale=su_ug[:], after_lo=rotated)

                dve.sem_inc(M.hidden_steps, 2 * LINKS)
                for j in range(GC - 2):
                    split_lo(0, j)
                def body(g, last):
                    def add_x(b):
                        dve.wait_ge(M.hidden_free, (g * B + b + 1) * GC + 2)
                        for lt in range(TT):
                            t = TT * b + lt
                            dve.tensor_tensor(x[:, t, :], psY[lt][:], x[:, t, :], ALU.add).then_inc(M.y_added, 1)

                    for s in range(STEPS):
                        b, j = divmod(s, GC)
                        if s < 2:
                            split_lo(g, GC - 2 + s)
                        if b == B - 1 and j >= 2 and not last:
                            split_lo(g + 1, j - 2)
                        at = g * STEPS + s
                        n = (at + 2) * LINKS
                        hid = hidden[s % 2]
                        dve.wait_ge(M.up_done, at + 1)
                        dve.wait_ge(M.silu_done, at + 1)
                        if moe:
                            dve.tensor_tensor(prod[:], psU[s % 2][:], act_out[s % 2][:], ALU.mult).then_inc(M.hidden_steps, 1)
                            dve.wait_ge(M.hidden_steps, n + 1)
                            scale = row_scale[0 if j < 2 else 1][:, b * S:(b + 1) * S]
                            dve.tensor_tensor(hid[:], prod[:], scale, ALU.mult).then_inc(M.hidden_steps, 1)
                            dve.wait_ge(M.hidden_steps, n + 2)
                        else:
                            dve.scalar_tensor_tensor(out=hid[:], in0=psU[s % 2][:], scalar=now[:, 0, j:j + 1],
                                                     in1=act_out[s % 2][:], op0=ALU.mult, op1=ALU.mult).then_inc(M.hidden_steps, 1)
                            dve.wait_ge(M.hidden_steps, n + 1)
                        dve.wait_ge(M.hidden_free, at + 1)
                        dve.tensor_copy(hhi[s % 2][:], hid[:]).then_inc(M.hidden_steps, 1)
                        dve.wait_ge(M.hidden_steps, n + LINKS)
                        dve.tensor_tensor(hlo[s % 2][:], hid[:], f32(hhi[s % 2][:]), ALU.subtract).then_inc(M.hidden_ready, 1)
                        if j == 0 and b >= 1:
                            add_x(b - 1)
                    if not moe and not last:
                        dve.tensor_copy(now[:], scales[:, :, bass.ds((g + 1) * GC, GC)]).then_inc(M.now_ready, 1)
                    add_x(B - 1)

                groups(dve, body)

            @block.tensor
            def _(pe):
                if moe:
                    ln_tensor(pe, R, ident)
                    pe.wait_ge(R.xT_ready, NT)
                    pe.wait_ge(M.prep, 1)
                    for t in range(NT):
                        for k in range(KC):
                            tok = slice(t * P, (t + 1) * P)
                            last = product(pe, psG[0][:, t * RG:(t + 1) * RG], (G.xTh[:, k, tok], G.xTl[:, k, tok]),
                                           (grh[:, k, :], grl[:, k, :]), k == 0, k == KC - 1)
                    last.then_inc(M.prep_pe, 1)
                    ROUTE_LINKS = 1 + 5 + 4 * 5 + 2
                    for t in range(NT):
                        pe.wait_ge(M.prep, ROUTE_LINKS + 2 * t + 2)
                        if t >= 2:
                            pe.wait_ge(M.prep_act, 4 + 2 * (t - 1))
                        for i in range(2):
                            last = pe.transpose(psU[t % 2][:, i * P:(i + 1) * P], rep[t % 2][:, i, :], ident)
                        last.then_inc(M.prep_pe, 1)
                    pe.wait_ge(M.prep_act, 4 + 2 * NT)
                else:
                    def rotate(t):
                        if t % TT == TT - 1:
                            b = t // TT
                            pe.wait_ge(R.xT_ready, t + 1)
                            pe.wait_ge(M.prep_act, 2)
                            for m in range(KC):
                                if KC * b + m >= 2:
                                    pe.wait_ge(M.prep, 3 + KC * b + m - 1)
                                for k in range(KC):
                                    sign = bin(k & m).count("1") % 2
                                    pe.matmul(psG[m % 2][:], hadr[:, sign, :], uTh[:, k, :], start=k == 0, stop=False)
                                    last = pe.matmul(psG[m % 2][:], hadr[:, sign, :], uTl[:, k, :], start=False, stop=k == KC - 1)
                                last.then_inc(M.prep_pe, 1)
                    ln_tensor(pe, R, ident, after=rotate)
                    pe.wait_ge(M.prep, 3 + KC * B)

                pe.sem_inc(M.hidden_free, 2)

                def gate_up(g, s):
                    b, j = divmod(s % STEPS, GC)
                    at = g * STEPS + s
                    pe.wait_ge(M.w_ready, (g * GC + (s // STEPS) * GC + j + 1) * 3)
                    pe.wait_ge(M.hidden_steps, at * LINKS + 1)
                    for bank, o, done in ((psG, 0, M.gate_done), (psU, C, M.up_done)):
                        for k in range(KC):
                            c = slice(o + k * P, o + (k + 1) * P)
                            tok = slice(b * S, (b + 1) * S)
                            last = product(pe, bank[s % 2][:], (whi[j][:, c], wlo[j][:, c]),
                                           (G.xTh[:, k, tok], G.xTl[:, k, tok]), k == 0, k == KC - 1)
                        last.then_inc(done, 1)

                def down_step(g, s):
                    b, j = divmod(s, GC)
                    at = g * STEPS + s
                    pe.wait_ge(M.hidden_ready, at + 1)
                    if j == 0:
                        pe.wait_ge(M.y_added, (g * B + b) * TT)
                    for lt in range(TT):
                        m = slice(lt * P, (lt + 1) * P)
                        last = product(pe, psY[lt][:], (hhi[s % 2][:, m], hlo[s % 2][:, m]),
                                       (whi[j][:, 2 * C:], wlo[j][:, 2 * C:]), j == 0, j == GC - 1)
                    last.then_inc(M.hidden_free, 1)

                def body(g, last):
                    for s in range(STEPS):
                        if not (last and s == STEPS - 1):
                            gate_up(g, s + 1)
                        down_step(g, s)

                gate_up(0, 0)
                groups(pe, body)


def cross_attention(nc, io, G):
    UNITS = B * HPG
    TILES = UNITS * TT
    LASTU = GROUPS * UNITS - 1
    LASTI = GROUPS * TILES - 1
    SCALE = float(D) ** -0.5
    with ExitStack() as ctx:
        sb, ps, sem = scope(nc, ctx, "xa")
        x, ident = G.x, G.ident
        ctxr = sb("ctx", [P, B, KV, S], F32)
        ctxh, ctxl = sb("ctx_hi", [P, KV, S], F32R), sb("ctx_lo", [P, KV, S], F32R)
        NQ, NKV, NO = KC * HPG * D, 2 * KV * D, HPG * C
        raw = sb("w_raw", [P, NQ + NKV], F32)
        rqkv, ro = raw, raw[:, 0:NO]
        NQK = NQ + NKV // 2
        qkvh, qkvl = sb("wqkv_hi", [P, NQ + NKV], F32R), sb("wqkv_lo", [P, NQ + NKV], F32R)
        woh, wol = sb("wo_hi", [P, NO], F32R), sb("wo_lo", [P, NO], F32R)
        qh, ql = ([sb(f"q_{n}{i}", [P, S], F32R) for i in range(2)] for n in ("hi", "lo"))
        kh, kl = ([sb(f"k_{n}{i}", [P, S], F32R) for i in range(2)] for n in ("hi", "lo"))
        vh, vl = sb("v_hi", [P, S], F32R), sb("v_lo", [P, S], F32R)
        oh = [sb(f"out_hi{i}", [P, S], F32R) for i in range(HPG)]
        ol = [sb(f"out_lo{i}", [P, S], F32R) for i in range(HPG)]
        prob = [sb(f"prob{i}", [P, S], F32) for i in range(4)]
        PTh, PTl = sb("probT_hi", [P, TT, S], F32R), sb("probT_lo", [P, TT, S], F32R)
        mask8 = sb("mask", [P, B * S], U8)
        maskb = sb("mask_bias", [P, B * S], mybir.dt.bfloat16)
        some = sb("any_key", [P, B], F32)
        mx, nmx = sb("max", [P, 4], F32), sb("minus_max", [P, 4], F32)
        tot, inv = sb("total", [P, 4], F32), sb("inverse", [P, 4], F32)
        idle = sb("idle", [P, 1], F32)
        psS = [ps(f"ps_s{i}") for i in range(2)]
        psT = [ps(f"ps_t{i}") for i in range(2)]
        psP = [ps(f"ps_p{i}") for i in range(2)]
        psO = [ps(f"ps_o{i}") for i in range(2)]
        banks = iter(psT)
        R = ln_buffers(sb, lambda n: next(banks), sem, xn=prob[2:])
        M = Bag()
        M.ctx_loaded = sem("ctx_loaded")
        M.mask_loaded = sem("mask_loaded")
        M.qkv_loaded = sem("qkv_loaded")
        M.o_loaded = sem("o_loaded")
        M.mask_ready = sem("mask_ready")
        M.qk_hi = sem("qk_hi")
        M.qk_ready = sem("qk_ready")
        M.wv_hi = sem("wv_hi")
        M.wv_ready = sem("wv_ready")
        M.wo_hi = sem("wo_hi")
        M.wo_ready = sem("wo_ready")
        M.ctx_hi = sem("ctx_hi")
        M.ctx_ready = sem("ctx_ready")
        M.proj_done = sem("proj_done")
        M.proj_hi = sem("proj_hi")
        M.proj_ready = sem("proj_ready")
        M.s_done = sem("s_done")
        M.max_ready = sem("max_ready")
        M.exp_done = sem("exp_done")
        M.norm_ready = sem("norm_ready")
        M.p_turned = sem("p_turned")
        M.pt_hi = sem("pt_hi")
        M.pt_ready = sem("pt_ready")
        M.o_done = sem("o_done")
        M.x_added = sem("x_added")
        M.chain = sem("chain")

        FIRST_K, FIRST_Q, SECOND_Q = Place(0, 0), Place(1, 1), Place(2, 0)
        FINAL_PV = Place(2 + 6 * (LASTU // 2) + 3, 1)

        def last_pv(pair, h, end):
            return Place(2 + 6 * pair + (0 if h == 0 else 2 if end else 4), 0)

        def this_v(pair):
            return Place(2 + 6 * pair + 1, 1)

        def next_q(pair, h):
            return Place(2 + 6 * pair + (2 if h == 0 else 5), h)

        def next_k(pair):
            return Place(2 + 6 * pair + 3, 1)

        def at_least(eng, s, v):
            if not isinstance(v, int) or v > 0:
                eng.wait_ge(s, v)

        def groups(eng, body):
            body(0, "first")
            with eng.Fori(1, GROUPS - 1) as g:
                body(g, "middle")
            body(GROUPS - 1, "last")

        def units(g, which):
            for ul in range(UNITS):
                left = UNITS - 1 - ul if which == "last" else UNITS
                yield ul, ul // HPG, ul % HPG, g * B + ul // HPG, g * UNITS + ul, g * TILES + TT * ul, left

        with nc.Block() as block:

            @block.sync
            def _(sp):
                sp.dma_start(mask8[:], io["mask"].partition_broadcast(P)).then_inc(M.mask_loaded, 16)
                sp.dma_start(ctxr[:], io["ctxT"].rearrange("b p k s -> p b k s")).then_inc(M.ctx_loaded, 16)
                with sp.Fori(0, GROUPS) as g:
                    sp.wait_ge(M.wo_ready, g)
                    sp.dma_start(rqkv[:], io["xa_w"][g, :, 0:NQ + NKV]).then_inc(M.qkv_loaded, 16)
                    sp.wait_ge(M.wv_ready, g + 1)
                    sp.dma_start(ro, io["xa_w"][g, :, NQ + NKV:]).then_inc(M.o_loaded, 16)

            @block.gpsimd
            def _(pool):
                ln_gpsimd(pool, R)

                def ctx_low(pair, b):
                    pool.wait_ge(M.ctx_hi, pair + 1)
                    pool.tensor_tensor(ctxl[:], ctxr[:, b, :, :], f32(ctxh[:]), ALU.subtract).then_inc(M.ctx_ready, 1)

                ctx_low(0, 0)

                def body(g, which):
                    for b in range(B):
                        if not (which == "last" and b == B - 1):
                            ctx_low(g * B + b + 1, (b + 1) % B)
                groups(pool, body)

            @block.scalar
            def _(act):
                def split_qk(g):
                    act.wait_ge(M.qkv_loaded, 16 * (g + 1))
                    act.activation(qkvh[:, 0:NQK], rqkv[:, 0:NQK], ACT.Copy).then_inc(M.qk_hi, 1)

                def split_v(g):
                    act.activation(qkvh[:, NQK:], rqkv[:, NQK:], ACT.Copy).then_inc(M.wv_hi, 1)

                def split_o(g):
                    act.wait_ge(M.o_loaded, 16 * (g + 1))
                    act.activation(woh[:], ro, ACT.Copy).then_inc(M.wo_hi, 1)

                def proj_high(at, out):
                    act.wait_ge(M.proj_done, at.n + 1)
                    act.activation(out[:], psP[at.bank][:], ACT.Copy).then_inc(M.proj_hi, 1)

                def exp(i, slot):
                    act.wait_ge(M.max_ready, i + 1)
                    act.activation(prob[slot][:], prob[slot][:], ACT.Exp, bias=nmx[:, slot:slot + 1], scale=SCALE,
                                   accum_out=tot[:, slot:slot + 1]).then_inc(M.exp_done, 1)

                def turned_high(i, tt):
                    act.wait_ge(M.p_turned, i + 1)
                    act.activation(PTh[:, :, tt * P:(tt + 1) * P], psT[tt % 2][:].rearrange("p (k n) -> p k n", k=TT),
                                   ACT.Copy).then_inc(M.pt_hi, 1)

                act.wait_ge(M.ctx_loaded, 16)
                act.activation(ctxh[:], ctxr[:, 0, :, :], ACT.Copy).then_inc(M.ctx_hi, 1)
                split_qk(0)
                split_v(0)
                ln_scalar(act, R, xT_tile(G))
                proj_high(FIRST_K, kh[0])
                proj_high(FIRST_Q, qh[0])
                proj_high(SECOND_Q, qh[1])
                for t in range(3):
                    exp(t, t)

                def body(g, which):
                    for ul, b, h, pair, u, i, left in units(g, which):
                        has_pv = not (which == "first" and ul == 0)
                        exp(i + 3, 3)
                        if has_pv:
                            act.wait_ge(M.proj_done, last_pv(pair, h, left < 2).n + 1)
                        turned_high(i, 0)
                        if has_pv:
                            proj_high(last_pv(pair, h, left < 2), oh[1 - h])
                        if ul == UNITS - 2 and which != "last":
                            act.wait_ge(M.proj_done, next_q(pair - 1, 1).n + 1)
                            split_qk(g + 1)
                        turned_high(i + 1, 1)
                        if left >= 1:
                            exp(i + 4, 0)
                        if h == 0:
                            proj_high(this_v(pair), vh)
                            if left >= 2:
                                act.activation(ctxh[:], ctxr[:, (b + 1) % B, :, :], ACT.Copy).then_inc(M.ctx_hi, 1)
                        if ul == 1:
                            act.wait_ge(M.o_done, g * B * TT)
                            split_o(g)
                        turned_high(i + 2, 2)
                        if left >= 1:
                            exp(i + 5, 1)
                        if ul == UNITS - 2 and which != "last":
                            split_v(g + 1)
                        turned_high(i + 3, 3)
                        if left >= 1:
                            exp(i + 6, 2)
                        if left >= 2:
                            proj_high(next_q(pair, h), qh[h])
                            if h == 0:
                                proj_high(next_k(pair), kh[(b + 1) % 2])

                groups(act, body)
                proj_high(FINAL_PV, oh[1])

            @block.vector
            def _(dve):
                def split_qk(g):
                    dve.wait_ge(M.qk_hi, g + 1)
                    dve.tensor_tensor(qkvl[:, 0:NQK], rqkv[:, 0:NQK], f32(qkvh[:, 0:NQK]), ALU.subtract).then_inc(M.qk_ready, 1)

                def split_v(g):
                    dve.wait_ge(M.wv_hi, g + 1)
                    dve.tensor_tensor(qkvl[:, NQK:], rqkv[:, NQK:], f32(qkvh[:, NQK:]), ALU.subtract).then_inc(M.wv_ready, 1)

                def split_o(g):
                    dve.wait_ge(M.wo_hi, g + 1)
                    dve.tensor_tensor(wol[:], ro, f32(woh[:]), ALU.subtract).then_inc(M.wo_ready, 1)

                def proj_low(at, hi, lo):
                    dve.wait_ge(M.proj_hi, at.n + 1)
                    dve.tensor_tensor(lo[:], psP[at.bank][:], f32(hi[:]), ALU.subtract).then_inc(M.proj_ready, 1)

                def masked_max(i, slot, b, n):
                    dve.wait_ge(M.s_done, i + 1)
                    at_least(dve, M.p_turned, i - 3)
                    dve.memset(idle[:], 0.0)
                    dve.tensor_tensor_reduce(out=prob[slot][:], in0=psS[slot % 2][:], in1=maskb[:, b * S:(b + 1) * S],
                                             scale=1.0, scalar=-3.4e38, op0=ALU.add, op1=ALU.max,
                                             accum_out=mx[:, slot:slot + 1]).then_inc(M.chain, 1)
                    dve.wait_ge(M.chain, n)
                    dve.tensor_scalar(nmx[:, slot:slot + 1], mx[:, slot:slot + 1], -SCALE, None,
                                      ALU.mult).then_inc(M.max_ready, 1)

                def normalise(i, slot, b, n):
                    dve.wait_ge(M.exp_done, i + 1)
                    dve.reciprocal(inv[:, slot:slot + 1], tot[:, slot:slot + 1]).then_inc(M.chain, 1)
                    dve.wait_ge(M.chain, n)
                    dve.tensor_scalar(prob[slot][:], prob[slot][:], inv[:, slot:slot + 1], some[:, b:b + 1],
                                      ALU.mult, ALU.mult).then_inc(M.norm_ready, 1)

                def turned_low(i, tt):
                    dve.wait_ge(M.pt_hi, i + 1)
                    dve.tensor_tensor(PTl[:, :, tt * P:(tt + 1) * P], psT[tt % 2][:].rearrange("p (k n) -> p k n", k=TT),
                                      f32(PTh[:, :, tt * P:(tt + 1) * P]), ALU.subtract).then_inc(M.pt_ready, 1)

                def add_x(pair, b, tt):
                    dve.wait_ge(M.o_done, pair * TT + tt + 1)
                    t = TT * b + tt
                    dve.tensor_tensor(x[:, t, :], psO[tt % 2][:], x[:, t, :], ALU.add).then_inc(M.x_added, 1)

                dve.wait_ge(M.mask_loaded, 16)
                dve.tensor_scalar(maskb[:], mask8[:], MASKED, -MASKED, ALU.mult, ALU.add).then_inc(M.mask_ready, 1)
                dve.reduce_max(some[:], mask8[:].rearrange("p (b s) -> p b s", b=B), axis=AX.X).then_inc(M.mask_ready, 1)
                split_qk(0)
                split_v(0)
                ln_vector(dve, R, x, xT_tile(G))
                dve.wait_ge(M.mask_ready, 2)
                proj_low(FIRST_K, kh[0], kl[0])
                proj_low(FIRST_Q, qh[0], ql[0])
                proj_low(SECOND_Q, qh[1], ql[1])
                for t in range(3):
                    masked_max(t, t, 0, t + 1)
                for t in range(2):
                    normalise(t, t, 0, t + 4)

                def body(g, which):
                    for ul, b, h, pair, u, i, left in units(g, which):
                        nb = (ul + 1) // HPG % B
                        links = 5 + 2 * i
                        has_pv = not (which == "first" and ul == 0)
                        has_output = h == 0 and has_pv
                        ob = (b - 1) % B
                        masked_max(i + 3, 3, b, links + 1)
                        normalise(i + 2, 2, b, links + 2)
                        if h == 1 and not (which == "first" and ul == 1):
                            add_x(pair - 1, ob, 3)
                        turned_low(i, 0)
                        if has_pv:
                            proj_low(last_pv(pair, h, left < 2), oh[1 - h], ol[1 - h])
                        if ul == UNITS - 2 and which != "last":
                            split_qk(g + 1)
                        if left >= 1:
                            masked_max(i + 4, 0, nb, links + 3)
                        normalise(i + 3, 3, b, links + (4 if left >= 1 else 3))
                        turned_low(i + 1, 1)
                        if h == 0:
                            proj_low(this_v(pair), vh, vl)
                        if ul == 1:
                            split_o(g)
                        if has_output:
                            add_x(pair - 1, ob, 0)
                        if left >= 1:
                            masked_max(i + 5, 1, nb, links + 5)
                            normalise(i + 4, 0, nb, links + 6)
                        turned_low(i + 2, 2)
                        if has_output:
                            add_x(pair - 1, ob, 1)
                        if ul == UNITS - 2 and which != "last":
                            split_v(g + 1)
                        if left >= 1:
                            masked_max(i + 6, 2, nb, links + 7)
                            normalise(i + 5, 1, nb, links + 8)
                        turned_low(i + 3, 3)
                        if left >= 2:
                            proj_low(next_q(pair, h), qh[h], ql[h])
                        if has_output:
                            add_x(pair - 1, ob, 2)
                        if left >= 2 and h == 0:
                            proj_low(next_k(pair), kh[(b + 1) % 2], kl[(b + 1) % 2])

                groups(dve, body)
                proj_low(FINAL_PV, oh[1], ol[1])
                for tt in range(TT):
                    add_x(GROUPS * B - 1, B - 1, tt)

            @block.tensor
            def _(pe):
                def wq(h, k):
                    c = slice(k * HPG * D + h * D, k * HPG * D + (h + 1) * D)
                    return qkvh[:, c], qkvl[:, c]

                def wkv(j, k):
                    c = slice(NQ + (j * KV + k) * D, NQ + (j * KV + k + 1) * D)
                    return qkvh[:, c], qkvl[:, c]

                def bank_free(at):
                    at_least(pe, M.proj_ready, at.n - 1)

                def query(at, b, h, ks):
                    for k in ks:
                        tok = slice(b * S, (b + 1) * S)
                        last = product(pe, psP[at.bank][:], wq(h, k), (G.xTh[:, k, tok], G.xTl[:, k, tok]),
                                       k == 0, k == KC - 1)
                        if k == KC - 1:
                            last.then_inc(M.proj_done, 1)

                def key(at):
                    for k in range(KV):
                        last = product(pe, psP[at.bank][:], wkv(0, k), (ctxh[:, k, :], ctxl[:, k, :]), k == 0, k == KV - 1)
                    last.then_inc(M.proj_done, 1)

                def value(at):
                    for st in range(TT):
                        s = slice(st * P, (st + 1) * P)
                        for k in range(KV):
                            last = product(pe, psP[at.bank][:, s], (ctxh[:, k, s], ctxl[:, k, s]), wkv(1, k), k == 0, k == KV - 1)
                    last.then_inc(M.proj_done, 1)

                def scores(i, tt, q, k):
                    at_least(pe, M.max_ready, i - 1)
                    m = slice(tt * P, (tt + 1) * P)
                    product(pe, psS[tt % 2][:], (qh[q][:, m], ql[q][:, m]), (kh[k][:], kl[k][:]), True, True).then_inc(M.s_done, 1)

                def turn(i, tt):
                    pe.wait_ge(M.norm_ready, i + 1)
                    at_least(pe, M.pt_ready, i - 1)
                    for k in range(TT):
                        last = pe.transpose(psT[tt % 2][:, k * P:(k + 1) * P], prob[tt][:, k * P:(k + 1) * P], ident)
                    last.then_inc(M.p_turned, 1)

                def weighted(at, u):
                    pe.wait_ge(M.pt_ready, TT * (u + 1))
                    bank_free(at)
                    for st in range(TT):
                        s = slice(st * P, (st + 1) * P)
                        last = product(pe, psP[at.bank][:], (vh[:, s], vl[:, s]), (PTh[:, st, :], PTl[:, st, :]),
                                       st == 0, st == TT - 1)
                    last.then_inc(M.proj_done, 1)

                def output(pair, tt):
                    at_least(pe, M.x_added, pair * TT + tt - 1)
                    m = slice(tt * P, (tt + 1) * P)
                    for h in range(HPG):
                        last = product(pe, psO[tt % 2][:], (oh[h][:, m], ol[h][:, m]),
                                       (woh[:, h * C:(h + 1) * C], wol[:, h * C:(h + 1) * C]), h == 0, h == HPG - 1)
                    last.then_inc(M.o_done, 1)

                ln_tensor(pe, R, ident)
                pe.wait_ge(M.wv_ready, 1)
                pe.wait_ge(M.ctx_ready, 1)
                key(FIRST_K)
                pe.wait_ge(R.xT_ready, NT)
                query(FIRST_Q, 0, 0, range(KC))
                bank_free(SECOND_Q)
                query(SECOND_Q, 0, 1, range(KC))
                pe.wait_ge(M.proj_ready, SECOND_Q.n + 1)
                for t in range(3):
                    scores(t, t, 0, 0)

                def body(g, which):
                    for ul, b, h, pair, u, i, left in units(g, which):
                        nk = (ul + 1) // HPG % 2
                        has_pv = not (which == "first" and ul == 0)
                        has_output = h == 0 and has_pv
                        qb = (b + 1) % B
                        nq = next_q(pair, h)
                        scores(i + 3, 3, h, b % 2)
                        turn(i, 0)
                        if h == 1 and not (which == "first" and ul == 1):
                            output(pair - 1, 3)
                        if has_pv:
                            if h == 1:
                                pe.wait_ge(M.proj_ready, this_v(pair).n + 1)
                            weighted(last_pv(pair, h, left < 2), u - 1)
                        if left >= 1:
                            pe.wait_ge(M.proj_ready, (next_k(pair) if h == 1 else next_q(pair - 1, 1)).n + 1)
                            scores(i + 4, 0, 1 - h, nk)
                        turn(i + 1, 1)
                        if h == 0:
                            bank_free(this_v(pair))
                            value(this_v(pair))
                        if has_output:
                            pe.wait_ge(M.proj_ready, last_pv(pair, h, left < 2).n + 1)
                            if ul == HPG:
                                pe.wait_ge(M.wo_ready, g + 1)
                            output(pair - 1, 0)
                        if left >= 1:
                            scores(i + 5, 1, 1 - h, nk)
                        turn(i + 2, 2)
                        if left >= 2:
                            if ul == UNITS - 2:
                                pe.wait_ge(M.qk_ready, g + 2)
                            bank_free(nq)
                            query(nq, qb, h, range(0, KC // 2))
                        if has_output:
                            output(pair - 1, 1)
                        if left >= 1:
                            scores(i + 6, 2, 1 - h, nk)
                        turn(i + 3, 3)
                        if left >= 2:
                            query(nq, qb, h, range(KC // 2, KC))
                        if has_output:
                            output(pair - 1, 2)
                        if left >= 2 and h == 0:
                            pe.wait_ge(M.ctx_ready, pair + 2)
                            bank_free(next_k(pair))
                            key(next_k(pair))
                            if ul == UNITS - 2:
                                pe.wait_ge(M.wv_ready, g + 2)

                groups(pe, body)
                weighted(FINAL_PV, LASTU)
                pe.wait_ge(M.proj_ready, FINAL_PV.n + 1)
                for tt in range(TT):
                    output(GROUPS * B - 1, tt)


def kernel(**inputs):
    import concourse.bacc as bacc
    from concourse.bass_utils import run_bass_kernel_spmd

    a = {k: np.asarray(v) for k, v in inputs.items()}

    def chunks_T(w):
        n = w.shape[0] // P
        return w.reshape(n, P, -1, P).transpose(0, 3, 2, 1).reshape(n, P, -1)

    def by_expert(w):
        r = P // E
        return w.reshape(E, F_MOE // r, r, C).transpose(1, 0, 2, 3).reshape(E * F_MOE, C)

    def interleaved(experts, shared):
        n = F_SHARED // P
        return np.concatenate([experts.reshape(n, 2, P, -1), shared.reshape(n, 1, P, -1)], axis=1).reshape(3 * n, P, -1)

    moe_w = np.concatenate([
        interleaved(chunks_T(by_expert(a["L0_ffn_expert_fc1"])), chunks_T(a["L0_ffn_shared_fc1"])),
        interleaved(chunks_T(by_expert(a["L0_ffn_expert_fc2"])), chunks_T(a["L0_ffn_shared_fc2"])),
        interleaved(by_expert(a["L0_ffn_expert_proj"].transpose(0, 2, 1)), a["L0_ffn_shared_proj"].T)], axis=2)
    router = np.concatenate([a["L0_ffn_gate_w"], a["L0_ffn_shared_gate_w"], np.zeros((1, C), np.float32)])

    def rows(w, per_group):
        return w.reshape(-1, P, GROUPS, per_group).transpose(2, 1, 0, 3).reshape(GROUPS, P, -1)

    h = np.ones((1, 1), np.float32)
    while h.shape[0] < P:
        h = np.block([[h, h], [h, -h]]).astype(np.float32)
    wsc = a["L1_ffn_Wscale_ug"].reshape(2, NF, P)
    arrays = {
        "x": a["x"],
        "ctxT": a["ctx_1024"].reshape(B, S, KV, P).transpose(0, 3, 2, 1),
        "mask": a["mask_BxS2_bf1"].view(np.uint8).reshape(B * S),
        "ident": np.eye(P, dtype=np.float32),
        "h128": h,
        "lower": np.tril(np.ones((E, E), np.float32), -1),
        "ca_w": np.stack([chunks_T(a["L0_xattn_Wq"])[0], chunks_T(a["L0_xattn_Wk"])[0]], axis=1).reshape(P, 2, KV, D),
        "ca_b": np.stack([a["L0_xattn_bq"], a["L0_xattn_bk"]], axis=1),
        "moe_w": moe_w,
        "router": router.reshape(RG, KC, P).transpose(2, 1, 0),
        "xa_w": np.concatenate([
            rows(a["L1_xattn_Wq"], HPG * D), rows(a["L1_xattn_Wk"], D), rows(a["L1_xattn_Wv"], D),
            a["L1_xattn_Wo"].reshape(GROUPS, HPG, D, C).transpose(0, 2, 1, 3).reshape(GROUPS, D, HPG * C)], axis=2),
        "ffn_w": np.concatenate([chunks_T(a["L1_ffn_W_gate"]), chunks_T(a["L1_ffn_W_up"])], axis=2),
        "wdT": a["L1_ffn_W_down"].T.reshape(NF, P, C),
        "wscale_dp": a["L1_ffn_Wscale_dp"],
        "su_ug": a["L1_ffn_SU_ug"],
        "ffn_tables": np.stack([wsc[0].T, wsc[1].T, a["L1_ffn_SU_dp"].reshape(NF, P).T], axis=1),
    }
    arrays = {f"in_{k}": np.ascontiguousarray(v) for k, v in arrays.items()}
    nc = bacc.Bacc("TRN2", target_bir_lowering=False, num_devices=1)
    io = {k[3:]: nc.dram_tensor(k, v.shape, mybir.dt.from_np(v.dtype), kind="ExternalInput").ap() for k, v in arrays.items()}
    io["out"] = nc.dram_tensor("out", (B, S, C), F32, kind="ExternalOutput").ap()
    program(nc, io)
    result = run_bass_kernel_spmd(nc, [arrays], core_ids=[0])
    return result.results[0]["out"]
```

```python
from contextlib import ExitStack

import numpy as np

import concourse.bass as bass
from concourse import mybir

F32 = mybir.dt.float32
F32R = mybir.dt.float32r
U8 = mybir.dt.uint8
I32 = mybir.dt.int32
ALU = mybir.AluOpType
ACT = mybir.ActivationFunctionType
AX = mybir.AxisListType

P = 128
B, S, C = 4, 512, 512
CV = 256
TOK = B * S
NT = TOK // P
TT = S // P
KC = C // P
KV = CV // P
D = 128
E, F_MOE, F_SHARED = 8, 352, 1408
RG = E + 2
GROUPS, HPG = 8, 2
INTER = 2048
NF = INTER // P
EPS = 1e-5
MASKED = 3.0e38
SLOTS = 256
SUBS = SLOTS // P
TILES = (2 * TOK + E * (SLOTS - 1)) // SLOTS
FCH = -(-F_MOE // P)
EW = 2 * KC * F_MOE + FCH * C
WSLICE = 3 * C


class Chain:

    def __init__(self, eng, sem):
        self.eng, self.sem, self.n = eng, sem, 0

    def link(self, ins):
        ins.then_inc(self.sem, 1)
        self.n += 1
        self.eng.wait_ge(self.sem, self.n)


class Bag:
    pass


class Place:

    def __init__(self, n, bank):
        self.n, self.bank = n, bank


def f32(ap):
    return ap.bitcast(F32)


def product(pe, out, lhs, rhs, start, stop):
    (lh, ll), (rh, rl) = lhs, rhs
    pe.matmul(out, lh, rh, start=start, stop=False)
    pe.matmul(out, lh, rl, start=False, stop=False)
    return pe.matmul(out, ll, rh, start=False, stop=stop)


def ln_buffers(sb, ps, sem, xn=None):
    R = Bag()
    R.xTh, R.xTl = sb("xT_hi", [P, KC, TOK], F32R), sb("xT_lo", [P, KC, TOK], F32R)
    R.stats = sb("ln_stats", [P, NT, 6], F32)
    R.mv = sb("ln_mean_var", [P, NT, 2], F32)
    R.veps = sb("ln_var_eps", [P, NT], F32)
    R.rstd = sb("ln_rstd", [P, NT], F32)
    R.mhalf = sb("ln_minus_half", [P, TT], F32)
    R.xn = xn or [sb(f"ln_xn{i}", [P, C], F32) for i in range(2)]
    R.psT = [ps(f"ps_xnT{i}") for i in range(2)]
    R.chain = sem("ln_chain")
    R.stats_done = sem("ln_stats_done")
    R.pool_chain = sem("ln_pool_chain")
    R.rstd_ready = sem("ln_rstd_ready")
    R.xn_ready = sem("ln_xn_ready")
    R.xn_turned = sem("ln_xn_turned")
    R.hi_ready = sem("ln_hi_ready")
    R.xT_ready = sem("ln_xT_ready")
    return R


def ln_gpsimd(pool, R):
    ch = Chain(pool, R.pool_chain)
    ch.link(pool.memset(R.mhalf[:], -0.5))
    for b in range(B):
        t = slice(TT * b, TT * b + TT)
        pool.wait_ge(R.stats_done, b + 1)
        ch.link(pool.tensor_scalar(R.veps[:, t], R.mv[:, t, 1], EPS, None, ALU.add))
        pool.tensor_tensor(R.rstd[:, t], R.veps[:, t], R.mhalf[:], ALU.pow).then_inc(R.rstd_ready, 1)


def ln_vector(dve, R, x, dst, x_loaded=None, col_scale=None, after_lo=None, stored=None):
    ch = Chain(dve, R.chain)

    def low(t):
        dve.wait_ge(R.hi_ready, t + 1)
        hi, lo = dst(t)
        dve.tensor_tensor(lo, R.psT[t % 2][:].rearrange("p (k n) -> p k n", k=KC), f32(hi),
                          ALU.subtract).then_inc(R.xT_ready, 1)
        if after_lo is not None:
            after_lo(t)

    for b in range(B + 1):
        if b < B:
            if x_loaded is not None:
                dve.wait_ge(x_loaded[b], 16)
            for t in range(TT * b, TT * b + TT):
                last = dve.bn_stats(R.stats[:, t, :], x[:, t, :])
                if t < TT * b + TT - 1:
                    last.then_inc(R.chain, 1)
                    ch.n += 1
            ch.link(last)
            for t in range(TT * b, TT * b + TT):
                last = dve.bn_aggr(R.mv[:, t, :], R.stats[:, t, :])
                last.then_inc(R.chain, 1)
                ch.n += 1
            dve.wait_ge(R.chain, ch.n)
            dve.sem_inc(R.stats_done, 1)
        if b >= 1:
            dve.wait_ge(R.rstd_ready, b)
            for t in range(TT * b - TT, TT * b):
                xn = R.xn[t % len(R.xn)]
                if t >= len(R.xn):
                    dve.wait_ge(R.xn_turned, t - len(R.xn) + 1)
                    if stored is not None:
                        dve.wait_ge(stored[t % len(R.xn)], 16 * (t // len(R.xn)))
                norm = dve.tensor_scalar(xn[:], x[:, t, :], R.mv[:, t, 0:1], R.rstd[:, t:t + 1],
                                         ALU.subtract, ALU.mult)
                if col_scale is not None:
                    ch.link(norm)
                    norm = dve.tensor_tensor(xn[:], xn[:], col_scale, ALU.mult)
                norm.then_inc(R.xn_ready, 1)
                if t >= 1:
                    low(t - 1)
    low(NT - 1)


def ln_tensor(pe, R, ident, after=None):
    for t in range(NT):
        pe.wait_ge(R.xn_ready, t + 1)
        if t >= 2:
            pe.wait_ge(R.xT_ready, t - 1)
        for k in range(KC):
            last = pe.transpose(R.psT[t % 2][:, k * P:(k + 1) * P], R.xn[t % len(R.xn)][:, k * P:(k + 1) * P], ident)
        last.then_inc(R.xn_turned, 1)
        if after is not None:
            after(t)


def ln_scalar(act, R, dst, before=None, after=None):
    for t in range(NT):
        if before is not None:
            before(t)
        act.wait_ge(R.xn_turned, t + 1)
        act.activation(dst(t)[0], R.psT[t % 2][:].rearrange("p (k n) -> p k n", k=KC),
                       ACT.Copy).then_inc(R.hi_ready, 1)
        if after is not None:
            after(t)


def program(nc, io):
    out = io["out"]
    had_dram = nc.dram_tensor("wd_h128", (NF, P, C), F32, kind="Internal").ap()
    xn_dram = nc.dram_tensor("moe_xn", (TOK, C), F32, kind="Internal").ap()
    table_dram = nc.dram_tensor("moe_slot_token", (P * TILES * SUBS, 1), I32, kind="Internal").ap()
    y_dram = nc.dram_tensor("moe_y", (TILES * SLOTS, C), F32, kind="Internal").ap()
    fold_dram = nc.dram_tensor("wd_folded", (NF, P, C), F32, kind="Internal").ap()
    with ExitStack() as top:
        x = top.enter_context(nc.sbuf_tensor("x", [P, NT, C], F32))
        ident = top.enter_context(nc.sbuf_tensor("ident", [P, P], F32))
        G = Bag()
        G.x, G.ident, G.ident_t = x, ident[:], ident
        G.had_dram, G.fold_dram = had_dram, fold_dram
        G.xn_dram, G.table_dram, G.y_dram = xn_dram, table_dram, y_dram
        channel_attention(nc, io, G)
        with ExitStack() as moe:
            sb, _, _ = scope(nc, moe, "route")
            G.pos = [sb(f"slot{k}", [P, NT], I32) for k in range(2)]
            G.weight = [sb(f"weight{k}", [P, NT], F32) for k in range(2)]
            G.slot_token = sb("slot_token", [P, TILES * SUBS], I32)
            G.tile_expert = sb("tile_expert", [P, TILES], I32)
            gated_ffn(nc, io, G, "moe", weights=io["shared_w"], down=None, NG=3, GC=4, LAST=3)
            sparse_experts(nc, io, G)
        cross_attention(nc, io, G)
        gated_ffn(nc, io, G, "ffn", weights=io["ffn_w"], down=fold_dram, NG=4, GC=4, LAST=4)


def scope(nc, ctx, name):
    def sb(n, shape, dt):
        return ctx.enter_context(nc.sbuf_tensor(f"{name}_{n}", shape, dt))

    def ps(n, cols=512):
        return ctx.enter_context(nc.psum_tensor(f"{name}_{n}", [P, cols], F32))

    def sem(n):
        return ctx.enter_context(nc.semaphore(f"{name}_{n}"))

    return sb, ps, sem


def xT_tile(R):
    return lambda t: (R.xTh[:, :, t * P:(t + 1) * P], R.xTl[:, :, t * P:(t + 1) * P])


def channel_attention(nc, io, G):
    with ExitStack() as ctx:
        sb, ps, sem = scope(nc, ctx, "ca")
        first_sem = sem("first")
        R = ln_buffers(sb, ps, sem)
        x, ident = G.x, G.ident
        ctxr = sb("ctx", [P, B, KV, S], F32)
        ctxh, ctxl = sb("ctx_hi", [P, B, KV, S], F32R), sb("ctx_lo", [P, B, KV, S], F32R)
        wr = sb("wqk", [P, 2, KV, D], F32)
        wh, wl = sb("wqk_hi", [P, 2, KV, D], F32R), sb("wqk_lo", [P, 2, KV, D], F32R)
        bias = sb("bqk", [P, 2], F32)
        qkh, qkl = sb("qk_hi", [P, 2, S], F32R), sb("qk_lo", [P, 2, S], F32R)
        prob = [sb(f"prob{i}", [P, S], F32) for i in range(4)]
        mx = sb("max", [P, NT], F32)
        nmx = sb("minus_max", [P, NT], F32)
        tot = sb("total", [P, NT], F32)
        inv = sb("inverse", [P, NT], F32)
        Ah, Al = sb("attnT_hi", [P, TT, S], F32R), sb("attnT_lo", [P, TT, S], F32R)
        had = sb("h128", [P, P], F32)
        hadr = sb("h128_r", [P, P], F32R)
        wdp = sb("wscale_dp", [P, C], F32)
        wdr = [sb(f"wd_raw{i}", [P, C], F32) for i in range(2)]
        wds = [sb(f"wd_scaled{i}", [P, C], F32) for i in range(2)]
        wdh = [sb(f"wd_hi{i}", [P, C], F32R) for i in range(2)]
        wdl = [sb(f"wd_lo{i}", [P, C], F32R) for i in range(2)]
        wdz = R.xn
        psS = [ps(f"ps_s{i}") for i in range(2)]
        psQ = [ps(f"ps_q{i}") for i in range(2)]
        psX = [ps(f"ps_x{i}") for i in range(2)]
        psA = R.psT
        x_loaded = [sem(f"x_loaded{b}") for b in range(B)]
        M = Bag()
        M.small_loaded = sem("small_loaded")
        M.ctx_loaded = sem("ctx_loaded")
        M.const_loaded = sem("const_loaded")
        M.wd_loaded0 = sem("wd_loaded0")
        M.wd_loaded1 = sem("wd_loaded1")
        M.wd_stored0 = sem("wd_stored0")
        M.wd_stored1 = sem("wd_stored1")
        M.w_hi = sem("w_hi")
        M.w_ready = sem("w_ready")
        M.ctx_hi = sem("ctx_hi")
        M.ctx_ready = sem("ctx_ready")
        M.had_ready = sem("had_ready")
        M.qk_done = sem("qk_done")
        M.qk_hi = sem("qk_hi")
        M.qk_ready = sem("qk_ready")
        M.s_done = sem("s_done")
        M.max_ready = sem("max_ready")
        M.exp_done = sem("exp_done")
        M.norm_ready = sem("norm_ready")
        M.a_turned = sem("a_turned")
        M.a_hi = sem("a_hi")
        M.a_ready = sem("a_ready")
        M.x_done = sem("x_done")
        M.x_added = sem("x_added")
        M.chain = sem("chain")
        M.wd_scaled = sem("wd_scaled")
        M.wd_hi = sem("wd_hi")
        M.wd_ready = sem("wd_ready")
        M.wd_done = sem("wd_done")
        M.wd_out = sem("wd_out")
        wd_loaded, wd_stored = [M.wd_loaded0, M.wd_loaded1], [M.wd_stored0, M.wd_stored1]
        G.used_sems = range(first_sem.num, M.wd_out.num + 1)

        with nc.Block() as block:

            @block.sync
            def _(sp):
                sp.dma_start(G.ident_t[:], io["ident"]).then_inc(M.const_loaded, 16)
                for b in range(B):
                    sp.dma_start(x[:, TT * b:TT * b + TT, :],
                                 io["x"][b].rearrange("(t p) c -> p t c", p=P)).then_inc(x_loaded[b], 16)
                sp.dma_start(wr[:], io["ca_w"]).then_inc(M.small_loaded, 16)
                sp.dma_start(bias[:], io["ca_b"]).then_inc(M.small_loaded, 16)
                sp.dma_start(ctxr[:], io["ctxT"].rearrange("b p k s -> p b k s")).then_inc(M.ctx_loaded, 16)
                sp.dma_start(had[:], io["h128"]).then_inc(M.const_loaded, 16)
                sp.dma_start(wdp[:], io["wscale_dp"].partition_broadcast(P)).then_inc(M.const_loaded, 16)
                for n in range(NF):
                    if n >= 2:
                        sp.wait_ge(M.wd_scaled, n - 1)
                    sp.dma_start(wdr[n % 2][:], io["wdT"][n]).then_inc(wd_loaded[n % 2], 16)
                    if n >= 1:
                        sp.wait_ge(M.wd_out, n)
                        sp.dma_start(G.had_dram[n - 1], wdz[(n - 1) % 2][:]).then_inc(wd_stored[(n - 1) % 2], 16)
                sp.wait_ge(M.wd_out, NF)
                sp.dma_start(G.had_dram[NF - 1], wdz[(NF - 1) % 2][:]).then_inc(wd_stored[(NF - 1) % 2], 16)
                for i in range(2):
                    sp.wait_ge(wd_stored[i], 16 * (NF // 2))

            @block.gpsimd
            def _(pool):
                ln_gpsimd(pool, R)
                for n in range(NF):
                    pool.wait_ge(M.wd_hi, n + 1)
                    if n >= 2:
                        pool.wait_ge(M.wd_done, n - 1)
                    pool.tensor_tensor(wdl[n % 2][:], wds[n % 2][:], f32(wdh[n % 2][:]),
                                       ALU.subtract).then_inc(M.wd_ready, 1)

            def quarters():
                return range(NT)

            @block.scalar
            def _(act):
                act.wait_ge(M.small_loaded, 32)
                act.activation(wh[:], wr[:], ACT.Copy).then_inc(M.w_hi, 1)
                act.wait_ge(M.ctx_loaded, 16)
                act.activation(ctxh[:], ctxr[:], ACT.Copy).then_inc(M.ctx_hi, 1)
                ln_scalar(act, R, xT_tile(R))
                act.wait_ge(M.const_loaded, 48)
                act.activation(hadr[:], had[:], ACT.Copy).then_inc(M.had_ready, 1)

                def qk_high(b):
                    for j in range(2):
                        act.wait_ge(M.qk_done, 2 * b + j + 1)
                        act.activation(qkh[:, j, :], psQ[j][:], ACT.Identity,
                                       bias=bias[:, j:j + 1]).then_inc(M.qk_hi, 1)

                def exp(i):
                    act.wait_ge(M.max_ready, i + 1)
                    if i >= 4:
                        act.wait_ge(M.a_turned, i - 3)
                    act.activation(prob[i % 4][:], psS[i % 2][:], ACT.Exp, bias=nmx[:, i:i + 1],
                                   accum_out=tot[:, i:i + 1]).then_inc(M.exp_done, 1)

                def wd_high(n):
                    act.wait_ge(M.wd_scaled, n + 1)
                    if n >= 2:
                        act.wait_ge(M.wd_done, n - 1)
                    act.activation(wdh[n % 2][:], wds[n % 2][:], ACT.Copy).then_inc(M.wd_hi, 1)

                def wd_out(n):
                    act.wait_ge(M.wd_done, n + 1)
                    if n >= 2:
                        act.wait_ge(wd_stored[n % 2], 16 * (n // 2))
                    act.activation(wdz[n % 2][:], psX[n % 2][:], ACT.Copy).then_inc(M.wd_out, 1)

                qk_high(0)
                exp(0)
                exp(1)
                for i in quarters():
                    b, tt = divmod(i, TT)
                    wd_high(i)
                    act.wait_ge(M.a_turned, i + 1)
                    if tt == 0 and b >= 1:
                        act.wait_ge(M.x_done, TT * b)
                    act.activation(Ah[:, :, tt * P:(tt + 1) * P], psA[i % 2][:].rearrange("p (k n) -> p k n", k=TT),
                                   ACT.Copy).then_inc(M.a_hi, 1)
                    if tt < 2:
                        exp(i + 2)
                    wd_out(i)
                    if tt == 3 and b + 1 < B:
                        qk_high(b + 1)
                        exp(i + 1)
                        exp(i + 2)

            @block.vector
            def _(dve):
                dve.wait_ge(M.w_hi, 1)
                dve.tensor_tensor(wl[:], wr[:], f32(wh[:]), ALU.subtract).then_inc(M.w_ready, 1)
                ln_vector(dve, R, x, xT_tile(R), x_loaded=x_loaded)
                dve.wait_ge(M.ctx_hi, 1)
                dve.tensor_tensor(ctxl[:], ctxr[:], f32(ctxh[:]), ALU.subtract).then_inc(M.ctx_ready, 1)
                dve.wait_ge(M.const_loaded, 48)
                ch = Chain(dve, M.chain)

                def qk_low(b):
                    for j in range(2):
                        dve.wait_ge(M.qk_hi, 2 * b + j + 1)
                        dve.scalar_tensor_tensor(out=qkl[:, j, :], in0=psQ[j][:], scalar=bias[:, j:j + 1],
                                                 in1=f32(qkh[:, j, :]), op0=ALU.add,
                                                 op1=ALU.subtract).then_inc(M.qk_ready, 1)

                def row_max(i):
                    dve.wait_ge(M.s_done, i + 1)
                    ch.link(dve.reduce_max(mx[:, i:i + 1], psS[i % 2][:], axis=AX.X))
                    dve.tensor_scalar(nmx[:, i:i + 1], mx[:, i:i + 1], -1.0, None, ALU.mult).then_inc(M.max_ready, 1)

                def normalise(i):
                    dve.wait_ge(M.exp_done, i + 1)
                    ch.link(dve.reciprocal(inv[:, i:i + 1], tot[:, i:i + 1]))
                    dve.tensor_scalar(prob[i % 4][:], prob[i % 4][:], inv[:, i:i + 1], None,
                                      ALU.mult).then_inc(M.norm_ready, 1)

                def attn_low(i):
                    tt = i % TT
                    dve.wait_ge(M.a_hi, i + 1)
                    dve.tensor_tensor(Al[:, :, tt * P:(tt + 1) * P], psA[i % 2][:].rearrange("p (k n) -> p k n", k=TT),
                                      f32(Ah[:, :, tt * P:(tt + 1) * P]), ALU.subtract).then_inc(M.a_ready, 1)

                def scale_wd(n):
                    dve.wait_ge(wd_loaded[n % 2], 16 * (n // 2 + 1))
                    if n >= 2:
                        dve.wait_ge(M.wd_ready, n - 1)
                    dve.tensor_tensor(wds[n % 2][:], wdr[n % 2][:], wdp[:], ALU.mult).then_inc(M.wd_scaled, 1)

                def add_x(b):
                    for lt in range(TT):
                        t = TT * b + lt
                        dve.wait_ge(M.x_done, t + 1)
                        dve.tensor_tensor(x[:, t, :], psX[lt % 2][:], x[:, t, :], ALU.add).then_inc(M.x_added, 1)

                qk_low(0)
                row_max(0)
                row_max(1)
                for i in quarters():
                    b, tt = divmod(i, TT)
                    scale_wd(i)
                    normalise(i)
                    attn_low(i)
                    if tt < 2:
                        row_max(i + 2)
                    if tt == 3:
                        if b + 1 < B:
                            qk_low(b + 1)
                            row_max(i + 1)
                            row_max(i + 2)
                        add_x(b)

            @block.tensor
            def _(pe):
                pe.wait_ge(M.const_loaded, 48)
                ln_tensor(pe, R, ident)
                pe.wait_ge(M.w_ready, 1)
                pe.wait_ge(M.ctx_ready, 1)

                def qk(b):
                    if b >= 1:
                        pe.wait_ge(M.qk_ready, 2 * b)
                    for j in range(2):
                        for k in range(KV):
                            last = product(pe, psQ[j][:], (wh[:, j, k, :], wl[:, j, k, :]),
                                           (ctxh[:, b, k, :], ctxl[:, b, k, :]), k == 0, k == KV - 1)
                        last.then_inc(M.qk_done, 1)

                def scores(i):
                    b, mt = divmod(i, TT)
                    pe.wait_ge(M.qk_ready, 2 * b + 2)
                    if i >= 2:
                        pe.wait_ge(M.exp_done, i - 1)
                    m = slice(mt * P, (mt + 1) * P)
                    product(pe, psS[i % 2][:], (qkh[:, 0, m], qkl[:, 0, m]), (qkh[:, 1, :], qkl[:, 1, :]),
                            True, True).then_inc(M.s_done, 1)

                def turn(i):
                    pe.wait_ge(M.norm_ready, i + 1)
                    pe.wait_ge(R.xT_ready, NT)
                    if i >= 2:
                        pe.wait_ge(M.a_ready, i - 1)
                    for k in range(TT):
                        last = pe.transpose(psA[i % 2][:, k * P:(k + 1) * P], prob[i % 4][:, k * P:(k + 1) * P], ident)
                    last.then_inc(M.a_turned, 1)

                def wd(n):
                    pe.wait_ge(M.had_ready, 1)
                    pe.wait_ge(M.wd_ready, n + 1)
                    if n >= 2:
                        pe.wait_ge(M.wd_out, n - 1)
                    if n >= TT:
                        pe.wait_ge(M.x_added, TT * (n // TT))
                    pe.matmul(psX[n % 2][:], hadr[:], wdh[n % 2][:], start=True, stop=False)
                    pe.matmul(psX[n % 2][:], hadr[:], wdl[n % 2][:], start=False, stop=True).then_inc(M.wd_done, 1)

                def weighted(b):
                    pe.wait_ge(M.a_ready, TT * b + TT)
                    pe.wait_ge(M.wd_out, TT * b + TT)
                    for lt in range(TT):
                        t = TT * b + lt
                        if lt >= 2:
                            pe.wait_ge(M.x_added, t - 1)
                        for k in range(KC):
                            last = product(pe, psX[lt % 2][:], (R.xTh[:, k, t * P:(t + 1) * P], R.xTl[:, k, t * P:(t + 1) * P]),
                                           (Ah[:, k, :], Al[:, k, :]), k == 0, k == KC - 1)
                        last.then_inc(M.x_done, 1)

                qk(0)
                scores(0)
                scores(1)
                for i in quarters():
                    b, tt = divmod(i, TT)
                    turn(i)
                    if tt < 2:
                        scores(i + 2)
                    wd(i)
                    if tt == 3:
                        if b + 1 < B:
                            qk(b + 1)
                            scores(i + 1)
                            scores(i + 2)
                        weighted(b)


def gated_ffn(nc, io, G, name, weights, down, NG, GC, LAST):
    moe = name == "moe"
    STEPS = B * GC
    LINKS = 2
    with ExitStack() as ctx:
        sb, ps, sem = scope(nc, ctx, name)
        x, ident = G.x, G.ident
        raw = [sb(f"w_raw{j}", [P, WSLICE], F32) for j in range(GC)]
        whi = [sb(f"w_hi{j}", [P, WSLICE], F32R) for j in range(GC)]
        wlo = [sb(f"w_lo{j}", [P, WSLICE], F32R) for j in range(GC)]
        act_out = [sb(f"silu{i}", [P, S], F32) for i in range(2)]
        hhi = [sb(f"hidden_hi{i}", [P, S], F32R) for i in range(2)]
        hlo = [sb(f"hidden_lo{i}", [P, S], F32R) for i in range(2)]
        psG = [ps(f"ps_gate{i}") for i in range(2)]
        psU = [ps(f"ps_up{i}") for i in range(2)]
        psY = [ps(f"ps_y{i}") for i in range(TT)]
        banks = iter((psY[0], psY[1]))
        xn = [sb(f"xn{i}", [P, C], F32) for i in range(4 if moe else 2)]
        R = ln_buffers(sb, lambda n: next(banks), sem, xn=xn)
        hidden = xn[0:2]
        M = Bag()
        M.w_hi = sem("w_hi")
        M.w_ready = sem("w_ready")
        M.gate_done = sem("gate_done")
        M.up_done = sem("up_done")
        M.silu_done = sem("silu_done")
        M.hidden_steps = sem("hidden_steps")
        M.hidden_ready = sem("hidden_ready")
        M.hidden_free = sem("hidden_free")
        M.y_added = sem("y_added")
        M.const_loaded = sem("const_loaded")
        M.stored = sem("stored")
        M.prep = sem("prep")
        M.prep_pool = sem("prep_pool")
        M.prep_pe = sem("prep_pe")
        M.prep_act = sem("prep_act")
        M.fold_loaded = sem("fold_loaded")
        M.fold_stored = sem("fold_stored")
        M.now_ready = sem("now_ready")
        raw_loaded = [sem(f"raw_loaded{j}") for j in range(GC)]
        raw_parts = 1 if down is None else 2
        if moe:
            gr = sb("router", [P, KC, RG], F32)
            grh, grl = sb("router_hi", [P, KC, RG], F32R), sb("router_lo", [P, KC, RG], F32R)
            consts = sb("route_consts", [P, E * E + E + TILES], F32)
            lower = consts[:, 0:E * E].rearrange("p (a b) -> p a b", a=E)
            fills = consts[:, E * E:E * E + E]
            tiles = consts[:, E * E + E:]
            sums = sb("sums", [P, 2, P], F32)
            sums_r = sb("sums_r", [P, 2, P], F32R)
            lg = sb("logits", [P, NT, RG], F32)
            pr = sb("probs", [P, NT, E], F32)
            sc1 = sb("row_scratch", [P, NT], F32)
            sig = sb("shared_gate", [P, NT], F32)
            beats = sb("beats", [P, NT // 4, E, E], F32)
            ties = sb("ties", [P, NT // 4, E, E], F32)
            rank = sb("rank", [P, NT, E], F32)
            first = [sb(f"is_entry{k}", [P, NT, E], F32) for k in range(2)]
            chosen = sb("chosen", [P, NT, E], F32R)
            slot = sb("slot", [P, NT, E], F32)
            scr = sb("route_scratch", [P, NT, E], F32)
            load = sb("expert_load", [P, E], F32)
            ntile = sb("expert_tiles", [P, E], F32)
            start = sb("expert_start", [P, E], F32)
            end = sb("expert_end", [P, E], F32)
            ge = sb("tile_past", [P, TILES, E], F32)
            te = sb("tile_expert_f", [P, TILES], F32)
            posf = [sb(f"slot_f{k}", [P, NT], F32) for k in range(2)]
            low7 = sb("slot_low", [P, NT], I32)
            high = sb("slot_high", [P, NT], I32)
            place = [sb(f"table_place{k}", [P, NT], I32) for k in range(2)]
            ids = sb("token_ids", [P, NT], I32)
            nothing = sb("zeros", [P, TILES * SUBS], I32)
            xn_stored = [sem(f"xn_stored{i}") for i in range(4)]
            M.routed = sem("routed")
            M.counted = sem("counted")
            M.route_chain = sem("route_chain")
            M.places_ready = sem("places_ready")
            M.fill_ready = sem("fill_ready")
            M.table_filled = sem("table_filled")
            M.scattered = sem("scattered")
            M.table_loaded = sem("table_loaded")
            FOLD = 32
            fold = [sb(f"fold{i}", [P, NF, FOLD], F32) for i in range(2)]
        else:
            had = sb("h128", [P, P], F32)
            hadr = sb("h128_r", [P, 2, P], F32R)
            su_ug = sb("su_ug", [P, C], F32)
            tabs = sb("tables", [P, 3, NF], F32)
            scales = sb("scales", [P, 2, NF], F32)
            now = sb("scales_now", [P, 2, GC], F32)
            uTh, uTl = sb("uT_hi", [P, KC, S], F32R), sb("uT_lo", [P, KC, S], F32R)

        def u_tile(t):
            tt = t % TT
            return uTh[:, :, tt * P:(tt + 1) * P], uTl[:, :, tt * P:(tt + 1) * P]

        ln_dst = xT_tile(R) if moe else u_tile

        def groups(eng, body):
            with eng.Fori(0, NG - 1) as g:
                body(g, GC, False)
            body(NG - 1, LAST, True)

        with nc.Block() as block:

            @block.sync
            def _(sp):
                if moe:
                    sp.dma_start(gr[:], io["router"]).then_inc(M.const_loaded, 16)
                    sp.dma_start(consts[:], io["route_consts"].partition_broadcast(P)).then_inc(M.const_loaded, 16)
                    sp.dma_start(sums[:], io["sums"]).then_inc(M.const_loaded, 16)
                else:
                    sp.dma_start(had[:], io["h128"]).then_inc(M.const_loaded, 16)
                    sp.dma_start(su_ug[:], io["su_ug"].partition_broadcast(P)).then_inc(M.const_loaded, 16)
                    sp.dma_start(tabs[:], io["ffn_tables"]).then_inc(M.const_loaded, 16)

                def load_chunk(g, j):
                    if down is None:
                        sp.dma_start(raw[j][:], weights[g * GC + j]).then_inc(raw_loaded[j], 16)
                    else:
                        sp.dma_start(raw[j][:, 0:2 * C], weights[g * GC + j]).then_inc(raw_loaded[j], 16)
                        sp.dma_start(raw[j][:, 2 * C:], down[g * GC + j]).then_inc(raw_loaded[j], 16)

                for j in range(GC):
                    load_chunk(0, j)
                if moe:
                    for t in range(NT):
                        sp.wait_ge(R.xn_ready, t + 1)
                        sp.dma_start(G.xn_dram[t * P:(t + 1) * P, :], xn[t % 4][:]).then_inc(xn_stored[t % 4], 16)

                def refill(g, gc):
                    for j in range(gc):
                        sp.wait_ge(M.w_ready, ((g - 1) * GC + j + 1) * 3)
                        load_chunk(g, j)

                with sp.Fori(1, NG - 1) as g:
                    refill(g, GC)
                refill(NG - 1, LAST)
                if moe:
                    for i in range(4):
                        sp.wait_ge(xn_stored[i], 16 * (NT // 4))
                if not moe:
                    for t in range(NT):
                        sp.wait_ge(M.y_added, NT * (NG - 1) + t + 2)
                        sp.dma_start(io["out"][t // TT, (t % TT) * P:(t % TT + 1) * P, :], x[:, t, :]).then_inc(M.stored, 16)
                    sp.wait_ge(M.stored, 16 * NT)

            @block.gpsimd
            def _(pool):
                ln_gpsimd(pool, R)
                if moe:
                    ch = Chain(pool, M.prep_pool)
                    had_v, fold_v = (d.rearrange("n p c -> p n c") for d in (G.had_dram, G.fold_dram))
                    for k in range(C // FOLD):
                        c = slice(k * FOLD, (k + 1) * FOLD)
                        if k >= 1:
                            pool.wait_ge(M.fold_stored, 16 * k)
                        pool.dma_start(fold[0][:], had_v[:, :, c]).then_inc(M.fold_loaded, 16)
                        pool.wait_ge(M.fold_loaded, 16 * (k + 1))
                        for st in range(4):
                            src = fold[st % 2][:].rearrange("p (a two b) c -> p a two (b c)", two=2, b=1 << st)
                            dst = fold[1 - st % 2][:].rearrange("p (a two b) c -> p a two (b c)", two=2, b=1 << st)
                            pool.tensor_tensor(dst[:, :, 0, :], src[:, :, 0, :], src[:, :, 1, :], ALU.add).then_inc(M.prep_pool, 1)
                            ch.n += 1
                            ch.link(pool.tensor_tensor(dst[:, :, 1, :], src[:, :, 0, :], src[:, :, 1, :], ALU.subtract))
                        pool.dma_start(fold_v[:, :, c], fold[0][:]).then_inc(M.fold_stored, 16)
                    pool.wait_ge(M.fold_stored, 16 * (C // FOLD))
                    pool.iota(ids[:], pattern=[[P, NT]], base=0, channel_multiplier=1).then_inc(M.fill_ready, 1)
                    pool.memset(nothing[:], 0).then_inc(M.fill_ready, 1)
                    pool.wait_ge(M.fill_ready, 2)
                    pool.dma_start(G.table_dram.rearrange("(p n) one -> p (n one)", p=P), nothing[:]).then_inc(M.table_filled, 16)
                    pool.wait_ge(M.table_filled, 16)
                    pool.wait_ge(M.places_ready, 2)
                    for k in range(2):
                        for t in range(NT):
                            pool.indirect_dma_start(
                                out=G.table_dram, out_offset=bass.IndirectOffsetOnAxis(ap=place[k][:, t:t + 1], axis=0),
                                in_=ids[:, t:t + 1], in_offset=None).then_inc(M.scattered, 16)
                    pool.wait_ge(M.scattered, 16 * 2 * NT)
                    pool.dma_start(G.slot_token[:], G.table_dram.rearrange("(p n) one -> p (n one)", p=P)).then_inc(M.table_loaded, 16)
                    pool.wait_ge(M.table_loaded, 16)

            @block.scalar
            def _(act):
                def split_hi(g, j):
                    act.wait_ge(raw_loaded[j], 16 * raw_parts * (g + 1))
                    for part in range(3):
                        c = slice(part * C, (part + 1) * C)
                        act.activation(whi[j][:, c], raw[j][:, c], ACT.Copy).then_inc(M.w_hi, 1)

                if moe:
                    act.wait_ge(M.const_loaded, 48)
                    act.activation(grh[:], gr[:], ACT.Copy).then_inc(M.prep_act, 1)
                    act.activation(sums_r[:], sums[:], ACT.Copy).then_inc(M.prep_act, 1)
                    ln_scalar(act, R, ln_dst)
                    act.wait_ge(M.prep_pe, 1)
                    act.activation(lg[:], psG[1][:, 0:NT * RG].rearrange("p (t e) -> p t e", t=NT), ACT.Copy).then_inc(M.prep_act, 1)
                    act.wait_ge(M.prep, 3)
                    act.activation(pr[:], pr[:], ACT.Exp).then_inc(M.prep_act, 1)
                    act.activation(sig[:], lg[:, :, E], ACT.Sigmoid).then_inc(M.prep_act, 1)
                else:
                    act.wait_ge(M.const_loaded, 48)
                    act.activation(hadr[:, 0, :], had[:], ACT.Copy).then_inc(M.prep_act, 1)
                    act.activation(hadr[:, 1, :], had[:], ACT.Copy, scale=-1.0).then_inc(M.prep_act, 1)

                    def rotated(t):
                        if t % TT == TT - 1:
                            b = t // TT
                            for m in range(KC):
                                act.wait_ge(M.prep_pe, KC * b + m + 1)
                                act.activation(R.xTh[:, m, b * S:(b + 1) * S], psG[m % 2][:], ACT.Copy).then_inc(M.prep_act, 1)

                    def uT_free(t):
                        if t % TT == 0 and t:
                            act.wait_ge(M.prep_pe, KC * (t // TT))
                    ln_scalar(act, R, ln_dst, before=uT_free, after=rotated)

                for j in range(GC - 2):
                    split_hi(0, j)

                def body(g, gc, last):
                    for s in range(B * gc):
                        b, j = divmod(s, gc)
                        if s < gc - (GC - 2):
                            act.wait_ge(M.hidden_free, g * STEPS + s + 1)
                            split_hi(g, GC - 2 + s)
                        if b == B - 1 and j >= 2 and not last:
                            act.wait_ge(M.hidden_free, g * STEPS + s + 1)
                            split_hi(g + 1, j - 2)
                        act.wait_ge(M.gate_done, g * STEPS + s + 1)
                        act.wait_ge(M.hidden_steps, (g * STEPS + s) * LINKS + 1)
                        if not moe and s == 0:
                            act.wait_ge(M.now_ready, g + 1)
                        ins = act.activation(act_out[s % 2][:], psG[s % 2][:], ACT.Silu, scale=1.0 if moe else now[:, 1, j:j + 1])
                        ins.then_inc(M.silu_done, 1)

                groups(act, body)

            @block.vector
            def _(dve):
                def split_lo(g, j):
                    for part in range(3):
                        c = slice(part * C, (part + 1) * C)
                        dve.wait_ge(M.w_hi, (g * GC + j) * 3 + part + 1)
                        last = dve.tensor_tensor(wlo[j][:, c], raw[j][:, c], f32(whi[j][:, c]), ALU.subtract)
                        last.then_inc(M.w_ready, 1)

                if moe:
                    dve.wait_ge(M.prep_act, 1)
                    dve.tensor_tensor(grl[:], gr[:], f32(grh[:]), ALU.subtract).then_inc(M.prep, 1)
                    ln_vector(dve, R, x, ln_dst, stored=xn_stored)
                    ch = Chain(dve, M.prep)
                    ch.n = 1
                    dve.wait_ge(M.prep_act, 3)
                    ch.link(dve.reduce_max(sc1[:], lg[:, :, 0:E], axis=AX.X))
                    ch.link(dve.tensor_tensor(pr[:], lg[:, :, 0:E], sc1[:].unsqueeze(2).broadcast_to([P, NT, E]), ALU.subtract))
                    for i in range(2):
                        dve.wait_ge(xn_stored[i], 16 * (NT // 4))
                    rt = Chain(dve, M.route_chain)

                    def rank_experts(q):
                        if q == 0:
                            dve.wait_ge(M.prep_act, 4)
                            rt.link(dve.reduce_sum(sc1[:], pr[:], axis=AX.X))
                            rt.link(dve.reciprocal(sc1[:], sc1[:]))
                            rt.link(dve.tensor_tensor(pr[:], pr[:], sc1[:].unsqueeze(2).broadcast_to([P, NT, E]), ALU.mult))
                        t = slice(4 * q, 4 * q + 4)
                        own = pr[:, t, :].unsqueeze(3).broadcast_to([P, 4, E, E])
                        other = pr[:, t, :].unsqueeze(2).broadcast_to([P, 4, E, E])
                        rt.link(dve.tensor_tensor(beats[:], other, own, ALU.is_gt))
                        rt.link(dve.tensor_tensor(ties[:], other, own, ALU.is_equal))
                        rt.link(dve.tensor_tensor(ties[:], ties[:], lower.unsqueeze(1).broadcast_to([P, 4, E, E]), ALU.mult))
                        rt.link(dve.tensor_tensor(beats[:], beats[:], ties[:], ALU.add))
                        rt.link(dve.reduce_sum(rank[:, t, :], beats[:], axis=AX.X))

                    def choose():
                        for k in range(2):
                            rt.link(dve.tensor_scalar(first[k][:], rank[:], float(k), None, ALU.is_equal))
                            rt.link(dve.tensor_tensor(scr[:], pr[:], first[k][:], ALU.mult))
                            rt.link(dve.reduce_sum(G.weight[k][:], scr[:], axis=AX.X))
                        dve.tensor_tensor(chosen[:], first[0][:], first[1][:], ALU.add).then_inc(M.routed, 1)

                    def count():
                        dve.wait_ge(M.counted, 1)
                        dve.tensor_copy(slot[:], psG[0][:, 0:NT * E].rearrange("p (t e) -> p t e", t=NT)).then_inc(M.routed, 1)
                        dve.tensor_copy(load[:], psU[0][:, 0:E]).then_inc(M.routed, 1)
                        dve.wait_ge(M.routed, 3)

                    def place_tiles():
                        rt.link(dve.tensor_tensor(beats[:, 0, :, :], load[:].unsqueeze(2).broadcast_to([P, E, E]),
                                                  fills.unsqueeze(1).broadcast_to([P, E, E]), ALU.is_gt))
                        rt.link(dve.reduce_sum(ntile[:], beats[:, 0, :, :], axis=AX.X))
                        rt.link(dve.tensor_tensor(ties[:, 0, :, :], ntile[:].unsqueeze(1).broadcast_to([P, E, E]), lower, ALU.mult))
                        rt.link(dve.reduce_sum(start[:], ties[:, 0, :, :], axis=AX.X))
                        rt.link(dve.tensor_tensor(end[:], start[:], ntile[:], ALU.add))
                        rt.link(dve.tensor_tensor(ge[:], end[:].unsqueeze(1).broadcast_to([P, TILES, E]),
                                                  tiles.unsqueeze(2).broadcast_to([P, TILES, E]), ALU.is_le))
                        rt.link(dve.reduce_sum(te[:], ge[:], axis=AX.X))
                        rt.link(dve.tensor_scalar(G.tile_expert[:], te[:], float(E - 1), None, ALU.min))
                        rt.link(dve.tensor_scalar(start[:], start[:], float(SLOTS), None, ALU.mult))
                        rt.link(dve.tensor_tensor(slot[:], slot[:], start[:].unsqueeze(1).broadcast_to([P, NT, E]), ALU.add))

                    def place_entries(k):
                        rt.link(dve.tensor_tensor(scr[:], slot[:], first[k][:], ALU.mult))
                        rt.link(dve.reduce_sum(posf[k][:], scr[:], axis=AX.X))
                        rt.link(dve.tensor_copy(G.pos[k][:], posf[k][:]))
                        rt.link(dve.tensor_scalar(low7[:], G.pos[k][:], P - 1, None, ALU.bitwise_and))
                        rt.link(dve.tensor_scalar(high[:], G.pos[k][:], P.bit_length() - 1, None, ALU.logical_shift_right))
                        rt.link(dve.tensor_scalar(posf[k][:], low7[:], float(TILES * SUBS), None, ALU.mult))
                        dve.tensor_tensor(place[k][:], posf[k][:], high[:], ALU.add).then_inc(M.places_ready, 1)

                    def route(s):
                        if s < 4:
                            rank_experts(s)
                        if s == 4:
                            choose()
                        if s == 5:
                            count()
                            place_tiles()
                        if s in (6, 7):
                            place_entries(s - 6)
                else:
                    dve.wait_ge(M.const_loaded, 48)
                    ch = Chain(dve, M.prep)
                    up_s, gate_s = scales[:, 0, :], scales[:, 1, :]
                    ch.link(dve.tensor_tensor(up_s, tabs[:, 0, :], tabs[:, 2, :], ALU.mult))
                    ch.link(dve.tensor_scalar(up_s, up_s, float((C * INTER) ** -0.5), None, ALU.mult))
                    ch.link(dve.tensor_scalar(gate_s, tabs[:, 1, :], float(C ** -0.5), None, ALU.mult))
                    dve.tensor_copy(now[:], scales[:, :, 0:GC]).then_inc(M.now_ready, 1)

                    def rotated(t):
                        if t % TT == TT - 1:
                            b = t // TT
                            for m in range(KC):
                                dve.wait_ge(M.prep_act, 2 + KC * b + m + 1)
                                dve.tensor_tensor(R.xTl[:, m, b * S:(b + 1) * S], psG[m % 2][:],
                                                  f32(R.xTh[:, m, b * S:(b + 1) * S]), ALU.subtract).then_inc(M.prep, 1)
                    ln_vector(dve, R, x, ln_dst, col_scale=su_ug[:], after_lo=rotated)

                dve.sem_inc(M.hidden_steps, 2 * LINKS)
                dve.sem_inc(M.y_added, 1)
                for j in range(GC - 2):
                    split_lo(0, j)
                def body(g, gc, last):
                    def add_x(b):
                        dve.wait_ge(M.hidden_free, g * STEPS + (b + 1) * gc + 2)
                        for lt in range(TT):
                            t = TT * b + lt
                            if moe:
                                if lt == 0:
                                    dve.wait_ge(M.prep_act, 5)
                                ins = dve.scalar_tensor_tensor(out=x[:, t, :], in0=psY[lt][:], scalar=sig[:, t:t + 1],
                                                               in1=x[:, t, :], op0=ALU.mult, op1=ALU.add)
                            else:
                                ins = dve.tensor_tensor(x[:, t, :], psY[lt][:], x[:, t, :], ALU.add)
                            ins.then_inc(M.y_added, 1)

                    for s in range(B * gc):
                        b, j = divmod(s, gc)
                        if s < gc - (GC - 2):
                            split_lo(g, GC - 2 + s)
                        if b == B - 1 and j >= 2 and not last:
                            split_lo(g + 1, j - 2)
                        at = g * STEPS + s
                        n = (at + 2) * LINKS
                        hid = hidden[s % 2]
                        dve.wait_ge(M.up_done, at + 1)
                        dve.wait_ge(M.silu_done, at + 1)
                        if moe:
                            ins = dve.tensor_tensor(hid[:], psU[s % 2][:], act_out[s % 2][:], ALU.mult)
                        else:
                            ins = dve.scalar_tensor_tensor(out=hid[:], in0=psU[s % 2][:], scalar=now[:, 0, j:j + 1],
                                                           in1=act_out[s % 2][:], op0=ALU.mult, op1=ALU.mult)
                        ins.then_inc(M.hidden_steps, 1)
                        dve.wait_ge(M.hidden_steps, n + 1)
                        dve.wait_ge(M.hidden_free, at + 1)
                        dve.tensor_copy(hhi[s % 2][:], hid[:]).then_inc(M.hidden_steps, 1)
                        dve.wait_ge(M.hidden_steps, n + LINKS)
                        dve.tensor_tensor(hlo[s % 2][:], hid[:], f32(hhi[s % 2][:]), ALU.subtract).then_inc(M.hidden_ready, 1)
                        if j == 0 and b >= 1:
                            add_x(b - 1)
                        if moe and last:
                            route(s)
                    if not moe and not last:
                        dve.tensor_copy(now[:], scales[:, :, bass.ds((g + 1) * GC, GC)]).then_inc(M.now_ready, 1)
                    add_x(B - 1)

                groups(dve, body)

            @block.tensor
            def _(pe):
                if moe:
                    ln_tensor(pe, R, ident)
                    pe.wait_ge(R.xT_ready, NT)
                    pe.wait_ge(M.prep, 1)
                    for t in range(NT):
                        for k in range(KC):
                            tok = slice(t * P, (t + 1) * P)
                            last = product(pe, psG[1][:, t * RG:(t + 1) * RG], (R.xTh[:, k, tok], R.xTl[:, k, tok]),
                                           (grh[:, k, :], grl[:, k, :]), k == 0, k == KC - 1)
                    last.then_inc(M.prep_pe, 1)
                    pe.wait_ge(M.prep_act, 3)

                    def count_entries(at):
                        pe.wait_ge(M.routed, 1)
                        pe.wait_ge(M.hidden_steps, at * LINKS + 1)
                        for d in range(NT):
                            pe.matmul(psG[0][:, d * E:NT * E], sums_r[:, min(d, 1), :],
                                      chosen[:, 0:NT - d, :].rearrange("p t e -> p (t e)"), start=d == 0, stop=d == NT - 1)
                        for t in range(NT):
                            last = pe.matmul(psU[0][:, 0:E], sums_r[:, 1, :], chosen[:, t, :], start=t == 0, stop=t == NT - 1)
                        last.then_inc(M.counted, 1)
                        pe.wait_ge(M.routed, 3)
                else:
                    def rotate(t):
                        if t % TT == TT - 1:
                            b = t // TT
                            pe.wait_ge(R.xT_ready, t + 1)
                            pe.wait_ge(M.prep_act, 2)
                            for m in range(KC):
                                if KC * b + m >= 2:
                                    pe.wait_ge(M.prep, 3 + KC * b + m - 1)
                                for k in range(KC):
                                    sign = bin(k & m).count("1") % 2
                                    pe.matmul(psG[m % 2][:], hadr[:, sign, :], uTh[:, k, :], start=k == 0, stop=False)
                                    last = pe.matmul(psG[m % 2][:], hadr[:, sign, :], uTl[:, k, :], start=False, stop=k == KC - 1)
                                last.then_inc(M.prep_pe, 1)
                    ln_tensor(pe, R, ident, after=rotate)
                    pe.wait_ge(M.prep, 3 + KC * B)

                pe.sem_inc(M.hidden_free, 2)

                def gate_up(g, gc, s):
                    b, j = divmod(s % (B * gc), gc)
                    at = g * STEPS + s
                    pe.wait_ge(M.w_ready, (g * GC + s // (B * gc) * gc + j + 1) * 3)
                    pe.wait_ge(M.hidden_steps, at * LINKS + 1)
                    for bank, o, done in ((psG, 0, M.gate_done), (psU, C, M.up_done)):
                        for k in range(KC):
                            c = slice(o + k * P, o + (k + 1) * P)
                            tok = slice(b * S, (b + 1) * S)
                            last = product(pe, bank[s % 2][:], (whi[j][:, c], wlo[j][:, c]),
                                           (R.xTh[:, k, tok], R.xTl[:, k, tok]), k == 0, k == KC - 1)
                        last.then_inc(done, 1)

                def down_step(g, gc, s):
                    b, j = divmod(s, gc)
                    at = g * STEPS + s
                    pe.wait_ge(M.hidden_ready, at + 1)
                    if j == 0:
                        pe.wait_ge(M.y_added, (g * B + b) * TT + 1)
                    for lt in range(TT):
                        m = slice(lt * P, (lt + 1) * P)
                        last = product(pe, psY[lt][:], (hhi[s % 2][:, m], hlo[s % 2][:, m]),
                                       (whi[j][:, 2 * C:], wlo[j][:, 2 * C:]), j == 0, j == gc - 1)
                    last.then_inc(M.hidden_free, 1)

                def body(g, gc, last):
                    for s in range(B * gc):
                        if moe and last and s == 5:
                            count_entries(g * STEPS + s + 1)
                        if not (last and s == B * gc - 1):
                            gate_up(g, gc, s + 1)
                        down_step(g, gc, s)

                gate_up(0, GC, 0)
                groups(pe, body)


def sparse_experts(nc, io, G):
    GATE, UP, DOWN = 0, KC * F_MOE, 2 * KC * F_MOE
    PARTS = ((GATE, UP), (UP, DOWN), (DOWN, EW))
    widths = [min(P, F_MOE - f * P) for f in range(FCH)]
    with ExitStack() as ctx:
        sb, ps, sem = scope(nc, ctx, "ex")
        x, ident = G.x, G.ident
        raw = [sb(f"w_raw{i}", [P, EW], F32) for i in range(2)]
        whi = [sb(f"w_hi{i}", [P, EW], F32R) for i in range(2)]
        wlo = [sb(f"w_lo{i}", [P, EW], F32R) for i in range(2)]
        rows = [[sb(f"rows{i}_{u}", [P, C], F32) for u in range(SUBS)] for i in range(2)]
        xh = [sb(f"xT_hi{i}", [P, KC, SLOTS], F32R) for i in range(2)]
        xl = [sb(f"xT_lo{i}", [P, KC, SLOTS], F32R) for i in range(2)]
        silu = [sb(f"silu{f}", [P, SLOTS], F32) for f in range(FCH)]
        prod = [sb(f"hidden{f}", [P, SLOTS], F32) for f in range(FCH)]
        hh = [sb(f"hidden_hi{f}", [P, SLOTS], F32R) for f in range(FCH)]
        hl = [sb(f"hidden_lo{f}", [P, SLOTS], F32R) for f in range(FCH)]
        ysb = [sb(f"y{u}", [P, C], F32) for u in range(SUBS)]
        psT = [ps(f"ps_t{u}") for u in range(SUBS)]
        psH = [ps(f"ps_h{f}") for f in range(FCH)]
        psY = [ps(f"ps_y{u}") for u in range(SUBS)]
        M = Bag()
        raw_loaded = [sem(f"raw_loaded{i}") for i in range(2)]
        rows_loaded = [sem(f"rows_loaded{i}") for i in range(2)]
        y_stored = [sem(f"y_stored{u}") for u in range(SUBS)]
        M.w_hi = sem("w_hi")
        M.w_ready = sem("w_ready")
        M.turned = sem("turned")
        M.x_hi = sem("x_hi")
        M.x_ready = sem("x_ready")
        M.h_done = sem("h_done")
        M.silu_done = sem("silu_done")
        M.hidden_steps = sem("hidden_steps")
        M.hidden_ready = sem("hidden_ready")
        M.y_done = sem("y_done")
        M.y_copied = sem("y_copied")
        M.added = sem("added")
        entry_loaded = [sem(f"entry_loaded{i}") for i in range(4)]
        M.entry_used = sem("entry_used")

        def tiles(eng, body):
            with eng.Fori(0, TILES // 2) as i:
                for p in range(2):
                    body(2 * i + p, p, False)
            if TILES % 2:
                body(TILES - 1, 0, True)

        with nc.Block() as block:

            @block.sync
            def _(sp):
                def load(j, p):
                    expert = sp.value_load(G.tile_expert[0:1, bass.ds(j, 1)], min_val=0, max_val=E - 1)
                    sp.dma_start(raw[p][:], io["expert_w"][bass.ds(expert, 1), :, :].rearrange("one p n -> p (one n)")).then_inc(raw_loaded[p], 16)

                def store(j):
                    for u in range(SUBS):
                        sp.wait_ge(M.y_copied, SUBS * (j + 1) + u + 1)
                        sp.dma_start(G.y_dram[bass.ds(j * SLOTS + u * P, P), :], ysb[u][:]).then_inc(y_stored[u], 16)

                for u in range(SUBS):
                    sp.sem_inc(y_stored[u], 16)
                for j in range(2):
                    load(j, j)
                sp.sem_clear(G.used_sems)
                with sp.Fori(0, TILES // 2 - 1) as i:
                    for p in range(2):
                        sp.wait_ge(M.w_ready, (2 * i + p + 1) * 3)
                        load(2 * i + p + 2, p)
                        store(2 * i + p)
                for j in range(2 * (TILES // 2 - 1), TILES):
                    if j + 2 < TILES:
                        sp.wait_ge(M.w_ready, (j + 1) * 3)
                        load(j + 2, j % 2)
                    store(j)

            @block.gpsimd
            def _(pool):
                for j in range(TILES):
                    if j >= 2:
                        pool.wait_ge(M.turned, SUBS * (j - 1))
                    for u in range(SUBS):
                        n = j * SUBS + u
                        pool.indirect_dma_start(
                            out=rows[j % 2][u][:], out_offset=None, in_=G.xn_dram,
                            in_offset=bass.IndirectOffsetOnAxis(ap=G.slot_token[:, n:n + 1], axis=0)).then_inc(rows_loaded[j % 2], 16)
                for u in range(SUBS):
                    pool.wait_ge(y_stored[u], 16 * (TILES + 1))
                for n in range(2 * NT):
                    t, k = divmod(n, 2)
                    if n >= 4:
                        pool.wait_ge(M.entry_used, n - 3)
                    pool.indirect_dma_start(
                        out=rows[n // 2 % 2][n % 2][:], out_offset=None, in_=G.y_dram,
                        in_offset=bass.IndirectOffsetOnAxis(ap=G.pos[k][:, t:t + 1], axis=0)).then_inc(entry_loaded[n % 4], 16)

            @block.scalar
            def _(act):
                def split_hi(j, p):
                    act.wait_ge(raw_loaded[p], (j + 2 - p) * 8)
                    for a, b in PARTS:
                        act.activation(whi[p][:, a:b], raw[p][:, a:b], ACT.Copy).then_inc(M.w_hi, 1)

                def turned_high(j, p):
                    for u in range(SUBS):
                        act.wait_ge(M.turned, SUBS * j + u + 1)
                        act.activation(xh[p][:, :, u * P:(u + 1) * P], psT[u][:].rearrange("p (k n) -> p k n", k=KC),
                                       ACT.Copy).then_inc(M.x_hi, 1)

                act.sem_inc(M.y_copied, SUBS)
                split_hi(0, 0)
                turned_high(0, 0)

                def body(j, p, last):
                    if not last:
                        act.wait_ge(M.y_done, SUBS * (j + 1))
                        split_hi(j + 1, 1 - p)
                    for f, w in enumerate(widths):
                        act.wait_ge(M.h_done, FCH * j + f + 1)
                        act.wait_ge(M.hidden_ready, FCH * (j + 1))
                        act.activation(silu[f][0:w, :], psH[f][0:w, 0:SLOTS], ACT.Silu).then_inc(M.silu_done, 1)
                    if not last:
                        turned_high(j + 1, 1 - p)
                    for u in range(SUBS):
                        act.wait_ge(M.y_done, SUBS * (j + 1) + u + 1)
                        act.wait_ge(y_stored[u], 16 * (j + 1))
                        act.activation(ysb[u][:], psY[u][:], ACT.Copy).then_inc(M.y_copied, 1)

                tiles(act, body)

            @block.vector
            def _(dve):
                def split_lo(j, p):
                    for n, (a, b) in enumerate(PARTS):
                        dve.wait_ge(M.w_hi, 3 * j + n + 1)
                        dve.tensor_tensor(wlo[p][:, a:b], raw[p][:, a:b], f32(whi[p][:, a:b]), ALU.subtract).then_inc(M.w_ready, 1)

                def turned_low(j, p):
                    for u in range(SUBS):
                        dve.wait_ge(M.x_hi, SUBS * j + u + 1)
                        dve.tensor_tensor(xl[p][:, :, u * P:(u + 1) * P], psT[u][:].rearrange("p (k n) -> p k n", k=KC),
                                          f32(xh[p][:, :, u * P:(u + 1) * P]), ALU.subtract).then_inc(M.x_ready, 1)

                dve.sem_inc(M.hidden_ready, FCH)
                split_lo(0, 0)
                turned_low(0, 0)

                def body(j, p, last):
                    if not last:
                        split_lo(j + 1, 1 - p)
                    for f, w in enumerate(widths):
                        n = 2 * (FCH * j + f)
                        dve.wait_ge(M.silu_done, FCH * j + f + 1)
                        dve.tensor_tensor(prod[f][0:w, :], psH[f][0:w, SLOTS:], silu[f][0:w, :], ALU.mult).then_inc(M.hidden_steps, 1)
                        dve.wait_ge(M.hidden_steps, n + 1)
                        dve.wait_ge(M.y_done, SUBS * (j + 1))
                        dve.tensor_copy(hh[f][0:w, :], prod[f][0:w, :]).then_inc(M.hidden_steps, 1)
                        dve.wait_ge(M.hidden_steps, n + 2)
                        dve.tensor_tensor(hl[f][0:w, :], prod[f][0:w, :], f32(hh[f][0:w, :]), ALU.subtract).then_inc(M.hidden_ready, 1)
                    if not last:
                        turned_low(j + 1, 1 - p)

                tiles(dve, body)
                for n in range(2 * NT):
                    t, k = divmod(n, 2)
                    dve.wait_ge(entry_loaded[n % 4], 16 * (n // 4 + 1))
                    if k:
                        dve.wait_ge(M.entry_used, n)
                    dve.scalar_tensor_tensor(out=x[:, t, :], in0=rows[n // 2 % 2][n % 2][:], scalar=G.weight[k][:, t:t + 1],
                                             in1=x[:, t, :], op0=ALU.mult, op1=ALU.add).then_inc(M.entry_used, 1)

            @block.tensor
            def _(pe):
                def turn(j, p):
                    pe.wait_ge(rows_loaded[p], (j + 2 - p) * 8 * SUBS)
                    pe.wait_ge(M.x_ready, SUBS * j)
                    for u in range(SUBS):
                        for k in range(KC):
                            last = pe.transpose(psT[u][:, k * P:(k + 1) * P], rows[p][u][:, k * P:(k + 1) * P], ident)
                        last.then_inc(M.turned, 1)

                pe.sem_inc(M.y_done, SUBS)
                turn(0, 0)

                def body(j, p, last):
                    pe.wait_ge(M.w_ready, 3 * (j + 1))
                    pe.wait_ge(M.x_ready, SUBS * (j + 1))
                    pe.wait_ge(M.hidden_ready, FCH * (j + 1))
                    for f, w in enumerate(widths):
                        for o, half in ((GATE, 0), (UP, SLOTS)):
                            for k in range(KC):
                                c = slice(o + k * F_MOE + f * P, o + k * F_MOE + f * P + w)
                                ins = product(pe, psH[f][0:w, half:half + SLOTS], (whi[p][:, c], wlo[p][:, c]),
                                              (xh[p][:, k, :], xl[p][:, k, :]), k == 0, k == KC - 1)
                        ins.then_inc(M.h_done, 1)
                    if not last:
                        turn(j + 1, 1 - p)
                    pe.wait_ge(M.hidden_ready, FCH * (j + 2))
                    pe.wait_ge(M.y_copied, SUBS * (j + 1))
                    for u in range(SUBS):
                        m = slice(u * P, (u + 1) * P)
                        for f, w in enumerate(widths):
                            c = slice(DOWN + f * C, DOWN + (f + 1) * C)
                            ins = product(pe, psY[u][:], (hh[f][0:w, m], hl[f][0:w, m]),
                                          (whi[p][0:w, c], wlo[p][0:w, c]), f == 0, f == FCH - 1)
                        ins.then_inc(M.y_done, 1)

                tiles(pe, body)


def cross_attention(nc, io, G):
    UNITS = B * HPG
    TILES = UNITS * TT
    LASTU = GROUPS * UNITS - 1
    LASTI = GROUPS * TILES - 1
    SCALE = float(D) ** -0.5
    with ExitStack() as ctx:
        sb, ps, sem = scope(nc, ctx, "xa")
        x, ident = G.x, G.ident
        ctxr = sb("ctx", [P, B, KV, S], F32)
        ctxh, ctxl = sb("ctx_hi", [P, KV, S], F32R), sb("ctx_lo", [P, KV, S], F32R)
        NQ, NKV, NO = KC * HPG * D, 2 * KV * D, HPG * C
        raw = sb("w_raw", [P, NQ + NKV], F32)
        rqkv, ro = raw, raw[:, 0:NO]
        NQK = NQ + NKV // 2
        qkvh, qkvl = sb("wqkv_hi", [P, NQ + NKV], F32R), sb("wqkv_lo", [P, NQ + NKV], F32R)
        woh, wol = sb("wo_hi", [P, NO], F32R), sb("wo_lo", [P, NO], F32R)
        qh, ql = ([sb(f"q_{n}{i}", [P, S], F32R) for i in range(2)] for n in ("hi", "lo"))
        kh, kl = ([sb(f"k_{n}{i}", [P, S], F32R) for i in range(2)] for n in ("hi", "lo"))
        vh, vl = sb("v_hi", [P, S], F32R), sb("v_lo", [P, S], F32R)
        oh = [sb(f"out_hi{i}", [P, S], F32R) for i in range(HPG)]
        ol = [sb(f"out_lo{i}", [P, S], F32R) for i in range(HPG)]
        prob = [sb(f"prob{i}", [P, S], F32) for i in range(4)]
        PTh, PTl = sb("probT_hi", [P, TT, S], F32R), sb("probT_lo", [P, TT, S], F32R)
        mask8 = sb("mask", [P, B * S], U8)
        maskb = sb("mask_bias", [P, B * S], mybir.dt.bfloat16)
        some = sb("any_key", [P, B], F32)
        mx, nmx = sb("max", [P, 4], F32), sb("minus_max", [P, 4], F32)
        tot, inv = sb("total", [P, 4], F32), sb("inverse", [P, 4], F32)
        idle = sb("idle", [P, 1], F32)
        psS = [ps(f"ps_s{i}") for i in range(2)]
        psT = [ps(f"ps_t{i}") for i in range(2)]
        psP = [ps(f"ps_p{i}") for i in range(2)]
        psO = [ps(f"ps_o{i}") for i in range(2)]
        banks = iter(psT)
        R = ln_buffers(sb, lambda n: next(banks), sem, xn=prob[2:])
        M = Bag()
        M.ctx_loaded = sem("ctx_loaded")
        M.mask_loaded = sem("mask_loaded")
        M.qkv_loaded = sem("qkv_loaded")
        M.o_loaded = sem("o_loaded")
        M.mask_ready = sem("mask_ready")
        M.qk_hi = sem("qk_hi")
        M.qk_ready = sem("qk_ready")
        M.wv_hi = sem("wv_hi")
        M.wv_ready = sem("wv_ready")
        M.wo_hi = sem("wo_hi")
        M.wo_ready = sem("wo_ready")
        M.ctx_hi = sem("ctx_hi")
        M.ctx_ready = sem("ctx_ready")
        M.proj_done = sem("proj_done")
        M.proj_hi = sem("proj_hi")
        M.proj_ready = sem("proj_ready")
        M.s_done = sem("s_done")
        M.max_ready = sem("max_ready")
        M.exp_done = sem("exp_done")
        M.norm_ready = sem("norm_ready")
        M.p_turned = sem("p_turned")
        M.pt_hi = sem("pt_hi")
        M.pt_ready = sem("pt_ready")
        M.o_done = sem("o_done")
        M.x_added = sem("x_added")
        M.chain = sem("chain")

        FIRST_K, FIRST_Q, SECOND_Q = Place(0, 0), Place(1, 1), Place(2, 0)
        FINAL_PV = Place(2 + 6 * (LASTU // 2) + 3, 1)

        def last_pv(pair, h, end):
            return Place(2 + 6 * pair + (0 if h == 0 else 2 if end else 4), 0)

        def this_v(pair):
            return Place(2 + 6 * pair + 1, 1)

        def next_q(pair, h):
            return Place(2 + 6 * pair + (2 if h == 0 else 5), h)

        def next_k(pair):
            return Place(2 + 6 * pair + 3, 1)

        def at_least(eng, s, v):
            if not isinstance(v, int) or v > 0:
                eng.wait_ge(s, v)

        def groups(eng, body):
            body(0, "first")
            with eng.Fori(1, GROUPS - 1) as g:
                body(g, "middle")
            body(GROUPS - 1, "last")

        def units(g, which):
            for ul in range(UNITS):
                left = UNITS - 1 - ul if which == "last" else UNITS
                yield ul, ul // HPG, ul % HPG, g * B + ul // HPG, g * UNITS + ul, g * TILES + TT * ul, left

        with nc.Block() as block:

            @block.sync
            def _(sp):
                sp.dma_start(mask8[:], io["mask"].partition_broadcast(P)).then_inc(M.mask_loaded, 16)
                sp.dma_start(ctxr[:], io["ctxT"].rearrange("b p k s -> p b k s")).then_inc(M.ctx_loaded, 16)
                with sp.Fori(0, GROUPS) as g:
                    sp.wait_ge(M.wo_ready, g + 1)
                    sp.dma_start(rqkv[:], io["xa_w"][g, :, 0:NQ + NKV]).then_inc(M.qkv_loaded, 16)
                    sp.wait_ge(M.wv_ready, g + 1)
                    sp.dma_start(ro, io["xa_w"][g, :, NQ + NKV:]).then_inc(M.o_loaded, 16)

            @block.gpsimd
            def _(pool):
                ln_gpsimd(pool, R)

                def ctx_low(pair, b):
                    pool.wait_ge(M.ctx_hi, pair + 1)
                    pool.tensor_tensor(ctxl[:], ctxr[:, b, :, :], f32(ctxh[:]), ALU.subtract).then_inc(M.ctx_ready, 1)

                ctx_low(0, 0)

                def body(g, which):
                    for b in range(B):
                        if not (which == "last" and b == B - 1):
                            ctx_low(g * B + b + 1, (b + 1) % B)
                groups(pool, body)

            @block.scalar
            def _(act):
                def split_qk(g):
                    act.wait_ge(M.qkv_loaded, 16 * (g + 1))
                    act.activation(qkvh[:, 0:NQK], rqkv[:, 0:NQK], ACT.Copy).then_inc(M.qk_hi, 1)

                def split_v(g):
                    act.activation(qkvh[:, NQK:], rqkv[:, NQK:], ACT.Copy).then_inc(M.wv_hi, 1)

                def split_o(g):
                    act.wait_ge(M.o_loaded, 16 * (g + 1))
                    act.activation(woh[:], ro, ACT.Copy).then_inc(M.wo_hi, 1)

                def proj_high(at, out):
                    act.wait_ge(M.proj_done, at.n + 1)
                    act.activation(out[:], psP[at.bank][:], ACT.Copy).then_inc(M.proj_hi, 1)

                def exp(i, slot):
                    act.wait_ge(M.max_ready, i + 1)
                    act.activation(prob[slot][:], prob[slot][:], ACT.Exp, bias=nmx[:, slot:slot + 1], scale=SCALE,
                                   accum_out=tot[:, slot:slot + 1]).then_inc(M.exp_done, 1)

                def turned_high(i, tt):
                    act.wait_ge(M.p_turned, i + 1)
                    act.activation(PTh[:, :, tt * P:(tt + 1) * P], psT[tt % 2][:].rearrange("p (k n) -> p k n", k=TT),
                                   ACT.Copy).then_inc(M.pt_hi, 1)

                act.wait_ge(M.ctx_loaded, 16)
                act.activation(ctxh[:], ctxr[:, 0, :, :], ACT.Copy).then_inc(M.ctx_hi, 1)
                split_qk(0)
                split_v(0)
                ln_scalar(act, R, xT_tile(R))
                proj_high(FIRST_K, kh[0])
                proj_high(FIRST_Q, qh[0])
                proj_high(SECOND_Q, qh[1])
                for t in range(3):
                    exp(t, t)

                def body(g, which):
                    for ul, b, h, pair, u, i, left in units(g, which):
                        has_pv = not (which == "first" and ul == 0)
                        exp(i + 3, 3)
                        if has_pv:
                            act.wait_ge(M.proj_done, last_pv(pair, h, left < 2).n + 1)
                        turned_high(i, 0)
                        if has_pv:
                            proj_high(last_pv(pair, h, left < 2), oh[1 - h])
                        if ul == UNITS - 2 and which != "last":
                            act.wait_ge(M.proj_done, next_q(pair - 1, 1).n + 1)
                            split_qk(g + 1)
                        turned_high(i + 1, 1)
                        if left >= 1:
                            exp(i + 4, 0)
                        if h == 0:
                            proj_high(this_v(pair), vh)
                            if left >= 2:
                                act.activation(ctxh[:], ctxr[:, (b + 1) % B, :, :], ACT.Copy).then_inc(M.ctx_hi, 1)
                        if ul == 1:
                            act.wait_ge(M.o_done, g * B * TT)
                            split_o(g)
                        turned_high(i + 2, 2)
                        if left >= 1:
                            exp(i + 5, 1)
                        if ul == UNITS - 2 and which != "last":
                            split_v(g + 1)
                        turned_high(i + 3, 3)
                        if left >= 1:
                            exp(i + 6, 2)
                        if left >= 2:
                            proj_high(next_q(pair, h), qh[h])
                            if h == 0:
                                proj_high(next_k(pair), kh[(b + 1) % 2])

                groups(act, body)
                proj_high(FINAL_PV, oh[1])

            @block.vector
            def _(dve):
                def split_qk(g):
                    dve.wait_ge(M.qk_hi, g + 1)
                    dve.tensor_tensor(qkvl[:, 0:NQK], rqkv[:, 0:NQK], f32(qkvh[:, 0:NQK]), ALU.subtract).then_inc(M.qk_ready, 1)

                def split_v(g):
                    dve.wait_ge(M.wv_hi, g + 1)
                    dve.tensor_tensor(qkvl[:, NQK:], rqkv[:, NQK:], f32(qkvh[:, NQK:]), ALU.subtract).then_inc(M.wv_ready, 1)

                def split_o(g):
                    dve.wait_ge(M.wo_hi, g + 1)
                    dve.tensor_tensor(wol[:], ro, f32(woh[:]), ALU.subtract).then_inc(M.wo_ready, 1)

                def proj_low(at, hi, lo):
                    dve.wait_ge(M.proj_hi, at.n + 1)
                    dve.tensor_tensor(lo[:], psP[at.bank][:], f32(hi[:]), ALU.subtract).then_inc(M.proj_ready, 1)

                def masked_max(i, slot, b, n):
                    dve.wait_ge(M.s_done, i + 1)
                    at_least(dve, M.p_turned, i - 3)
                    dve.memset(idle[:], 0.0)
                    dve.tensor_tensor_reduce(out=prob[slot][:], in0=psS[slot % 2][:], in1=maskb[:, b * S:(b + 1) * S],
                                             scale=1.0, scalar=-3.4e38, op0=ALU.add, op1=ALU.max,
                                             accum_out=mx[:, slot:slot + 1]).then_inc(M.chain, 1)
                    dve.wait_ge(M.chain, n)
                    dve.tensor_scalar(nmx[:, slot:slot + 1], mx[:, slot:slot + 1], -SCALE, None,
                                      ALU.mult).then_inc(M.max_ready, 1)

                def normalise(i, slot, b, n):
                    dve.wait_ge(M.exp_done, i + 1)
                    dve.reciprocal(inv[:, slot:slot + 1], tot[:, slot:slot + 1]).then_inc(M.chain, 1)
                    dve.wait_ge(M.chain, n)
                    dve.tensor_scalar(prob[slot][:], prob[slot][:], inv[:, slot:slot + 1], some[:, b:b + 1],
                                      ALU.mult, ALU.mult).then_inc(M.norm_ready, 1)

                def turned_low(i, tt):
                    dve.wait_ge(M.pt_hi, i + 1)
                    dve.tensor_tensor(PTl[:, :, tt * P:(tt + 1) * P], psT[tt % 2][:].rearrange("p (k n) -> p k n", k=TT),
                                      f32(PTh[:, :, tt * P:(tt + 1) * P]), ALU.subtract).then_inc(M.pt_ready, 1)

                def add_x(pair, b, tt):
                    dve.wait_ge(M.o_done, pair * TT + tt + 1)
                    t = TT * b + tt
                    dve.tensor_tensor(x[:, t, :], psO[tt % 2][:], x[:, t, :], ALU.add).then_inc(M.x_added, 1)

                dve.wait_ge(M.mask_loaded, 16)
                dve.tensor_scalar(maskb[:], mask8[:], MASKED, -MASKED, ALU.mult, ALU.add).then_inc(M.mask_ready, 1)
                dve.reduce_max(some[:], mask8[:].rearrange("p (b s) -> p b s", b=B), axis=AX.X).then_inc(M.mask_ready, 1)
                dve.sem_inc(M.wo_ready, 1)
                split_qk(0)
                split_v(0)
                ln_vector(dve, R, x, xT_tile(R))
                dve.wait_ge(M.mask_ready, 2)
                proj_low(FIRST_K, kh[0], kl[0])
                proj_low(FIRST_Q, qh[0], ql[0])
                proj_low(SECOND_Q, qh[1], ql[1])
                for t in range(3):
                    masked_max(t, t, 0, t + 1)
                for t in range(2):
                    normalise(t, t, 0, t + 4)

                def body(g, which):
                    for ul, b, h, pair, u, i, left in units(g, which):
                        nb = (ul + 1) // HPG % B
                        links = 5 + 2 * i
                        has_pv = not (which == "first" and ul == 0)
                        has_output = h == 0 and has_pv
                        ob = (b - 1) % B
                        masked_max(i + 3, 3, b, links + 1)
                        normalise(i + 2, 2, b, links + 2)
                        if h == 1 and not (which == "first" and ul == 1):
                            add_x(pair - 1, ob, 3)
                        turned_low(i, 0)
                        if has_pv:
                            proj_low(last_pv(pair, h, left < 2), oh[1 - h], ol[1 - h])
                        if ul == UNITS - 2 and which != "last":
                            split_qk(g + 1)
                        if left >= 1:
                            masked_max(i + 4, 0, nb, links + 3)
                        normalise(i + 3, 3, b, links + (4 if left >= 1 else 3))
                        turned_low(i + 1, 1)
                        if h == 0:
                            proj_low(this_v(pair), vh, vl)
                        if ul == 1:
                            split_o(g)
                        if has_output:
                            add_x(pair - 1, ob, 0)
                        if left >= 1:
                            masked_max(i + 5, 1, nb, links + 5)
                            normalise(i + 4, 0, nb, links + 6)
                        turned_low(i + 2, 2)
                        if has_output:
                            add_x(pair - 1, ob, 1)
                        if ul == UNITS - 2 and which != "last":
                            split_v(g + 1)
                        if left >= 1:
                            masked_max(i + 6, 2, nb, links + 7)
                            normalise(i + 5, 1, nb, links + 8)
                        turned_low(i + 3, 3)
                        if left >= 2:
                            proj_low(next_q(pair, h), qh[h], ql[h])
                        if has_output:
                            add_x(pair - 1, ob, 2)
                        if left >= 2 and h == 0:
                            proj_low(next_k(pair), kh[(b + 1) % 2], kl[(b + 1) % 2])

                groups(dve, body)
                proj_low(FINAL_PV, oh[1], ol[1])
                for tt in range(TT):
                    add_x(GROUPS * B - 1, B - 1, tt)

            @block.tensor
            def _(pe):
                def wq(h, k):
                    c = slice(k * HPG * D + h * D, k * HPG * D + (h + 1) * D)
                    return qkvh[:, c], qkvl[:, c]

                def wkv(j, k):
                    c = slice(NQ + (j * KV + k) * D, NQ + (j * KV + k + 1) * D)
                    return qkvh[:, c], qkvl[:, c]

                def bank_free(at):
                    at_least(pe, M.proj_ready, at.n - 1)

                def query(at, b, h, ks):
                    for k in ks:
                        tok = slice(b * S, (b + 1) * S)
                        last = product(pe, psP[at.bank][:], wq(h, k), (R.xTh[:, k, tok], R.xTl[:, k, tok]),
                                       k == 0, k == KC - 1)
                        if k == KC - 1:
                            last.then_inc(M.proj_done, 1)

                def key(at):
                    for k in range(KV):
                        last = product(pe, psP[at.bank][:], wkv(0, k), (ctxh[:, k, :], ctxl[:, k, :]), k == 0, k == KV - 1)
                    last.then_inc(M.proj_done, 1)

                def value(at):
                    for st in range(TT):
                        s = slice(st * P, (st + 1) * P)
                        for k in range(KV):
                            last = product(pe, psP[at.bank][:, s], (ctxh[:, k, s], ctxl[:, k, s]), wkv(1, k), k == 0, k == KV - 1)
                    last.then_inc(M.proj_done, 1)

                def scores(i, tt, q, k):
                    at_least(pe, M.max_ready, i - 1)
                    m = slice(tt * P, (tt + 1) * P)
                    product(pe, psS[tt % 2][:], (qh[q][:, m], ql[q][:, m]), (kh[k][:], kl[k][:]), True, True).then_inc(M.s_done, 1)

                def turn(i, tt):
                    pe.wait_ge(M.norm_ready, i + 1)
                    at_least(pe, M.pt_ready, i - 1)
                    for k in range(TT):
                        last = pe.transpose(psT[tt % 2][:, k * P:(k + 1) * P], prob[tt][:, k * P:(k + 1) * P], ident)
                    last.then_inc(M.p_turned, 1)

                def weighted(at, u):
                    pe.wait_ge(M.pt_ready, TT * (u + 1))
                    bank_free(at)
                    for st in range(TT):
                        s = slice(st * P, (st + 1) * P)
                        last = product(pe, psP[at.bank][:], (vh[:, s], vl[:, s]), (PTh[:, st, :], PTl[:, st, :]),
                                       st == 0, st == TT - 1)
                    last.then_inc(M.proj_done, 1)

                def output(pair, tt):
                    at_least(pe, M.x_added, pair * TT + tt - 1)
                    m = slice(tt * P, (tt + 1) * P)
                    for h in range(HPG):
                        last = product(pe, psO[tt % 2][:], (oh[h][:, m], ol[h][:, m]),
                                       (woh[:, h * C:(h + 1) * C], wol[:, h * C:(h + 1) * C]), h == 0, h == HPG - 1)
                    last.then_inc(M.o_done, 1)

                ln_tensor(pe, R, ident)
                pe.wait_ge(M.wv_ready, 1)
                pe.wait_ge(M.ctx_ready, 1)
                key(FIRST_K)
                pe.wait_ge(R.xT_ready, NT)
                query(FIRST_Q, 0, 0, range(KC))
                bank_free(SECOND_Q)
                query(SECOND_Q, 0, 1, range(KC))
                pe.wait_ge(M.proj_ready, SECOND_Q.n + 1)
                for t in range(3):
                    scores(t, t, 0, 0)

                def body(g, which):
                    for ul, b, h, pair, u, i, left in units(g, which):
                        nk = (ul + 1) // HPG % 2
                        has_pv = not (which == "first" and ul == 0)
                        has_output = h == 0 and has_pv
                        qb = (b + 1) % B
                        nq = next_q(pair, h)
                        scores(i + 3, 3, h, b % 2)
                        turn(i, 0)
                        if h == 1 and not (which == "first" and ul == 1):
                            output(pair - 1, 3)
                        if has_pv:
                            if h == 1:
                                pe.wait_ge(M.proj_ready, this_v(pair).n + 1)
                            weighted(last_pv(pair, h, left < 2), u - 1)
                        if left >= 1:
                            pe.wait_ge(M.proj_ready, (next_k(pair) if h == 1 else next_q(pair - 1, 1)).n + 1)
                            scores(i + 4, 0, 1 - h, nk)
                        turn(i + 1, 1)
                        if h == 0:
                            bank_free(this_v(pair))
                            value(this_v(pair))
                        if has_output:
                            pe.wait_ge(M.proj_ready, last_pv(pair, h, left < 2).n + 1)
                            if ul == HPG:
                                pe.wait_ge(M.wo_ready, g + 2)
                            output(pair - 1, 0)
                        if left >= 1:
                            scores(i + 5, 1, 1 - h, nk)
                        turn(i + 2, 2)
                        if left >= 2:
                            if ul == UNITS - 2:
                                pe.wait_ge(M.qk_ready, g + 2)
                            bank_free(nq)
                            query(nq, qb, h, range(0, KC // 2))
                        if has_output:
                            output(pair - 1, 1)
                        if left >= 1:
                            scores(i + 6, 2, 1 - h, nk)
                        turn(i + 3, 3)
                        if left >= 2:
                            query(nq, qb, h, range(KC // 2, KC))
                        if has_output:
                            output(pair - 1, 2)
                        if left >= 2 and h == 0:
                            pe.wait_ge(M.ctx_ready, pair + 2)
                            bank_free(next_k(pair))
                            key(next_k(pair))
                            if ul == UNITS - 2:
                                pe.wait_ge(M.wv_ready, g + 2)

                groups(pe, body)
                weighted(FINAL_PV, LASTU)
                pe.wait_ge(M.proj_ready, FINAL_PV.n + 1)
                for tt in range(TT):
                    output(GROUPS * B - 1, tt)


def kernel(**inputs):
    import concourse.bacc as bacc
    from concourse.bass_utils import run_bass_kernel_spmd

    a = {k: np.asarray(v) for k, v in inputs.items()}

    def chunks_T(w):
        n = w.shape[0] // P
        return w.reshape(n, P, -1, P).transpose(0, 3, 2, 1).reshape(n, P, -1)

    shared_w = np.concatenate([
        chunks_T(a["L0_ffn_shared_fc1"]), chunks_T(a["L0_ffn_shared_fc2"]),
        a["L0_ffn_shared_proj"].T.reshape(F_SHARED // P, P, C)], axis=2)

    def expert_in(w):
        return w.reshape(E, F_MOE, KC, P).transpose(0, 3, 2, 1).reshape(E, P, KC * F_MOE)

    down = np.concatenate([a["L0_ffn_expert_proj"].transpose(0, 2, 1), np.zeros((E, FCH * P - F_MOE, C), np.float32)], axis=1)
    expert_w = np.concatenate([
        expert_in(a["L0_ffn_expert_fc1"]), expert_in(a["L0_ffn_expert_fc2"]),
        down.reshape(E, FCH, P, C).transpose(0, 2, 1, 3).reshape(E, P, FCH * C)], axis=2)
    router = np.concatenate([a["L0_ffn_gate_w"], a["L0_ffn_shared_gate_w"], np.zeros((1, C), np.float32)])

    def rows(w, per_group):
        return w.reshape(-1, P, GROUPS, per_group).transpose(2, 1, 0, 3).reshape(GROUPS, P, -1)

    h = np.ones((1, 1), np.float32)
    while h.shape[0] < P:
        h = np.block([[h, h], [h, -h]]).astype(np.float32)
    wsc = a["L1_ffn_Wscale_ug"].reshape(2, NF, P)
    arrays = {
        "x": a["x"],
        "ctxT": a["ctx_1024"].reshape(B, S, KV, P).transpose(0, 3, 2, 1),
        "mask": a["mask_BxS2_bf1"].view(np.uint8).reshape(B * S),
        "ident": np.eye(P, dtype=np.float32),
        "h128": h,
        "sums": np.stack([np.triu(np.ones((P, P), np.float32), 1), np.ones((P, P), np.float32)], axis=1),
        "route_consts": np.concatenate([np.tril(np.ones((E, E)), -1).ravel(), np.arange(E) * SLOTS,
                                        np.arange(TILES)]).astype(np.float32),
        "ca_w": np.stack([chunks_T(a["L0_xattn_Wq"])[0], chunks_T(a["L0_xattn_Wk"])[0]], axis=1).reshape(P, 2, KV, D),
        "ca_b": np.stack([a["L0_xattn_bq"], a["L0_xattn_bk"]], axis=1),
        "shared_w": shared_w,
        "expert_w": expert_w,
        "router": router.reshape(RG, KC, P).transpose(2, 1, 0),
        "xa_w": np.concatenate([
            rows(a["L1_xattn_Wq"], HPG * D), rows(a["L1_xattn_Wk"], D), rows(a["L1_xattn_Wv"], D),
            a["L1_xattn_Wo"].reshape(GROUPS, HPG, D, C).transpose(0, 2, 1, 3).reshape(GROUPS, D, HPG * C)], axis=2),
        "ffn_w": np.concatenate([chunks_T(a["L1_ffn_W_gate"]), chunks_T(a["L1_ffn_W_up"])], axis=2),
        "wdT": a["L1_ffn_W_down"].T.reshape(NF, P, C),
        "wscale_dp": a["L1_ffn_Wscale_dp"],
        "su_ug": a["L1_ffn_SU_ug"],
        "ffn_tables": np.stack([wsc[0].T, wsc[1].T, a["L1_ffn_SU_dp"].reshape(NF, P).T], axis=1),
    }
    arrays = {f"in_{k}": np.ascontiguousarray(v) for k, v in arrays.items()}
    nc = bacc.Bacc("TRN2", target_bir_lowering=False, num_devices=1)
    io = {k[3:]: nc.dram_tensor(k, v.shape, mybir.dt.from_np(v.dtype), kind="ExternalInput").ap() for k, v in arrays.items()}
    io["out"] = nc.dram_tensor("out", (B, S, C), F32, kind="ExternalOutput").ap()
    program(nc, io)
    result = run_bass_kernel_spmd(nc, [arrays], core_ids=[0])
    return result.results[0]["out"]
```

```python
from contextlib import ExitStack

import numpy as np

import concourse.bass as bass
from concourse import mybir

F32 = mybir.dt.float32
F32R = mybir.dt.float32r
U8 = mybir.dt.uint8
I32 = mybir.dt.int32
ALU = mybir.AluOpType
ACT = mybir.ActivationFunctionType
AX = mybir.AxisListType

P = 128
B, S, C = 4, 512, 512
CV = 256
TOK = B * S
NT = TOK // P
TT = S // P
KC = C // P
KV = CV // P
D = 128
E, F_MOE, F_SHARED = 8, 352, 1408
RG = E + 2
GROUPS, HPG = 8, 2
INTER = 2048
NF = INTER // P
EPS = 1e-5
MASKED = 3.0e38
SLOTS = 256
SUBS = SLOTS // P
TILES = (2 * TOK + E * (SLOTS - 1)) // SLOTS
FCH = -(-F_MOE // P)
EW = 2 * KC * F_MOE + FCH * C
WSLICE = 3 * C
GROUP = 4


class Chain:

    def __init__(self, eng, sem, n=0):
        self.eng, self.sem, self.n = eng, sem, n

    def link(self, ins):
        ins.then_inc(self.sem, 1)
        self.n += 1
        self.eng.wait_ge(self.sem, self.n)


class Bag:
    pass


class Place:

    def __init__(self, n, bank):
        self.n, self.bank = n, bank


def f32(ap):
    return ap.bitcast(F32)


def product(pe, out, lhs, rhs, start, stop):
    (lh, ll), (rh, rl) = lhs, rhs
    pe.matmul(out, lh, rh, start=start, stop=False)
    pe.matmul(out, lh, rl, start=False, stop=False)
    return pe.matmul(out, ll, rh, start=False, stop=stop)


def ln_stat_buffers(sb, sem):
    R = Bag()
    R.stats = sb("ln_stats", [P, NT, 6], F32)
    R.mv = sb("ln_mean_var", [P, NT, 2], F32)
    R.veps = sb("ln_var_eps", [P, NT], F32)
    R.rstd = sb("ln_rstd", [P, NT], F32)
    R.mhalf = sb("ln_minus_half", [P, TT], F32)
    R.chain = sem("ln_chain")
    R.stats_done = sem("ln_stats_done")
    R.pool_chain = sem("ln_pool_chain")
    R.rstd_ready = sem("ln_rstd_ready")
    R.links, R.pool_links = 0, 0
    return R


def ln_buffers(sb, sem, xn, R=None):
    R = R or ln_stat_buffers(sb, sem)
    R.xTh, R.xTl = sb("xT_hi", [P, KC, TOK], F32R), sb("xT_lo", [P, KC, TOK], F32R)
    R.xn = xn
    R.xn_ready = sem("ln_xn_ready")
    R.xn_turned = sem("ln_xn_turned")
    R.hi_ready = sem("ln_hi_ready")
    R.xT_ready = sem("ln_xT_ready")
    return R


def ln_gpsimd(pool, R, shift=None):
    ch = Chain(pool, R.pool_chain, R.pool_links)
    if ch.n == 0:
        ch.link(pool.memset(R.mhalf[:], -0.5))

    def rstd(b):
        t = slice(TT * b, TT * b + TT)
        pool.wait_ge(R.stats_done, TT * (b + 1))
        ch.link(pool.tensor_scalar(R.veps[:, t], R.mv[:, t, 1], EPS, None, ALU.add))
        last = pool.tensor_tensor(R.rstd[:, t], R.veps[:, t], R.mhalf[:], ALU.pow)
        if shift is not None:
            ch.link(last)
            ch.link(pool.tensor_tensor(shift[:, t], R.mv[:, t, 0], R.rstd[:, t], ALU.mult))
            last = pool.tensor_scalar(shift[:, t], shift[:, t], -1.0, None, ALU.mult)
        last.then_inc(R.rstd_ready, 1)
        R.pool_links = ch.n

    return rstd


def ln_vector(dve, R, x, dst, bank, stored=None):
    ch = Chain(dve, R.chain, R.links)

    def stats(t):
        ch.link(dve.bn_stats(R.stats[:, t, :], x[:, t, :]))
        R.links = ch.n
        dve.bn_aggr(R.mv[:, t, :], R.stats[:, t, :]).then_inc(R.stats_done, 1)

    def norm(t):
        if t % TT == 0:
            dve.wait_ge(R.rstd_ready, t // TT + 1)
            dve.wait_ge(R.stats_done, t + TT)
        xn = R.xn[t % len(R.xn)]
        if t >= len(R.xn):
            dve.wait_ge(R.xn_turned, t - len(R.xn) + 1)
            if stored is not None:
                dve.wait_ge(stored[t % len(R.xn)], 16 * (t // len(R.xn)))
        dve.tensor_scalar(xn[:], x[:, t, :], R.mv[:, t, 0:1], R.rstd[:, t:t + 1], ALU.subtract,
                          ALU.mult).then_inc(R.xn_ready, 1)

    def low(t):
        dve.wait_ge(R.hi_ready, t + 1)
        hi, lo = dst(t)
        dve.tensor_tensor(lo, bank(t)[:].rearrange("p (k n) -> p k n", k=KC), f32(hi),
                          ALU.subtract).then_inc(R.xT_ready, 1)

    return stats, norm, low


def ln_tensor(pe, R, ident, bank):
    def turn(t):
        pe.wait_ge(R.xn_ready, t + 1)
        for k in range(KC):
            last = pe.transpose(bank(t)[:, k * P:(k + 1) * P], R.xn[t % len(R.xn)][:, k * P:(k + 1) * P], ident)
        last.then_inc(R.xn_turned, 1)

    return turn


def ln_scalar(act, R, dst, bank):
    def high(t):
        act.wait_ge(R.xn_turned, t + 1)
        act.activation(dst(t)[0], bank(t)[:].rearrange("p (k n) -> p k n", k=KC), ACT.Copy).then_inc(R.hi_ready, 1)

    return high


def program(nc, io):
    out = io["out"]
    had_dram = nc.dram_tensor("wd_h128", (NF, P, C), F32, kind="Internal").ap()
    xn_dram = nc.dram_tensor("moe_xn", (TOK + P, C), F32, kind="Internal").ap()
    x_dram = nc.dram_tensor("moe_x", (TOK + P, C), F32, kind="Internal").ap()
    table_dram = nc.dram_tensor("moe_slot_table", (P * TILES * SUBS, 2), I32, kind="Internal").ap()
    fold_dram = nc.dram_tensor("wd_folded", (NF, P, C), F32, kind="Internal").ap()
    with ExitStack() as top:
        x = top.enter_context(nc.sbuf_tensor("x", [P, NT, C], F32))
        ident = top.enter_context(nc.sbuf_tensor("ident", [P, P], F32))
        G = Bag()
        G.x, G.ident, G.ident_t = x, ident[:], ident
        sb, _, sem = scope(nc, top, "moe")
        G.moe_ln = ln_stat_buffers(sb, sem)
        G.had_dram, G.fold_dram = had_dram, fold_dram
        G.xn_dram, G.table_dram, G.x_dram = xn_dram, table_dram, x_dram
        channel_attention(nc, io, G)
        with ExitStack() as moe:
            sb, _, sem = scope(nc, moe, "route")
            G.weights = sb("weights", [P, 3 * WSLICE], F32)
            G.rows = sb("rows", [P, 2 * SUBS * C], F32)
            G.x_stored = sem("x_stored")
            G.gate_up_loaded = [sem(f"gate_up_loaded{i}") for i in range(2)]
            G.down_loaded = [sem(f"down_loaded{i}") for i in range(2)]
            G.rows_loaded = [sem(f"rows_loaded{i}") for i in range(2)]
            G.qkv_loaded = sem("qkv_loaded")
            G.ctx_loaded = [sem(f"ctx_loaded{i}") for i in range(2)]
            G.slot_token = sb("slot_token", [P, TILES * SUBS], I32)
            G.slot_weight = sb("slot_weight", [P, TILES * SUBS], F32)
            G.tile_expert = sb("tile_expert", [P, TILES], I32)
            gated_ffn(nc, io, G, "moe", weights=io["shared_w"], down=None, NG=3, GC=GROUP, LAST=3)
            G.mask_bias = sb("mask_bias", [P, B * S], mybir.dt.bfloat16)
            G.any_key = sb("any_key", [P, B], F32)
            sparse_experts(nc, io, G)
            cross_attention(nc, io, G)
        gated_ffn(nc, io, G, "ffn", weights=io["ffn_w"], down=fold_dram, NG=4, GC=GROUP, LAST=GROUP)


def scope(nc, ctx, name):
    def sb(n, shape, dt):
        return ctx.enter_context(nc.sbuf_tensor(f"{name}_{n}", shape, dt))

    def ps(n, cols=512):
        return ctx.enter_context(nc.psum_tensor(f"{name}_{n}", [P, cols], F32))

    def sem(n):
        return ctx.enter_context(nc.semaphore(f"{name}_{n}"))

    return sb, ps, sem


def xT_tile(R):
    return lambda t: (R.xTh[:, :, t * P:(t + 1) * P], R.xTl[:, :, t * P:(t + 1) * P])


def channel_attention(nc, io, G):
    WD_LAG = 2
    with ExitStack() as ctx:
        sb, ps, sem = scope(nc, ctx, "ca")
        first_sem = sem("first")

        def sum_bank(t):
            return psA if t >= NT - TT and t % 2 else psX

        R = ln_buffers(sb, sem, xn=[sb(f"xn{i}", [P, C], F32) for i in range(2)])
        x, ident = G.x, G.ident
        ctxr = [sb(f"ctx{i}", [P, KV, S], F32) for i in range(2)]
        ctxh, ctxl = ([sb(f"ctx_{n}{i}", [P, KV, S], F32R) for i in range(2)] for n in ("hi", "lo"))
        qkh, qkl = ([sb(f"qk_{n}{i}", [P, 2, S], F32R) for i in range(2)] for n in ("hi", "lo"))
        Ah, Al = ([sb(f"attnT_{n}{i}", [P, TT, S], F32R) for i in range(2)] for n in ("hi", "lo"))
        wr = sb("wqk", [P, 2, KV, D], F32)
        wh, wl = sb("wqk_hi", [P, 2, KV, D], F32R), sb("wqk_lo", [P, 2, KV, D], F32R)
        bias = sb("bqk", [P, 2], F32)
        NPROB = 3
        prob = [sb(f"prob{i}", [P, S], F32) for i in range(NPROB)]
        mx = sb("max", [P, NT], F32)
        nmx = sb("minus_max", [P, NT], F32)
        tot = sb("total", [P, NT], F32)
        inv = sb("inverse", [P, NT], F32)
        had = sb("h128", [P, P], F32)
        hadr = sb("h128_r", [P, P], F32R)
        wdp = sb("wscale_dp", [P, C], F32)
        wds = [sb(f"wd{i}", [P, C], F32) for i in range(2)]
        wdh = [sb(f"wd_hi{i}", [P, C], F32R) for i in range(2)]
        wdl = [sb(f"wd_lo{i}", [P, C], F32R) for i in range(2)]
        wdz = [sb(f"wd_out{i}", [P, C], F32) for i in range(2)]
        psS = [ps(f"ps_s{i}") for i in range(2)]
        psQ = [ps(f"ps_q{i}") for i in range(2)]
        psX, psW, psA, psT = ps("ps_x"), ps("ps_wd"), ps("ps_a"), ps("ps_xnT")
        x_loaded = [sem(f"x_loaded{b}") for b in range(B)]
        ctx_loaded = [sem(f"ctx_loaded{i}") for i in range(2)]
        wd_loaded = [sem(f"wd_loaded{i}") for i in range(2)]
        wd_stored = [sem(f"wd_stored{i}") for i in range(2)]
        M = Bag()
        M.ident_loaded = sem("ident_loaded")
        M.small_loaded = sem("small_loaded")
        M.const_loaded = sem("const_loaded")
        M.w_hi = sem("w_hi")
        M.w_ready = sem("w_ready")
        M.ctx_hi = sem("ctx_hi")
        M.ctx_ready = sem("ctx_ready")
        M.had_ready = sem("had_ready")
        M.qk_done = sem("qk_done")
        M.qk_hi = sem("qk_hi")
        M.qk_ready = sem("qk_ready")
        M.s_done = sem("s_done")
        M.max_ready = sem("max_ready")
        M.exp_done = sem("exp_done")
        M.norm_ready = sem("norm_ready")
        M.a_turned = sem("a_turned")
        M.a_hi = sem("a_hi")
        M.a_ready = sem("a_ready")
        M.x_done = sem("x_done")
        M.x_added = sem("x_added")
        M.chain = sem("chain")
        M.wd_scaled = sem("wd_scaled")
        M.wd_hi = sem("wd_hi")
        M.wd_ready = sem("wd_ready")
        M.wd_done = sem("wd_done")
        M.wd_out = sem("wd_out")
        G.used_sems = range(first_sem.num, M.wd_out.num + 1)

        def columns(ap):
            return ap.rearrange("p (k n) -> p k n", k=TT)

        with nc.Block() as block:

            @block.sync
            def _(sp):
                def load_ctx(b):
                    if b >= 2:
                        sp.wait_ge(M.ctx_ready, b - 1)
                    sp.dma_start(ctxr[b % 2][:], io["ctxT"][b]).then_inc(ctx_loaded[b % 2], 16)

                sp.dma_start(wr[:], io["ca_w"]).then_inc(M.small_loaded, 16)
                sp.dma_start(bias[:], io["ca_b"]).then_inc(M.small_loaded, 16)
                load_ctx(0)
                sp.dma_start(G.ident_t[:], io["ident"]).then_inc(M.ident_loaded, 16)
                for b in range(B):
                    sp.dma_start(x[:, TT * b:TT * b + TT, :],
                                 io["x"][b].rearrange("(t p) c -> p t c", p=P)).then_inc(x_loaded[b], 16)
                    if b == 0:
                        sp.dma_start(had[:], io["h128"]).then_inc(M.const_loaded, 16)
                        sp.dma_start(wdp[:], io["wscale_dp"].partition_broadcast(P)).then_inc(M.const_loaded, 16)
                        for n in range(2):
                            sp.dma_start(wds[n][:], io["wdT"][n]).then_inc(wd_loaded[n], 16)
                        load_ctx(1)
                for b in range(2, B):
                    load_ctx(b)
                for n in range(NF):
                    if n + 2 < NF:
                        sp.wait_ge(M.wd_ready, n + 1)
                        sp.dma_start(wds[n % 2][:], io["wdT"][n + 2]).then_inc(wd_loaded[n % 2], 16)
                    sp.wait_ge(M.wd_out, n + 1)
                    sp.dma_start(G.had_dram[n], wdz[n % 2][:]).then_inc(wd_stored[n % 2], 16)
                for i in range(2):
                    sp.wait_ge(wd_stored[i], 16 * (NF // 2))

            @block.gpsimd
            def _(pool):
                rstd = ln_gpsimd(pool, R)

                def ctx_low(b):
                    pool.wait_ge(M.ctx_hi, b + 1)
                    if b >= 2:
                        pool.wait_ge(M.qk_done, 2 * (b - 1))
                    pool.tensor_tensor(ctxl[b % 2][:], ctxr[b % 2][:], f32(ctxh[b % 2][:]),
                                       ALU.subtract).then_inc(M.ctx_ready, 1)

                def scale_wd(n):
                    pool.wait_ge(wd_loaded[n % 2], 16 * (n // 2 + 1))
                    pool.tensor_tensor(wds[n % 2][:], wds[n % 2][:], wdp[:], ALU.mult).then_inc(M.wd_scaled, 1)

                def wd_low(n):
                    pool.wait_ge(M.wd_hi, n + 1)
                    if n >= 2:
                        pool.wait_ge(M.wd_done, n - 1)
                    pool.tensor_tensor(wdl[n % 2][:], wds[n % 2][:], f32(wdh[n % 2][:]),
                                       ALU.subtract).then_inc(M.wd_ready, 1)

                rstd(0)
                ctx_low(1)
                for i in range(NF + WD_LAG):
                    b, tt = divmod(i, TT)
                    n = i + 1 - WD_LAG
                    if 0 <= n < NF:
                        wd_low(n)
                    if i == 0:
                        pool.wait_ge(M.const_loaded, 32)
                    if i < NF:
                        scale_wd(i)
                    if tt == 1 and b + 1 < B:
                        rstd(b + 1)
                    if tt == 2 and b + 2 < B:
                        ctx_low(b + 2)
                ln_gpsimd(pool, G.moe_ln)(0)

            @block.scalar
            def _(act):
                high = ln_scalar(act, R, xT_tile(R), lambda t: psT)

                def ctx_high(b):
                    act.wait_ge(ctx_loaded[b % 2], 16 * (b // 2 + 1))
                    if b >= 2:
                        act.wait_ge(M.qk_done, 2 * (b - 1))
                    act.activation(ctxh[b % 2][:], ctxr[b % 2][:], ACT.Copy).then_inc(M.ctx_hi, 1)

                def qk_high(b):
                    for j in range(2):
                        act.wait_ge(M.qk_done, 2 * b + j + 1)
                        if b >= 2:
                            act.wait_ge(M.s_done, TT * (b - 1))
                        act.activation(qkh[b % 2][:, j, :], psQ[j][:], ACT.Identity,
                                       bias=bias[:, j:j + 1]).then_inc(M.qk_hi, 1)

                def exp(i):
                    act.wait_ge(M.max_ready, i + 1)
                    if i >= NPROB:
                        act.wait_ge(M.a_turned, i - NPROB + 1)
                    act.activation(prob[i % NPROB][:], psS[i % 2][:], ACT.Exp, bias=nmx[:, i:i + 1],
                                   accum_out=tot[:, i:i + 1]).then_inc(M.exp_done, 1)

                def attn_high(i):
                    b, tt = divmod(i, TT)
                    act.wait_ge(M.a_turned, i + 1)
                    if tt == 0 and b >= 2:
                        act.wait_ge(M.x_done, TT * (b - 1))
                    act.activation(Ah[b % 2][:, :, tt * P:(tt + 1) * P], columns(psA), ACT.Copy).then_inc(M.a_hi, 1)

                def wd_high(n):
                    act.wait_ge(M.wd_scaled, n + 1)
                    if n >= 2:
                        act.wait_ge(M.wd_done, n - 1)
                    act.activation(wdh[n % 2][:], wds[n % 2][:], ACT.Copy).then_inc(M.wd_hi, 1)

                def wd_out(n):
                    act.wait_ge(M.wd_done, n + 1)
                    if n >= 2:
                        act.wait_ge(wd_stored[n % 2], 16 * (n // 2))
                    act.activation(wdz[n % 2][:], psW[:], ACT.Copy).then_inc(M.wd_out, 1)

                act.wait_ge(M.small_loaded, 32)
                act.activation(wh[:], wr[:], ACT.Copy).then_inc(M.w_hi, 1)
                ctx_high(0)
                qk_high(0)
                exp(0)
                exp(1)
                ctx_high(1)
                for i in range(NF + WD_LAG):
                    b, tt = divmod(i, TT)
                    n = i + 1 - WD_LAG
                    if 0 <= n < NF:
                        wd_high(n)
                    if i < NT:
                        if tt == 1 and b + 1 < B:
                            qk_high(b + 1)
                        attn_high(i)
                        high(i)
                        if i + 2 < NT:
                            exp(i + 2)
                    if i == 0:
                        act.wait_ge(M.const_loaded, 32)
                        act.activation(hadr[:], had[:], ACT.Copy).then_inc(M.had_ready, 1)
                    if n >= 1:
                        wd_out(n - 1)
                    if tt == 2 and b + 2 < B:
                        ctx_high(b + 2)

            @block.vector
            def _(dve):
                ch = Chain(dve, M.chain)
                stats, norm, low = ln_vector(dve, R, x, xT_tile(R), lambda t: psT)

                def qk_low(b):
                    for j in range(2):
                        dve.wait_ge(M.qk_hi, 2 * b + j + 1)
                        dve.scalar_tensor_tensor(out=qkl[b % 2][:, j, :], in0=psQ[j][:], scalar=bias[:, j:j + 1],
                                                 in1=f32(qkh[b % 2][:, j, :]), op0=ALU.add,
                                                 op1=ALU.subtract).then_inc(M.qk_ready, 1)

                def row_max(i):
                    dve.wait_ge(M.s_done, i + 1)
                    ch.link(dve.reduce_max(mx[:, i:i + 1], psS[i % 2][:], axis=AX.X))
                    dve.tensor_scalar(nmx[:, i:i + 1], mx[:, i:i + 1], -1.0, None, ALU.mult).then_inc(M.max_ready, 1)

                def normalise(i):
                    dve.wait_ge(M.exp_done, i + 1)
                    ch.link(dve.reciprocal(inv[:, i:i + 1], tot[:, i:i + 1]))
                    dve.tensor_scalar(prob[i % NPROB][:], prob[i % NPROB][:], inv[:, i:i + 1], None,
                                      ALU.mult).then_inc(M.norm_ready, 1)

                def attn_low(i):
                    b, tt = divmod(i, TT)
                    m = slice(tt * P, (tt + 1) * P)
                    dve.wait_ge(M.a_hi, i + 1)
                    dve.tensor_tensor(Al[b % 2][:, :, m], columns(psA), f32(Ah[b % 2][:, :, m]),
                                      ALU.subtract).then_inc(M.a_ready, 1)

                def x_stats(t):
                    if t % TT == 0:
                        dve.wait_ge(x_loaded[t // TT], 16)
                    stats(t)

                def add_x(t):
                    dve.wait_ge(M.x_done, t + 1)
                    dve.tensor_tensor(x[:, t, :], sum_bank(t)[:], x[:, t, :], ALU.add).then_inc(M.x_added, 1)

                dve.wait_ge(M.w_hi, 1)
                dve.tensor_tensor(wl[:], wr[:], f32(wh[:]), ALU.subtract).then_inc(M.w_ready, 1)
                dve.wait_ge(M.ctx_hi, 1)
                dve.tensor_tensor(ctxl[0][:], ctxr[0][:], f32(ctxh[0][:]), ALU.subtract).then_inc(M.ctx_ready, 1)
                for t in range(TT - 1):
                    x_stats(t)
                qk_low(0)
                x_stats(TT - 1)
                row_max(0)
                row_max(1)
                normalise(0)
                norm(0)
                for t in range(TT, TT + 2):
                    x_stats(t)
                for i in range(NT):
                    b, tt = divmod(i, TT)
                    if i + 1 < NT:
                        normalise(i + 1)
                    if i > TT:
                        add_x(i - TT - 1)
                    if tt == 1 and b + 1 < B:
                        qk_low(b + 1)
                    if i + 1 < NT:
                        norm(i + 1)
                    if i + TT + 2 < NT:
                        x_stats(i + TT + 2)
                    attn_low(i)
                    low(i)
                    if i + 2 < NT:
                        row_max(i + 2)
                next_stats, _, _ = ln_vector(dve, G.moe_ln, x, None, None)
                add_x(NT - TT - 1)
                dve.wait_ge(M.x_added, TT)
                for t in range(TT):
                    next_stats(t)
                    add_x(NT - TT + t)

            @block.tensor
            def _(pe):
                turn_x = ln_tensor(pe, R, ident, lambda t: psT)

                def qk(b):
                    pe.wait_ge(M.ctx_ready, b + 1)
                    if b >= 1:
                        pe.wait_ge(M.qk_ready, 2 * b)
                    for j in range(2):
                        for k in range(KV):
                            last = product(pe, psQ[j][:], (wh[:, j, k, :], wl[:, j, k, :]),
                                           (ctxh[b % 2][:, k, :], ctxl[b % 2][:, k, :]), k == 0, k == KV - 1)
                        last.then_inc(M.qk_done, 1)

                def scores(i):
                    b, mt = divmod(i, TT)
                    pe.wait_ge(M.qk_ready, 2 * b + 2)
                    if i >= 2:
                        pe.wait_ge(M.exp_done, i - 1)
                    m = slice(mt * P, (mt + 1) * P)
                    hi, lo = qkh[b % 2], qkl[b % 2]
                    product(pe, psS[i % 2][:], (hi[:, 0, m], lo[:, 0, m]), (hi[:, 1, :], lo[:, 1, :]),
                            True, True).then_inc(M.s_done, 1)

                def turn(i):
                    pe.wait_ge(M.norm_ready, i + 1)
                    if i >= 1:
                        pe.wait_ge(M.a_ready, i)
                    for k in range(TT):
                        last = pe.transpose(psA[:, k * P:(k + 1) * P], prob[i % NPROB][:, k * P:(k + 1) * P], ident)
                    last.then_inc(M.a_turned, 1)

                def wd(n):
                    pe.wait_ge(M.had_ready, 1)
                    pe.wait_ge(M.wd_ready, n + 1)
                    if n >= 1:
                        pe.wait_ge(M.wd_out, n)
                    pe.matmul(psW[:], hadr[:], wdh[n % 2][:], start=True, stop=False)
                    pe.matmul(psW[:], hadr[:], wdl[n % 2][:], start=False, stop=True).then_inc(M.wd_done, 1)

                def weighted(t):
                    b = t // TT
                    if t % TT == 0:
                        pe.wait_ge(M.a_ready, t + TT)
                    pe.wait_ge(R.xT_ready, t + 1)
                    if t > NT - TT:
                        pe.wait_ge(M.x_added, t - 1)
                    elif t >= 1:
                        pe.wait_ge(M.x_added, t)
                    tok = slice(t * P, (t + 1) * P)
                    for k in range(KC):
                        last = product(pe, sum_bank(t)[:], (R.xTh[:, k, tok], R.xTl[:, k, tok]),
                                       (Ah[b % 2][:, k, :], Al[b % 2][:, k, :]), k == 0, k == KC - 1)
                    last.then_inc(M.x_done, 1)

                pe.wait_ge(M.w_ready, 1)
                qk(0)
                scores(0)
                scores(1)
                pe.wait_ge(M.ident_loaded, 16)
                for i in range(NT + TT):
                    b, tt = divmod(i, TT)
                    if i < NT:
                        turn(i)
                        if i >= 1:
                            pe.wait_ge(R.xT_ready, i)
                        turn_x(i)
                        if i + 2 < NT:
                            scores(i + 2)
                    if 0 <= i - WD_LAG < NF:
                        wd(i - WD_LAG)
                    if i >= TT:
                        weighted(i - TT)
                    if tt == 0 and b + 1 < B:
                        qk(b + 1)


def gated_ffn(nc, io, G, name, weights, down, NG, GC, LAST):
    moe = name == "moe"
    XN = 2 * SUBS if moe else 2
    STEPS = B * GC
    COUNT_STEP = 7
    LINKS = 2
    with ExitStack() as ctx:
        sb, ps, sem = scope(nc, ctx, name)
        x, ident = G.x, G.ident
        if moe:
            raw = [G.weights[:, j * WSLICE:(j + 1) * WSLICE] for j in range(3)] + [sb("w_raw3", [P, WSLICE], F32)]
            xn = [G.rows[:, i * C:(i + 1) * C] for i in range(XN)]
        else:
            raw = [sb(f"w_raw{j}", [P, WSLICE], F32) for j in range(GC)]
            xn = [sb(f"xn{i}", [P, C], F32) for i in range(XN)]
        whi = [sb(f"w_hi{j}", [P, WSLICE], F32R) for j in range(GC)]
        wlo = [sb(f"w_lo{j}", [P, WSLICE], F32R) for j in range(GC)]
        act_out = [sb(f"silu{i}", [P, S], F32) for i in range(2)]
        hhi = [sb(f"hidden_hi{i}", [P, S], F32R) for i in range(2)]
        hlo = [sb(f"hidden_lo{i}", [P, S], F32R) for i in range(2)]
        psG = [ps(f"ps_gate{i}") for i in range(2)]
        psU = [ps(f"ps_up{i}") for i in range(2)]
        psY = [ps(f"ps_y{i}") for i in range(TT)]
        R = ln_buffers(sb, sem, xn, G.moe_ln if moe else None)
        PAIRS, EARLY = NT // 2, 2
        M = Bag()
        M.w_hi = sem("w_hi")
        M.w_ready = sem("w_ready")
        M.gate_done = sem("gate_done")
        M.up_done = sem("up_done")
        M.silu_done = sem("silu_done")
        M.hidden_steps = sem("hidden_steps")
        M.hidden_ready = sem("hidden_ready")
        M.hidden_free = sem("hidden_free")
        M.y_added = sem("y_added")
        M.const_loaded = sem("const_loaded")
        M.stored = sem("stored")
        M.prep = sem("prep")
        M.prep_pool = sem("prep_pool")
        M.prep_pe = sem("prep_pe")
        M.prep_act = sem("prep_act")
        M.normed = sem("normed")
        M.flown = sem("flown")
        M.rot_done = sem("rot_done")
        M.rot_hi = sem("rot_hi")
        M.rot_ready = sem("rot_ready")
        M.fold_loaded = sem("fold_loaded")
        M.fold_stored = sem("fold_stored")
        M.now_ready = sem("now_ready")
        raw_loaded = [sem(f"raw_loaded{j}") for j in range(GC)]
        raw_parts = 1 if down is None else 2
        if moe:
            gr = sb("router", [P, KC, RG], F32)
            grs = sb("router_hi_lo", [P, KC, 2 * RG], F32R)
            grh, grl = grs[:, :, 0:RG], grs[:, :, RG:]
            lgT = sb("logitsT", [2 * RG, S], F32)
            add_parts = sb("sum_of_parts", [2 * RG, RG], F32)
            consts = sb("route_consts", [P, E * E + E + TILES], F32)
            lower = consts[:, 0:E * E].rearrange("p (a b) -> p a b", a=E)
            fills = consts[:, E * E:E * E + E]
            tiles = consts[:, E * E + E:]
            sums = sb("sums", [P, 2, P], F32)
            sums_r = sb("sums_r", [P, 2, P], F32R)
            lg = sb("logits", [P, NT, RG], F32)
            pr = sb("probs", [P, NT, E], F32)
            sc1 = sb("row_scratch", [P, NT], F32)
            sig = sb("shared_gate", [P, NT], F32)
            beats = sb("beats", [P, NT // 4, E, E], F32)
            ties = sb("ties", [P, NT // 4, E, E], F32)
            rank = sb("rank", [P, NT, E], F32)
            first = [sb(f"is_entry{k}", [P, NT, E], F32) for k in range(2)]
            chosen = sb("chosen", [P, NT, E], F32R)
            slot = sb("slot", [P, NT, E], F32)
            scr = sb("route_scratch", [P, NT, E], F32)
            load = sb("expert_load", [P, E], F32)
            ntile = sb("expert_tiles", [P, E], F32)
            start = sb("expert_start", [P, E], F32)
            end = sb("expert_end", [P, E], F32)
            ge = sb("tile_past", [P, TILES, E], F32)
            te = sb("tile_expert_f", [P, TILES], F32)
            posf = [sb(f"slot_f{k}", [P, NT], F32) for k in range(2)]
            low7 = sb("slot_low", [P, NT], I32)
            high = sb("slot_high", [P, NT], I32)
            place = [sb(f"table_place{k}", [P, NT], I32) for k in range(2)]
            pos = [sb(f"slot{k}", [P, NT], I32) for k in range(2)]
            weight = [sb(f"weight{k}", [P, NT], F32) for k in range(2)]
            entries = [sb(f"entries{k}", [P, NT, 2], I32) for k in range(2)]
            slots = sb("slot_entries", [P, TILES * SUBS, 2], I32)
            xn_stored = [sem(f"xn_stored{i}") for i in range(XN)]
            M.routed = sem("routed")
            M.counted = sem("counted")
            M.route_chain = sem("route_chain")
            M.places_ready = sem("places_ready")
            M.fill_ready = sem("fill_ready")
            M.table_filled = sem("table_filled")
            M.scattered = sem("scattered")
            M.table_loaded = sem("table_loaded")
            FOLD = 32
            fold = [sb(f"fold{i}", [P, NF, FOLD], F32) for i in range(2)]
        else:
            had = sb("h128", [P, P], F32)
            hadr = sb("h128_r", [P, P], F32R)
            half_turned = sb("butterfly", [P, C], F32)
            shift = sb("ln_shift", [P, NT], F32)
            su_ug = sb("su_ug", [P, C], F32)
            tabs = sb("tables", [P, 3, NF], F32)
            scales = sb("scales", [P, 2, NF], F32)
            now = sb("scales_now", [P, 2, GC], F32)
            uTh, uTl = sb("uT_hi", [P, KC, S], F32R), sb("uT_lo", [P, KC, S], F32R)

        def u_tile(t):
            tt = t % TT
            return uTh[:, :, tt * P:(tt + 1) * P], uTl[:, :, tt * P:(tt + 1) * P]

        ln_dst = xT_tile(R) if moe else u_tile

        def ln_bank(t):
            if t < 2 * EARLY:
                return psY[t]
            return (psG, psU)[t % 2][0 if t // 2 == EARLY else 1]

        rot_bank = (psG[0], psU[0])

        def pair_columns(n):
            return slice(n * 2 * P, (n + 1) * 2 * P)

        def turned_at(s):
            n = (s + 1) // 2 + EARLY
            return n if (s % 2 or s == 0) and n < PAIRS else None

        def rotated_at(s):
            n = s // 2 + EARLY
            return n if not moe and s % 2 == 0 and n < PAIRS else None

        def groups(eng, body):
            body(0, GC, "first")
            if NG == 3:
                body(1, GC, "middle")
            else:
                with eng.Fori(1, NG - 1) as g:
                    body(g, GC, "middle")
            body(NG - 1, LAST, "last")

        with nc.Block() as block:

            @block.sync
            def _(sp):
                if moe:
                    sp.dma_start(gr[:], io["router"]).then_inc(M.const_loaded, 16)
                    sp.dma_start(consts[:], io["route_consts"].partition_broadcast(P)).then_inc(M.const_loaded, 16)
                    sp.dma_start(sums[:], io["sums"]).then_inc(M.const_loaded, 16)
                else:
                    sp.dma_start(had[:], io["h128"]).then_inc(M.const_loaded, 16)
                    sp.dma_start(su_ug[:], io["su_ug"].partition_broadcast(P)).then_inc(M.const_loaded, 16)
                    sp.dma_start(tabs[:], io["ffn_tables"]).then_inc(M.const_loaded, 16)

                def load_chunk(g, j):
                    if down is None:
                        sp.dma_start(raw[j][:], weights[g * GC + j]).then_inc(raw_loaded[j], 16)
                    else:
                        sp.dma_start(raw[j][:, 0:2 * C], weights[g * GC + j]).then_inc(raw_loaded[j], 16)
                        sp.dma_start(raw[j][:, 2 * C:], down[g * GC + j]).then_inc(raw_loaded[j], 16)

                for j in range(GC):
                    load_chunk(0, j)
                if moe:
                    for t in range(NT):
                        sp.wait_ge(R.xn_ready, t + 1)
                        sp.dma_start(G.xn_dram[t * P:(t + 1) * P, :], xn[t % XN][:]).then_inc(xn_stored[t % XN], 16)
                        if t == NT - 1:
                            sp.dma_start(G.xn_dram[TOK:, :], xn[t % XN][:]).then_inc(M.stored, 16)

                def refill(g, gc):
                    for j in range(gc):
                        sp.wait_ge(M.w_ready, ((g - 1) * GC + j + 1) * 3)
                        load_chunk(g, j)

                if NG == 3:
                    refill(1, GC)
                else:
                    with sp.Fori(1, NG - 1) as g:
                        refill(g, GC)
                refill(NG - 1, LAST)
                if moe:
                    sp.wait_ge(M.places_ready, 2)
                    sp.wait_ge(M.w_ready, ((NG - 1) * GC + LAST) * 3)
                    load_expert(sp, io, G, 0, G.weights[:, 0:EW], 0)
                for t in range(NT):
                    sp.wait_ge(M.y_added, NT * (NG - 1) + t + 2)
                    to = G.x_dram[t * P:(t + 1) * P, :] if moe else io["out"][t // TT, (t % TT) * P:(t % TT + 1) * P, :]
                    sp.dma_start(to, x[:, t, :]).then_inc(G.x_stored if moe else M.stored, 16)
                if moe:
                    sp.dma_start(G.x_dram[TOK:, :], x[:, NT - 1, :]).then_inc(G.x_stored, 16)
                else:
                    sp.wait_ge(M.stored, 16 * NT)

            @block.gpsimd
            def _(pool):
                rstd = ln_gpsimd(pool, R, None if moe else shift)

                def split_lo(j):
                    for part in range(3):
                        c = slice(part * C, (part + 1) * C)
                        pool.wait_ge(M.w_hi, j * 3 + part + 1)
                        pool.wait_ge(M.w_ready, j * 3 + part)
                        pool.tensor_tensor(wlo[j][:, c], raw[j][:, c], f32(whi[j][:, c]), ALU.subtract).then_inc(M.w_ready, 1)

                for b in range(1 if moe else 0, B):
                    rstd(b)
                    if not moe and b == 0:
                        split_lo(1)
                    if not moe and b == 1:
                        split_lo(2)
                        split_lo(3)
                if moe:
                    ch = Chain(pool, M.prep_pool)
                    had_v, fold_v = (d.rearrange("n p c -> p n c") for d in (G.had_dram, G.fold_dram))
                    for k in range(C // FOLD):
                        c = slice(k * FOLD, (k + 1) * FOLD)
                        if k >= 1:
                            pool.wait_ge(M.fold_stored, 16 * k)
                        pool.dma_start(fold[0][:], had_v[:, :, c]).then_inc(M.fold_loaded, 16)
                        pool.wait_ge(M.fold_loaded, 16 * (k + 1))
                        for st in range(4):
                            src = fold[st % 2][:].rearrange("p (a two b) c -> p a two (b c)", two=2, b=1 << st)
                            dst = fold[1 - st % 2][:].rearrange("p (a two b) c -> p a two (b c)", two=2, b=1 << st)
                            pool.tensor_tensor(dst[:, :, 0, :], src[:, :, 0, :], src[:, :, 1, :], ALU.add).then_inc(M.prep_pool, 1)
                            ch.n += 1
                            ch.link(pool.tensor_tensor(dst[:, :, 1, :], src[:, :, 0, :], src[:, :, 1, :], ALU.subtract))
                        pool.dma_start(fold_v[:, :, c], fold[0][:]).then_inc(M.fold_stored, 16)
                    pool.wait_ge(M.fold_stored, 16 * (C // FOLD))
                    ch.link(pool.memset(slots[:], 0))
                    pool.iota(slots[:, :, 0], pattern=[[0, TILES * SUBS]], base=TOK, channel_multiplier=1).then_inc(M.fill_ready, 1)
                    for k in range(2):
                        pool.iota(entries[k][:, :, 0], pattern=[[P, NT]], base=0, channel_multiplier=1).then_inc(M.fill_ready, 1)
                    pool.wait_ge(M.fill_ready, 3)
                    table = G.table_dram.rearrange("(p n) two -> p n two", p=P)
                    pool.dma_start(table, slots[:]).then_inc(M.table_filled, 16)
                    pool.wait_ge(M.table_filled, 16)
                    pool.wait_ge(M.places_ready, 2)
                    for k in range(2):
                        for t in range(NT):
                            pool.indirect_dma_start(
                                out=G.table_dram, out_offset=bass.IndirectOffsetOnAxis(ap=place[k][:, t:t + 1], axis=0),
                                in_=entries[k][:, t, :], in_offset=None).then_inc(M.scattered, 16)
                    pool.wait_ge(M.scattered, 16 * 2 * NT)
                    pool.dma_start(slots[:], table).then_inc(M.table_loaded, 16)
                    pool.wait_ge(M.table_loaded, 16)
                    pool.tensor_copy(G.slot_weight[:], slots[:].bitcast(F32)[:, :, 1])
                    ch.link(pool.tensor_copy(G.slot_token[:], slots[:, :, 0]))
                    pool.wait_ge(R.xn_turned, NT)
                    for i in range(XN):
                        pool.wait_ge(xn_stored[i], 16 * (NT // XN))
                    pool.wait_ge(M.stored, 16)
                    for j in range(2):
                        gather_rows(pool, G, j)

            @block.scalar
            def _(act):
                def split_hi(g, j):
                    act.wait_ge(raw_loaded[j], 16 * raw_parts * (g + 1))
                    for part in range(3):
                        c = slice(part * C, (part + 1) * C)
                        act.activation(whi[j][:, c], raw[j][:, c], ACT.Copy).then_inc(M.w_hi, 1)

                high = ln_scalar(act, R, ln_dst, ln_bank)

                def rot_high(n):
                    for half in range(2):
                        act.wait_ge(M.rot_done, 2 * n + half + 1)
                        act.activation(R.xTh[:, 2 * half:2 * half + 2, pair_columns(n)],
                                       rot_bank[half][:].rearrange("p (m n) -> p m n", m=2), ACT.Copy).then_inc(M.rot_hi, 1)

                def high_pair(n):
                    if not moe and n >= 2:
                        act.wait_ge(M.rot_done, 2 * (n - 1))
                    high(2 * n)
                    high(2 * n + 1)


                def norm_pair(n):
                    for t in (2 * n, 2 * n + 1):
                        if t % TT == 0:
                            act.wait_ge(R.rstd_ready, t // TT + 1)
                        if t >= XN:
                            act.wait_ge(R.xn_turned, t - XN + 1)
                        act.activation(xn[t % XN][:], x[:, t, :], ACT.Identity, bias=shift[:, t:t + 1],
                                       scale=R.rstd[:, t:t + 1]).then_inc(M.normed, 1)

                if not moe:
                    norm_pair(0)
                    act.wait_ge(M.const_loaded, 48)
                    act.activation(hadr[:], had[:], ACT.Copy).then_inc(M.prep_act, 1)
                high_pair(0)
                if moe:
                    act.wait_ge(M.const_loaded, 48)
                    act.activation(grh, gr[:], ACT.Copy).then_inc(M.prep_act, 1)
                    act.activation(sums_r[:], sums[:], ACT.Copy).then_inc(M.prep_act, 1)
                if not moe:
                    norm_pair(1)
                split_hi(0, 0)
                high_pair(1)
                if not moe:
                    rot_high(0)
                    rot_high(1)
                split_hi(0, 1)
                if not moe:
                    norm_pair(2)

                def gates(b):
                    t = slice(TT * b, TT * b + TT)
                    act.wait_ge(M.prep_pe, 2 * b + 2)
                    act.activation(lg[:, t, :], psU[0][:, 0:TT * RG].rearrange("p (t e) -> p t e", t=TT), ACT.Copy).then_inc(M.prep_act, 1)
                    act.wait_ge(M.prep_act, 4 + 3 * b)
                    act.activation(sig[:, t], lg[:, t, E], ACT.Sigmoid).then_inc(M.prep_act, 1)

                def beside(s):
                    if turned_at(s) is not None:
                        high_pair(turned_at(s))
                    if rotated_at(s) is not None:
                        rot_high(rotated_at(s))
                    if not moe and turned_at(s + 1) is not None:
                        norm_pair(turned_at(s + 1))
                    if moe and s % GC == 2:
                        act.wait_ge(M.prep_pe, 2 * (s // GC) + 1)
                        act.activation(lgT[:], psG[0][0:2 * RG, :], ACT.Copy).then_inc(M.prep_act, 1)

                def body(g, gc, which):
                    for s in range(B * gc):
                        b, j = divmod(s, gc)
                        if s < gc - (GC - 2):
                            act.wait_ge(M.hidden_free, g * STEPS + s + 1)
                            split_hi(g, GC - 2 + s)
                        if b == B - 1 and j >= 2 and which != "last":
                            act.wait_ge(M.hidden_free, g * STEPS + s + 1)
                            split_hi(g + 1, j - 2)
                        act.wait_ge(M.gate_done, g * STEPS + s + 1)
                        act.wait_ge(M.hidden_ready, g * STEPS + s + 1)
                        if not moe and s == 0:
                            act.wait_ge(M.now_ready, g + 1)
                        ins = act.activation(act_out[s % 2][:], psG[s % 2][:], ACT.Silu, scale=1.0 if moe else now[:, 1, j:j + 1])
                        ins.then_inc(M.silu_done, 1)
                        if which == "first":
                            if moe and s % GC == 3:
                                gates(s // GC)
                            beside(s)
                        if moe and which == "middle" and s == 1:
                            act.wait_ge(M.prep, 4)
                            act.activation(pr[:], pr[:], ACT.Exp).then_inc(M.prep_act, 1)

                groups(act, body)

            @block.vector
            def _(dve):
                def split_lo(g, j):
                    for part in range(3):
                        c = slice(part * C, (part + 1) * C)
                        dve.wait_ge(M.w_hi, (g * GC + j) * 3 + part + 1)
                        last = dve.tensor_tensor(wlo[j][:, c], raw[j][:, c], f32(whi[j][:, c]), ALU.subtract)
                        last.then_inc(M.w_ready, 1)

                dve.sem_inc(M.hidden_steps, 2 * LINKS)
                dve.sem_inc(M.y_added, 1)
                dve.sem_inc(M.hidden_ready, 2)
                stats, norm, low = ln_vector(dve, R, x, ln_dst, ln_bank, stored=xn_stored if moe else None)
                fly = Chain(dve, M.flown)

                def scale_and_fly(t):
                    dve.wait_ge(M.normed, t + 1)
                    row = xn[t % XN]
                    fly.link(dve.tensor_tensor(row[:], row[:], su_ug[:], ALU.mult))

                    def butterfly(dst, src, view):
                        src, dst = (v[:].rearrange(view, two=2, n=P) for v in (src, dst))
                        dve.tensor_tensor(dst[:, :, 0, :], src[:, :, 0, :], src[:, :, 1, :], ALU.add).then_inc(M.flown, 1)
                        fly.n += 1
                        return dve.tensor_tensor(dst[:, :, 1, :], src[:, :, 0, :], src[:, :, 1, :], ALU.subtract)

                    fly.link(butterfly(half_turned, row, "p (a two n) -> p a two n"))
                    fly.link(butterfly(row, half_turned, "p (two a n) -> p a two n"))
                    dve.sem_inc(R.xn_ready, 1)

                def rot_low(n):
                    for half in range(2):
                        dve.wait_ge(M.rot_hi, 2 * n + half + 1)
                        rows = (slice(None), slice(2 * half, 2 * half + 2), pair_columns(n))
                        dve.tensor_tensor(R.xTl[rows], rot_bank[half][:].rearrange("p (m n) -> p m n", m=2),
                                          f32(R.xTh[rows]), ALU.subtract).then_inc(M.rot_ready, 1)

                if not moe:
                    for t in range(TT):
                        stats(t)
                ch = Chain(dve, M.prep)
                if moe:
                    rt = Chain(dve, M.route_chain)

                    def rank_experts(q):
                        if q == 0:
                            dve.wait_ge(M.prep_act, 3 + 3 * B)
                            rt.link(dve.reduce_sum(sc1[:], pr[:], axis=AX.X))
                            rt.link(dve.reciprocal(sc1[:], sc1[:]))
                            rt.link(dve.tensor_tensor(pr[:], pr[:], sc1[:].unsqueeze(2).broadcast_to([P, NT, E]), ALU.mult))
                        t = slice(4 * q, 4 * q + 4)
                        own = pr[:, t, :].unsqueeze(3).broadcast_to([P, 4, E, E])
                        other = pr[:, t, :].unsqueeze(2).broadcast_to([P, 4, E, E])
                        rt.link(dve.tensor_tensor(beats[:], other, own, ALU.is_gt))
                        rt.link(dve.tensor_tensor(ties[:], other, own, ALU.is_equal))
                        rt.link(dve.tensor_tensor(ties[:], ties[:], lower.unsqueeze(1).broadcast_to([P, 4, E, E]), ALU.mult))
                        rt.link(dve.tensor_tensor(beats[:], beats[:], ties[:], ALU.add))
                        rt.link(dve.reduce_sum(rank[:, t, :], beats[:], axis=AX.X))

                    def choose():
                        for k in range(2):
                            rt.link(dve.tensor_scalar(first[k][:], rank[:], float(k), None, ALU.is_equal))
                            rt.link(dve.tensor_tensor(scr[:], pr[:], first[k][:], ALU.mult))
                            rt.link(dve.reduce_sum(weight[k][:], scr[:], axis=AX.X))
                        dve.tensor_tensor(chosen[:], first[0][:], first[1][:], ALU.add).then_inc(M.routed, 1)

                    def count():
                        dve.wait_ge(M.counted, 1)
                        dve.tensor_copy(slot[:], psG[1][:, 0:NT * E].rearrange("p (t e) -> p t e", t=NT)).then_inc(M.routed, 1)
                        dve.reduce_sum(load[:], psU[1][:, 0:NT * E].rearrange("p (t e) -> p e t", t=NT),
                                       axis=AX.X).then_inc(M.routed, 1)
                        dve.wait_ge(M.routed, 3)

                    def place_tiles():
                        rt.link(dve.tensor_tensor(beats[:, 0, :, :], load[:].unsqueeze(2).broadcast_to([P, E, E]),
                                                  fills.unsqueeze(1).broadcast_to([P, E, E]), ALU.is_gt))
                        rt.link(dve.reduce_sum(ntile[:], beats[:, 0, :, :], axis=AX.X))
                        rt.link(dve.tensor_tensor(ties[:, 0, :, :], ntile[:].unsqueeze(1).broadcast_to([P, E, E]), lower, ALU.mult))
                        rt.link(dve.reduce_sum(start[:], ties[:, 0, :, :], axis=AX.X))
                        rt.link(dve.tensor_tensor(end[:], start[:], ntile[:], ALU.add))
                        rt.link(dve.tensor_tensor(ge[:], end[:].unsqueeze(1).broadcast_to([P, TILES, E]),
                                                  tiles.unsqueeze(2).broadcast_to([P, TILES, E]), ALU.is_le))
                        rt.link(dve.reduce_sum(te[:], ge[:], axis=AX.X))
                        rt.link(dve.tensor_scalar(G.tile_expert[:], te[:], float(E - 1), None, ALU.min))
                        rt.link(dve.tensor_scalar(start[:], start[:], float(SLOTS), None, ALU.mult))
                        rt.link(dve.tensor_tensor(slot[:], slot[:], start[:].unsqueeze(1).broadcast_to([P, NT, E]), ALU.add))

                    def place_entries(k):
                        rt.link(dve.tensor_tensor(scr[:], slot[:], first[k][:], ALU.mult))
                        rt.link(dve.reduce_sum(posf[k][:], scr[:], axis=AX.X))
                        rt.link(dve.tensor_copy(pos[k][:], posf[k][:]))
                        rt.link(dve.tensor_scalar(low7[:], pos[k][:], P - 1, None, ALU.bitwise_and))
                        rt.link(dve.tensor_scalar(high[:], pos[k][:], P.bit_length() - 1, None, ALU.logical_shift_right))
                        rt.link(dve.tensor_copy(entries[k][:].bitcast(F32)[:, :, 1], weight[k][:]))
                        rt.link(dve.tensor_scalar(posf[k][:], low7[:], float(TILES * SUBS), None, ALU.mult))
                        dve.tensor_tensor(place[k][:], posf[k][:], high[:], ALU.add).then_inc(M.places_ready, 1)

                    def route(s):
                        if s == 0:
                            dve.wait_ge(M.prep_act, 2 + 3 * B)
                            ch.link(dve.reduce_max(sc1[:], lg[:, :, 0:E], axis=AX.X))
                            ch.link(dve.tensor_tensor(pr[:], lg[:, :, 0:E], sc1[:].unsqueeze(2).broadcast_to([P, NT, E]), ALU.subtract))
                        if 2 <= s < 6:
                            rank_experts(s - 2)
                        if s == 6:
                            choose()
                        if s == COUNT_STEP:
                            count()
                            place_tiles()
                        if s in (8, 9):
                            place_entries(s - 8)
                else:
                    dve.wait_ge(M.const_loaded, 48)

                prepare = norm if moe else scale_and_fly
                for t in range(TT):
                    prepare(t)
                    if t >= 1:
                        low(t - 1)
                low(TT - 1)
                split_lo(0, 0)
                if moe:
                    dve.wait_ge(M.prep_act, 1)
                    ch.link(dve.tensor_tensor(grl, gr[:], f32(grh), ALU.subtract))
                    ch.link(dve.tensor_tensor(add_parts[:], ident[0:2 * RG, 0:RG], ident[0:2 * RG, RG:2 * RG], ALU.add))
                if not moe:
                    rot_low(0)
                    rot_low(1)
                if moe:
                    split_lo(0, 1)
                for t in range(TT, 2 * TT):
                    stats(t)
                if not moe:
                    up_s, gate_s = scales[:, 0, :], scales[:, 1, :]
                    ch.link(dve.tensor_tensor(up_s, tabs[:, 0, :], tabs[:, 2, :], ALU.mult))
                    ch.link(dve.tensor_scalar(up_s, up_s, float((C * INTER) ** -0.5), None, ALU.mult))
                    ch.link(dve.tensor_scalar(gate_s, tabs[:, 1, :], float(C ** -0.5), None, ALU.mult))
                    dve.tensor_copy(now[:], scales[:, :, 0:GC]).then_inc(M.now_ready, 1)
                for t in range(2 * EARLY, 2 * EARLY + 2):
                    prepare(t)

                def beside(s):
                    if turned_at(s) is not None:
                        low(2 * turned_at(s))
                        low(2 * turned_at(s) + 1)
                    if rotated_at(s) is not None:
                        rot_low(rotated_at(s))
                    if turned_at(s + 1) is not None:
                        prepare(2 * turned_at(s + 1))
                        prepare(2 * turned_at(s + 1) + 1)
                    if s in (1, 3):
                        for t in range((s + 3) // 2 * TT, (s + 5) // 2 * TT):
                            stats(t)

                def body(g, gc, which):
                    def add_x(b):
                        dve.wait_ge(M.hidden_free, g * STEPS + (b + 1) * gc + 2)
                        for lt in range(TT):
                            t = TT * b + lt
                            if moe:
                                if lt == 0:
                                    dve.wait_ge(M.prep_act, 5 + 3 * b)
                                ins = dve.scalar_tensor_tensor(out=x[:, t, :], in0=psY[lt][:], scalar=sig[:, t:t + 1],
                                                               in1=x[:, t, :], op0=ALU.mult, op1=ALU.add)
                            else:
                                ins = dve.tensor_tensor(x[:, t, :], psY[lt][:], x[:, t, :], ALU.add)
                            ins.then_inc(M.y_added, 1)

                    for s in range(B * gc):
                        b, j = divmod(s, gc)
                        if s < gc - (GC - 2) and (moe or which != "first"):
                            split_lo(g, GC - 2 + s)
                        if b == B - 1 and j >= 2 and which != "last":
                            split_lo(g + 1, j - 2)
                        at = g * STEPS + s
                        n = (at + 2) * LINKS
                        hid = act_out[s % 2]
                        dve.wait_ge(M.up_done, at + 1)
                        dve.wait_ge(M.silu_done, at + 1)
                        if moe:
                            ins = dve.tensor_tensor(hid[:], psU[s % 2][:], act_out[s % 2][:], ALU.mult)
                        else:
                            ins = dve.scalar_tensor_tensor(out=hid[:], in0=psU[s % 2][:], scalar=now[:, 0, j:j + 1],
                                                           in1=act_out[s % 2][:], op0=ALU.mult, op1=ALU.mult)
                        ins.then_inc(M.hidden_steps, 1)
                        dve.wait_ge(M.hidden_steps, n + 1)
                        dve.wait_ge(M.hidden_free, at + 1)
                        dve.tensor_copy(hhi[s % 2][:], hid[:]).then_inc(M.hidden_steps, 1)
                        dve.wait_ge(M.hidden_steps, n + LINKS)
                        dve.tensor_tensor(hlo[s % 2][:], hid[:], f32(hhi[s % 2][:]), ALU.subtract).then_inc(M.hidden_ready, 1)
                        if j == 0 and b >= 1:
                            add_x(b - 1)
                        if which == "first":
                            beside(s)
                        if moe and which == "middle":
                            route(s)
                    if not moe and which != "last":
                        dve.tensor_copy(now[:], scales[:, :, bass.ds((g + 1) * GC, GC)]).then_inc(M.now_ready, 1)
                    add_x(B - 1)

                groups(dve, body)

            @block.tensor
            def _(pe):
                turn_x = ln_tensor(pe, R, ident, ln_bank)

                def rotate(n):
                    pe.wait_ge(R.xT_ready, 2 * n + 2)
                    pe.wait_ge(M.prep_act, 1)
                    if n >= 1:
                        pe.wait_ge(M.rot_ready, 2 * n)
                    c = slice(n % 2 * 2 * P, (n % 2 + 1) * 2 * P)
                    for k in range(KC):
                        rows = rot_bank[k // 2][:, k % 2 * 2 * P:(k % 2 + 1) * 2 * P]
                        pe.matmul(rows, hadr[:], uTh[:, k, c], start=True, stop=False)
                        last = pe.matmul(rows, hadr[:], uTl[:, k, c], start=False, stop=True)
                        if k % 2:
                            last.then_inc(M.rot_done, 1)

                def logits(b):
                    pe.wait_ge(M.prep, 1)
                    tok = slice(b * S, (b + 1) * S)
                    for k in range(KC):
                        pe.matmul(psG[0][0:2 * RG, :], grs[:, k, :], R.xTh[:, k, tok], start=k == 0, stop=False)
                        last = pe.matmul(psG[0][0:2 * RG, :], grs[:, k, :], R.xTl[:, k, tok], start=False, stop=k == KC - 1)
                    last.then_inc(M.prep_pe, 1)

                def turn_logits(b):
                    pe.wait_ge(M.prep, 2)
                    pe.wait_ge(M.prep_act, 3 + 3 * b)
                    for t in range(TT):
                        last = pe.matmul(psU[0][:, t * RG:(t + 1) * RG], lgT[:, t * P:(t + 1) * P], add_parts[:], start=True, stop=True)
                    last.then_inc(M.prep_pe, 1)

                if moe:
                    def count_entries(at):
                        pe.wait_ge(M.routed, 1)
                        pe.wait_ge(M.hidden_steps, (at + 2) * LINKS + 1)
                        for d in range(NT):
                            pe.matmul(psG[1][:, d * E:NT * E], sums_r[:, min(d, 1), :],
                                      chosen[:, 0:NT - d, :].rearrange("p t e -> p (t e)"), start=d == 0, stop=d == NT - 1)
                        pe.matmul(psU[1][:, 0:NT * E], sums_r[:, 1, :], chosen[:].rearrange("p t e -> p (t e)"),
                                  start=True, stop=True).then_inc(M.counted, 1)

                for t in range(TT):
                    turn_x(t)
                if not moe:
                    rotate(0)
                    rotate(1)
                pe.sem_inc(M.hidden_free, 2)

                def gate_up(g, gc, s, which):
                    b, j = divmod(s % (B * gc), gc)
                    at = g * STEPS + s
                    if which == "first":
                        if j == 0 and s < STEPS:
                            pe.wait_ge(R.xT_ready if moe else M.rot_ready, TT * (b + 1))
                        if s >= 2:
                            if turned_at(s - 2) is not None:
                                pe.wait_ge(R.xT_ready, 2 * turned_at(s - 2) + 2)
                            if rotated_at(s - 2) is not None:
                                pe.wait_ge(M.rot_ready, 2 * rotated_at(s - 2) + 2)
                            if moe and (s - 2) % GC == 2:
                                pe.wait_ge(M.prep_act, 4 + 3 * ((s - 2) // GC))
                    pe.wait_ge(M.w_ready, (g * GC + s // (B * gc) * gc + j + 1) * 3)
                    pe.wait_ge(M.hidden_steps, at * LINKS + 1)
                    for bank, o, done in ((psG, 0, M.gate_done), (psU, C, M.up_done)):
                        for k in range(KC):
                            c = slice(o + k * P, o + (k + 1) * P)
                            tok = slice(b * S, (b + 1) * S)
                            last = product(pe, bank[s % 2][:], (whi[j][:, c], wlo[j][:, c]),
                                           (R.xTh[:, k, tok], R.xTl[:, k, tok]), k == 0, k == KC - 1)
                        last.then_inc(done, 1)

                def down_step(g, gc, s, which):
                    b, j = divmod(s, gc)
                    at = g * STEPS + s
                    pe.wait_ge(M.hidden_ready, at + 3)
                    if j == 0:
                        pe.wait_ge(M.y_added, (g * B + b) * TT + 1)
                    for lt in range(TT):
                        m = slice(lt * P, (lt + 1) * P)
                        last = product(pe, psY[lt][:], (hhi[s % 2][:, m], hlo[s % 2][:, m]),
                                       (whi[j][:, 2 * C:], wlo[j][:, 2 * C:]), j == 0, j == gc - 1)
                        if moe and which == "first" and s % GC == 2 and lt == TT // 2 - 1:
                            turn_logits(s // GC)
                    last.then_inc(M.hidden_free, 1)

                def beside(s):
                    pe.wait_ge(M.hidden_steps, (s + 2) * LINKS + 1)
                    if turned_at(s) is not None:
                        turn_x(2 * turned_at(s))
                        turn_x(2 * turned_at(s) + 1)
                    if rotated_at(s) is not None and s > 0:
                        rotate(rotated_at(s))
                    if moe and s % GC == 2:
                        logits(s // GC)

                def body(g, gc, which):
                    for s in range(B * gc):
                        if moe and which == "middle" and s == COUNT_STEP + 1:
                            pe.wait_ge(M.routed, 3)
                        if not (which == "last" and s == B * gc - 1):
                            gate_up(g, gc, s + 1, which)
                        if which == "first":
                            beside(s)
                        if moe and which == "middle" and s == COUNT_STEP:
                            count_entries(g * STEPS + s)
                        down_step(g, gc, s, which)
                        if which == "first" and s == 0 and not moe:
                            rotate(rotated_at(s))

                gate_up(0, GC, 0, "first")
                groups(pe, body)


def load_expert(sp, io, G, j, raw, p):
    expert = sp.value_load(G.tile_expert[0:1, bass.ds(j, 1)], min_val=0, max_val=E - 1)
    w = io["expert_w"][bass.ds(expert, 1), :, :].rearrange("one p n -> p (one n)")
    down = 2 * KC * F_MOE
    sp.dma_start(raw[:, 0:down], w[:, 0:down]).then_inc(G.gate_up_loaded[p], 16)
    sp.dma_start(raw[:, down:], w[:, down:]).then_inc(G.down_loaded[p], 16)


def gather_rows(pool, G, j):
    for u in range(SUBS):
        n = j * SUBS + u
        at = (j % 2 * SUBS + u) * C
        pool.indirect_dma_start(
            out=G.rows[:, at:at + C], out_offset=None, in_=G.xn_dram,
            in_offset=bass.IndirectOffsetOnAxis(ap=G.slot_token[:, n:n + 1], axis=0)).then_inc(G.rows_loaded[j % 2], 16)


def sparse_experts(nc, io, G):
    GATE, UP, DOWN = 0, KC * F_MOE, 2 * KC * F_MOE
    widths = [min(P, F_MOE - f * P) for f in range(FCH)]
    with ExitStack() as ctx:
        sb, ps, sem = scope(nc, ctx, "ex")
        ident = G.ident
        raw = [G.weights[:, 0:EW], sb("w_raw1", [P, EW], F32)]
        whi = [sb(f"w_hi{i}", [P, EW], F32R) for i in range(2)]
        wlo = [sb(f"w_lo{i}", [P, EW], F32R) for i in range(2)]
        rows = [[G.rows[:, (i * SUBS + u) * C:(i * SUBS + u + 1) * C] for u in range(SUBS)] for i in range(2)]
        xh = [sb(f"xT_hi{i}", [P, KC, SLOTS], F32R) for i in range(2)]
        xl = [sb(f"xT_lo{i}", [P, KC, SLOTS], F32R) for i in range(2)]
        silu = [sb(f"silu{f}", [P, SLOTS], F32) for f in range(FCH)]
        prod = [sb(f"hidden{f}", [P, SLOTS], F32) for f in range(FCH)]
        hh = [sb(f"hidden_hi{f}", [P, SLOTS], F32R) for f in range(FCH)]
        hl = [sb(f"hidden_lo{f}", [P, SLOTS], F32R) for f in range(FCH)]
        ysb = [sb(f"y{u}", [P, C], F32) for u in range(SUBS)]
        mask8 = sb("mask", [P, B * S], U8)
        psT = [ps(f"ps_t{u}") for u in range(SUBS)]
        psH = [ps(f"ps_h{f}") for f in range(FCH)]
        psY = [ps(f"ps_y{u}") for u in range(SUBS)]
        M = Bag()
        gu_loaded, down_loaded, rows_loaded = G.gate_up_loaded, G.down_loaded, G.rows_loaded
        y_summed = [sem(f"y_summed{u}") for u in range(SUBS)]
        wnow = [sb(f"weight_now{i}", [P, SUBS], F32) for i in range(2)]
        M.weight_now = sem("weight_now")
        M.mask_loaded = sem("mask_loaded")
        M.gu_hi = sem("gate_up_hi")
        M.gu_ready = sem("gate_up_ready")
        M.down_hi = sem("down_hi")
        M.down_ready = sem("down_ready")
        M.turned = sem("turned")
        M.x_hi = sem("x_hi")
        M.x_ready = sem("x_ready")
        M.h_done = sem("h_done")
        M.silu_done = sem("silu_done")
        M.prod_done = sem("prod_done")
        M.hidden_hi = sem("hidden_hi")
        M.hidden_ready = sem("hidden_ready")
        M.y_done = sem("y_done")
        M.y_copied = sem("y_copied")

        def steps(eng, body):
            body(0, 0, "first")
            body(1, 1, "middle")
            pairs = (TILES - 4) // 2
            with eng.Fori(0, pairs) as i:
                for q in range(2):
                    body(2 * i + 2 + q, q, "middle")
            for j in range(2 * pairs + 2, TILES):
                body(j, j % 2, "last" if j == TILES - 1 else "middle")

        with nc.Block() as block:

            @block.sync
            def _(sp):
                load_expert(sp, io, G, 1, raw[1], 1)
                sp.dma_start(mask8[:], io["mask"].partition_broadcast(P)).then_inc(M.mask_loaded, 16)
                sp.sem_clear(G.used_sems)

                def body(j, p, which):
                    if not isinstance(j, int) or j + 2 < TILES:
                        sp.wait_ge(M.down_ready, j + 1)
                        load_expert(sp, io, G, j + 2, raw[p], p)

                steps(sp, body)
                sp.wait_ge(M.gu_ready, 2 * TILES)
                load_qkv(sp, io, G, 0)
                sp.wait_ge(M.turned, SUBS * (TILES - 1))
                load_context(sp, io, G, 0, 0)

            @block.gpsimd
            def _(pool):
                def add_rows(j):
                    for u in range(SUBS):
                        n = j * SUBS + u
                        pool.wait_ge(M.y_copied, SUBS * (j + 1) + u + 1)
                        if n >= 1:
                            pool.wait_ge(y_summed[1 - u], 16 * ((n + 1) // SUBS))
                        pool.indirect_dma_start(
                            out=G.x_dram, out_offset=bass.IndirectOffsetOnAxis(ap=G.slot_token[:, n:n + 1], axis=0),
                            in_=ysb[u][:], in_offset=None, compute_op=ALU.add).then_inc(y_summed[u], 16)

                for j in range(2, TILES):
                    pool.wait_ge(M.turned, SUBS * (j - 1))
                    gather_rows(pool, G, j)
                    if j == 3:
                        pool.wait_ge(G.x_stored, 16 * (NT + 1))
                    if j >= 3:
                        add_rows(j - 3)
                for j in range(TILES - 3, TILES):
                    add_rows(j)
                for u in range(SUBS):
                    pool.wait_ge(y_summed[u], 16 * TILES)

            @block.scalar
            def _(act):
                def split_gate_up(j, p):
                    act.wait_ge(gu_loaded[p], (j + 2 - p) * 8)
                    for a, b in ((GATE, UP), (UP, DOWN)):
                        act.activation(whi[p][:, a:b], raw[p][:, a:b], ACT.Copy).then_inc(M.gu_hi, 1)

                def split_down(j, p):
                    act.wait_ge(down_loaded[p], (j + 2 - p) * 8)
                    act.activation(whi[p][:, DOWN:], raw[p][:, DOWN:], ACT.Copy).then_inc(M.down_hi, 1)

                def turned_high(j, p):
                    for u in range(SUBS):
                        act.wait_ge(M.turned, SUBS * j + u + 1)
                        act.activation(xh[p][:, :, u * P:(u + 1) * P], psT[u][:].rearrange("p (k n) -> p k n", k=KC),
                                       ACT.Copy).then_inc(M.x_hi, 1)

                def weigh_y(j, p):
                    act.wait_ge(M.weight_now, j + 1)
                    for u in range(SUBS):
                        act.wait_ge(M.y_done, SUBS * j + u + 1)
                        if not isinstance(j, int) or j > 0:
                            act.wait_ge(y_summed[u], 16 * j)
                        act.activation(ysb[u][:], psY[u][:], ACT.Copy, scale=wnow[p][:, u:u + 1]).then_inc(M.y_copied, 1)

                act.sem_inc(M.y_copied, SUBS)
                split_gate_up(0, 0)
                turned_high(0, 0)
                split_down(0, 0)

                def body(j, p, which):
                    if which == "middle":
                        act.wait_ge(M.h_done, FCH * j)
                    if which != "last":
                        split_gate_up(j + 1, 1 - p)
                    for f, w in enumerate(widths):
                        act.wait_ge(M.h_done, FCH * j + f + 1)
                        if which != "first":
                            act.wait_ge(M.prod_done, FCH * j)
                        act.activation(silu[f][0:w, :], psH[f][0:w, 0:SLOTS], ACT.Silu).then_inc(M.silu_done, 1)
                    if which != "last":
                        turned_high(j + 1, 1 - p)
                    if which != "first":
                        weigh_y(j - 1, 1 - p)
                    if which != "last":
                        split_down(j + 1, 1 - p)

                steps(act, body)
                weigh_y(TILES - 1, (TILES - 1) % 2)

            @block.vector
            def _(dve):
                def split_gate_up(j, p):
                    for n, (a, b) in enumerate(((GATE, UP), (UP, DOWN))):
                        dve.wait_ge(M.gu_hi, 2 * j + n + 1)
                        dve.tensor_tensor(wlo[p][:, a:b], raw[p][:, a:b], f32(whi[p][:, a:b]), ALU.subtract).then_inc(M.gu_ready, 1)

                def split_down(j, p):
                    dve.wait_ge(M.down_hi, j + 1)
                    dve.tensor_tensor(wlo[p][:, DOWN:], raw[p][:, DOWN:], f32(whi[p][:, DOWN:]), ALU.subtract).then_inc(M.down_ready, 1)

                def turned_low(j, p):
                    for u in range(SUBS):
                        dve.wait_ge(M.x_hi, SUBS * j + u + 1)
                        dve.tensor_tensor(xl[p][:, :, u * P:(u + 1) * P], psT[u][:].rearrange("p (k n) -> p k n", k=KC),
                                          f32(xh[p][:, :, u * P:(u + 1) * P]), ALU.subtract).then_inc(M.x_ready, 1)

                split_gate_up(0, 0)
                turned_low(0, 0)
                split_down(0, 0)

                def body(j, p, which):
                    if not isinstance(j, int) or j >= 2:
                        dve.wait_ge(M.y_copied, SUBS * j)
                    dve.tensor_copy(wnow[p][:], G.slot_weight[:, bass.ds(j * SUBS, SUBS)]).then_inc(M.weight_now, 1)
                    if which != "last":
                        split_gate_up(j + 1, 1 - p)
                    for f, w in enumerate(widths):
                        dve.wait_ge(M.silu_done, FCH * j + f + 1)
                        if which != "first":
                            dve.wait_ge(M.hidden_ready, FCH * j)
                        dve.tensor_tensor(prod[f][0:w, :], psH[f][0:w, SLOTS:], silu[f][0:w, :], ALU.mult).then_inc(M.prod_done, 1)
                    if which != "last":
                        turned_low(j + 1, 1 - p)
                    for f, w in enumerate(widths):
                        dve.wait_ge(M.prod_done, FCH * j + f + 1)
                        if which != "first":
                            dve.wait_ge(M.y_done, SUBS * j)
                        dve.tensor_copy(hh[f][0:w, :], prod[f][0:w, :]).then_inc(M.hidden_hi, 1)
                        dve.wait_ge(M.hidden_hi, FCH * j + f + 1)
                        dve.tensor_tensor(hl[f][0:w, :], prod[f][0:w, :], f32(hh[f][0:w, :]), ALU.subtract).then_inc(M.hidden_ready, 1)
                    if which != "last":
                        split_down(j + 1, 1 - p)

                steps(dve, body)
                dve.wait_ge(M.mask_loaded, 16)
                dve.tensor_scalar(G.mask_bias[:], mask8[:], MASKED, -MASKED, ALU.mult, ALU.add)
                dve.reduce_max(G.any_key[:], mask8[:].rearrange("p (b s) -> p b s", b=B), axis=AX.X)

            @block.tensor
            def _(pe):
                def turn(j, p):
                    pe.wait_ge(rows_loaded[p], (j + 2 - p) * 8 * SUBS)
                    if not isinstance(j, int) or j > 0:
                        pe.wait_ge(M.x_ready, SUBS * j)
                    for u in range(SUBS):
                        for k in range(KC):
                            last = pe.transpose(psT[u][:, k * P:(k + 1) * P], rows[p][u][:, k * P:(k + 1) * P], ident)
                        last.then_inc(M.turned, 1)

                def down(j, p):
                    pe.wait_ge(M.hidden_ready, FCH * (j + 1))
                    pe.wait_ge(M.down_ready, j + 1)
                    pe.wait_ge(M.y_copied, SUBS * (j + 1))
                    for u in range(SUBS):
                        m = slice(u * P, (u + 1) * P)
                        for f, w in enumerate(widths):
                            c = slice(DOWN + f * C, DOWN + (f + 1) * C)
                            ins = product(pe, psY[u][:], (hh[f][0:w, m], hl[f][0:w, m]),
                                          (whi[p][0:w, c], wlo[p][0:w, c]), f == 0, f == FCH - 1)
                        ins.then_inc(M.y_done, 1)

                turn(0, 0)

                def body(j, p, which):
                    pe.wait_ge(M.gu_ready, 2 * (j + 1))
                    pe.wait_ge(M.x_ready, SUBS * (j + 1))
                    if which != "first":
                        pe.wait_ge(M.prod_done, FCH * j)
                    for f, w in enumerate(widths):
                        for o, half in ((GATE, 0), (UP, SLOTS)):
                            for k in range(KC):
                                c = slice(o + k * F_MOE + f * P, o + k * F_MOE + f * P + w)
                                ins = product(pe, psH[f][0:w, half:half + SLOTS], (whi[p][:, c], wlo[p][:, c]),
                                              (xh[p][:, k, :], xl[p][:, k, :]), k == 0, k == KC - 1)
                        ins.then_inc(M.h_done, 1)
                    if which != "last":
                        turn(j + 1, 1 - p)
                    if which != "first":
                        down(j - 1, 1 - p)

                steps(pe, body)
                down(TILES - 1, (TILES - 1) % 2)


def load_qkv(sp, io, G, g):
    n = KC * HPG * D + 2 * KV * D
    sp.dma_start(G.weights[:, 0:n], io["xa_w"][g, :, 0:n]).then_inc(G.qkv_loaded, 16)


def context_buffer(G, i):
    at = (TILES + i) % 2 * SUBS * C
    return G.rows[:, at:at + KV * S].rearrange("p (k n) -> p k n", k=KV)


def load_context(sp, io, G, b, i):
    sp.dma_start(context_buffer(G, i), io["ctxT"][b]).then_inc(G.ctx_loaded[i], 16)


def cross_attention(nc, io, G):
    UNITS = B * HPG
    TILES = UNITS * TT
    LASTU = GROUPS * UNITS - 1
    SCALE = float(D) ** -0.5
    LAG = 8
    with ExitStack() as ctx:
        sb, ps, sem = scope(nc, ctx, "xa")
        x, ident = G.x, G.ident
        ctxr = [context_buffer(G, i) for i in range(2)]
        ctxh, ctxl = sb("ctx_hi", [P, KV, S], F32R), sb("ctx_lo", [P, KV, S], F32R)
        NQ, NKV, NO = KC * HPG * D, 2 * KV * D, HPG * C
        raw = G.weights[:, 0:NQ + NKV]
        rqkv, ro = raw, raw[:, 0:NO]
        NQK = NQ + NKV // 2
        qkvh, qkvl = sb("wqkv_hi", [P, NQ + NKV], F32R), sb("wqkv_lo", [P, NQ + NKV], F32R)
        woh, wol = sb("wo_hi", [P, NO], F32R), sb("wo_lo", [P, NO], F32R)
        qh, ql = ([sb(f"q_{n}{i}", [P, S], F32R) for i in range(2)] for n in ("hi", "lo"))
        kh, kl = ([sb(f"k_{n}{i}", [P, S], F32R) for i in range(2)] for n in ("hi", "lo"))
        vh, vl = sb("v_hi", [P, S], F32R), sb("v_lo", [P, S], F32R)
        o_hi = [sb(f"out_hi{i}", [P, S], F32R) for i in range(3)]
        o_lo = [sb(f"out_lo{i}", [P, S], F32R) for i in range(3)]
        prob = [G.weights[:, NQ + NKV + i * S:NQ + NKV + (i + 1) * S] for i in range(4)]
        PTh, PTl = sb("probT_hi", [P, TT, S], F32R), sb("probT_lo", [P, TT, S], F32R)
        maskb, some = G.mask_bias, G.any_key
        mx, nmx = sb("max", [P, 4], F32), sb("minus_max", [P, 4], F32)
        tot, inv = sb("total", [P, 4], F32), sb("inverse", [P, 4], F32)
        idle = sb("idle", [P, 1], F32)
        psS = [ps(f"ps_s{i}") for i in range(2)]
        psT = [ps(f"ps_t{i}") for i in range(2)]
        psP = [ps(f"ps_p{i}") for i in range(2)]
        psO = [ps(f"ps_o{i}") for i in range(2)]
        R = ln_buffers(sb, sem, xn=prob[2:])
        x_loaded = [sem(f"x_loaded{b}") for b in range(B)]
        vT = G.weights[:, NQ + NKV + 4 * S:NQ + NKV + 5 * S]
        shift = sb("ln_shift", [P, NT], F32)
        M = Bag()
        ctx_loaded = G.ctx_loaded
        M.o_loaded = sem("o_loaded")
        M.qk_hi = sem("qk_hi")
        M.qk_ready = sem("qk_ready")
        M.wv_hi = sem("wv_hi")
        M.wv_ready = sem("wv_ready")
        M.wo_hi = sem("wo_hi")
        M.wo_ready = sem("wo_ready")
        M.ctx_hi = sem("ctx_hi")
        M.ctx_ready = sem("ctx_ready")
        M.proj_done = sem("proj_done")
        M.proj_hi = sem("proj_hi")
        M.proj_ready = sem("proj_ready")
        M.s_done = sem("s_done")
        M.max_ready = sem("max_ready")
        M.exp_done = sem("exp_done")
        M.norm_ready = sem("norm_ready")
        M.p_turned = sem("p_turned")
        M.pt_hi = sem("pt_hi")
        M.pt_ready = sem("pt_ready")
        M.o_done = sem("o_done")
        M.x_added = sem("x_added")
        M.chain = sem("chain")
        M.v_turned = sem("v_turned")
        M.v_hi = sem("v_hi")
        M.v_ready = sem("v_ready")

        EARLY = 8

        def ln_bank(t):
            return (psT + psO)[t % 4]

        def out_buf(b, h):
            return 2 if h == 1 else b % 2

        FIRST_K, FIRST_Q, SECOND_Q = Place(0, 0), Place(1, 1), Place(2, 0)
        FINAL_PV = Place(2 + 6 * (LASTU // 2) + 3, 1)

        def last_pv(pair, h, end):
            return Place(2 + 6 * pair + (0 if h == 0 else 2 if end else 4), 0)

        def this_v(pair):
            return Place(2 + 6 * pair + 1, 1)

        def next_q(pair, h):
            return Place(2 + 6 * pair + (2 if h == 0 else 5), h)

        def next_k(pair):
            return Place(2 + 6 * pair + 3, 1)

        def at_least(eng, s, v):
            if not isinstance(v, int) or v > 0:
                eng.wait_ge(s, v)

        def groups(eng, body):
            body(0, "first")
            with eng.Fori(1, GROUPS - 1) as g:
                body(g, "middle")
            body(GROUPS - 1, "last")

        def units(g, which):
            for ul in range(UNITS):
                left = UNITS - 1 - ul if which == "last" else UNITS
                yield ul, ul // HPG, ul % HPG, g * B + ul // HPG, g * UNITS + ul, g * TILES + TT * ul, left

        with nc.Block() as block:

            @block.sync
            def _(sp):
                def load_x(b):
                    rows = G.x_dram[b * S:(b + 1) * S, :].rearrange("(t p) c -> p t c", p=P)
                    sp.dma_start(x[:, TT * b:TT * b + TT, :], rows).then_inc(x_loaded[b], 16)

                load_x(0)

                def load_o(g):
                    sp.wait_ge(M.wv_ready, g + 1)
                    sp.dma_start(ro, io["xa_w"][g, :, NQ + NKV:]).then_inc(M.o_loaded, 16)

                def next_ctx(pair, b):
                    sp.wait_ge(M.ctx_ready, pair + 1)
                    load_context(sp, io, G, (b + 2) % B, b % 2)

                for b in range(1, B):
                    load_x(b)
                load_o(0)
                load_context(sp, io, G, 1, 1)
                next_ctx(0, 0)
                with sp.Fori(1, GROUPS) as g:
                    sp.wait_ge(M.wo_ready, g + 1)
                    load_qkv(sp, io, G, g)
                    for b in range(1, B + 1):
                        next_ctx((g - 1) * B + b, b % B)
                    load_o(g)
                next_ctx((GROUPS - 1) * B + 1, 1)

            @block.gpsimd
            def _(pool):
                rstd = ln_gpsimd(pool, R, shift)

                def ctx_low(pair, b):
                    pool.wait_ge(M.ctx_hi, pair + 1)
                    pool.tensor_tensor(ctxl[:], ctxr[b % 2][:], f32(ctxh[:]), ALU.subtract).then_inc(M.ctx_ready, 1)

                ctx_low(0, 0)
                for b in range(B):
                    rstd(b)

                def body(g, which):
                    for b in range(B):
                        if not (which == "last" and b == B - 1):
                            ctx_low(g * B + b + 1, (b + 1) % B)
                groups(pool, body)

            @block.scalar
            def _(act):
                def split_qk(g):
                    act.wait_ge(G.qkv_loaded, 16 * (g + 1))
                    act.activation(qkvh[:, 0:NQK], rqkv[:, 0:NQK], ACT.Copy).then_inc(M.qk_hi, 1)

                def split_v(g):
                    act.activation(qkvh[:, NQK:], rqkv[:, NQK:], ACT.Copy).then_inc(M.wv_hi, 1)

                def split_o(g):
                    act.wait_ge(M.o_loaded, 16 * (g + 1))
                    act.activation(woh[:], ro, ACT.Copy).then_inc(M.wo_hi, 1)

                def proj_high(at, out):
                    act.wait_ge(M.proj_done, at.n + 1)
                    act.activation(out[:], psP[at.bank][:], ACT.Copy).then_inc(M.proj_hi, 1)

                def exp(i, slot):
                    act.wait_ge(M.max_ready, i + 1)
                    act.activation(prob[slot][:], prob[slot][:], ACT.Exp, bias=nmx[:, slot:slot + 1], scale=SCALE,
                                   accum_out=tot[:, slot:slot + 1]).then_inc(M.exp_done, 1)

                def turned_high(i, tt):
                    act.wait_ge(M.p_turned, i + 1)
                    act.activation(PTh[:, :, tt * P:(tt + 1) * P], psT[tt % 2][:].rearrange("p (k n) -> p k n", k=TT),
                                   ACT.Copy).then_inc(M.pt_hi, 1)

                act.wait_ge(ctx_loaded[0], 16)
                act.activation(ctxh[:], ctxr[0][:], ACT.Copy).then_inc(M.ctx_hi, 1)
                split_qk(0)
                split_v(0)
                proj_high(FIRST_K, kh[0])
                high = ln_scalar(act, R, xT_tile(R), ln_bank)
                for t in range(NT + 1):
                    if t < NT:
                        if t % TT == 0:
                            act.wait_ge(R.rstd_ready, t // TT + 1)
                        if t >= 2:
                            act.wait_ge(R.xn_turned, t - 1)
                        act.activation(R.xn[t % 2][:], x[:, t, :], ACT.Identity, bias=shift[:, t:t + 1],
                                       scale=R.rstd[:, t:t + 1]).then_inc(R.xn_ready, 1)
                    if t >= 1:
                        high(t - 1)
                    if t == EARLY:
                        proj_high(FIRST_Q, qh[0])
                        proj_high(SECOND_Q, qh[1])
                for t in range(3):
                    exp(t, t)

                def body(g, which):
                    for ul, b, h, pair, u, i, left in units(g, which):
                        has_pv = not (which == "first" and ul == 0)
                        exp(i + 3, 3)
                        if has_pv:
                            act.wait_ge(M.proj_done, last_pv(pair, h, left < 2).n + 1)
                        turned_high(i, 0)
                        if has_pv:
                            proj_high(last_pv(pair, h, left < 2), o_hi[out_buf(b, 1 - h)])
                        if ul == UNITS - 2 and which != "last":
                            act.wait_ge(M.proj_done, next_q(pair - 1, 1).n + 1)
                            split_qk(g + 1)
                        turned_high(i + 1, 1)
                        if left >= 1:
                            exp(i + 4, 0)
                        if h == 0:
                            proj_high(this_v(pair), vT)
                            if left >= 2:
                                act.wait_ge(ctx_loaded[(b + 1) % 2], 16 * (g * (B // 2) + (b + 1) // 2 + 1))
                                act.activation(ctxh[:], ctxr[(b + 1) % 2][:], ACT.Copy).then_inc(M.ctx_hi, 1)
                        turned_high(i + 2, 2)
                        if left >= 1:
                            exp(i + 5, 1)
                        if h == 0:
                            act.wait_ge(M.v_turned, pair + 1)
                            act.activation(vh[:], psO[1][:], ACT.Copy).then_inc(M.v_hi, 1)
                        if ul == UNITS - 2 and which != "last":
                            split_v(g + 1)
                        turned_high(i + 3, 3)
                        if left >= 1:
                            exp(i + 6, 2)
                        if left >= 2:
                            proj_high(next_q(pair, h), qh[h])
                            if h == 0:
                                proj_high(next_k(pair), kh[(b + 1) % 2])
                        if ul == 1:
                            if which != "first":
                                act.wait_ge(M.o_done, g * B * TT)
                            split_o(g)

                groups(act, body)
                proj_high(FINAL_PV, o_hi[out_buf(B - 1, 1)])

            @block.vector
            def _(dve):
                def split_qk(g):
                    dve.wait_ge(M.qk_hi, g + 1)
                    dve.tensor_tensor(qkvl[:, 0:NQK], rqkv[:, 0:NQK], f32(qkvh[:, 0:NQK]), ALU.subtract).then_inc(M.qk_ready, 1)

                def split_v(g):
                    dve.wait_ge(M.wv_hi, g + 1)
                    dve.tensor_tensor(qkvl[:, NQK:], rqkv[:, NQK:], f32(qkvh[:, NQK:]), ALU.subtract).then_inc(M.wv_ready, 1)

                def split_o(g):
                    dve.wait_ge(M.wo_hi, g + 1)
                    dve.tensor_tensor(wol[:], ro, f32(woh[:]), ALU.subtract).then_inc(M.wo_ready, 1)

                def proj_low(at, hi, lo):
                    dve.wait_ge(M.proj_hi, at.n + 1)
                    dve.tensor_tensor(lo[:], psP[at.bank][:], f32(hi[:]), ALU.subtract).then_inc(M.proj_ready, 1)

                def masked_max(i, slot, b, n):
                    dve.wait_ge(M.s_done, i + 1)
                    at_least(dve, M.p_turned, i - 3)
                    dve.memset(idle[:], 0.0)
                    dve.tensor_tensor_reduce(out=prob[slot][:], in0=psS[slot % 2][:], in1=maskb[:, b * S:(b + 1) * S],
                                             scale=1.0, scalar=-3.4e38, op0=ALU.add, op1=ALU.max,
                                             accum_out=mx[:, slot:slot + 1]).then_inc(M.chain, 1)
                    dve.wait_ge(M.chain, n)
                    dve.tensor_scalar(nmx[:, slot:slot + 1], mx[:, slot:slot + 1], -SCALE, None,
                                      ALU.mult).then_inc(M.max_ready, 1)

                def normalise(i, slot, b, n):
                    dve.wait_ge(M.exp_done, i + 1)
                    dve.reciprocal(inv[:, slot:slot + 1], tot[:, slot:slot + 1]).then_inc(M.chain, 1)
                    dve.wait_ge(M.chain, n)
                    dve.tensor_scalar(prob[slot][:], prob[slot][:], inv[:, slot:slot + 1], some[:, b:b + 1],
                                      ALU.mult, ALU.mult).then_inc(M.norm_ready, 1)

                def turned_low(i, tt):
                    dve.wait_ge(M.pt_hi, i + 1)
                    dve.tensor_tensor(PTl[:, :, tt * P:(tt + 1) * P], psT[tt % 2][:].rearrange("p (k n) -> p k n", k=TT),
                                      f32(PTh[:, :, tt * P:(tt + 1) * P]), ALU.subtract).then_inc(M.pt_ready, 1)

                def add_x(pair, b, tt):
                    dve.wait_ge(M.o_done, pair * TT + tt + 1)
                    t = TT * b + tt
                    dve.tensor_tensor(x[:, t, :], psO[tt % 2][:], x[:, t, :], ALU.add).then_inc(M.x_added, 1)

                dve.sem_inc(M.wo_ready, 1)
                stats, _, low = ln_vector(dve, R, x, xT_tile(R), ln_bank)
                for i in range(NT + LAG):
                    if i < NT:
                        if i % TT == 0:
                            dve.wait_ge(x_loaded[i // TT], 16)
                        stats(i)
                    if i == 1:
                        split_qk(0)
                        split_v(0)
                    if i == LAG - 1:
                        proj_low(FIRST_K, kh[0], kl[0])
                    if i >= LAG:
                        low(i - LAG)
                    if i - LAG == EARLY:
                        proj_low(FIRST_Q, qh[0], ql[0])
                        proj_low(SECOND_Q, qh[1], ql[1])
                dve.wait_ge(R.xn_turned, NT)
                for t in range(3):
                    masked_max(t, t, 0, t + 1)
                for t in range(2):
                    normalise(t, t, 0, t + 4)

                def body(g, which):
                    for ul, b, h, pair, u, i, left in units(g, which):
                        nb = (ul + 1) // HPG % B
                        links = 5 + 2 * i
                        has_pv = not (which == "first" and ul == 0)
                        has_output = not (which == "first" and ul < HPG)
                        ob = (b - 1) % B
                        masked_max(i + 3, 3, b, links + 1)
                        normalise(i + 2, 2, b, links + 2)
                        turned_low(i, 0)
                        if has_pv:
                            proj_low(last_pv(pair, h, left < 2), o_hi[out_buf(b, 1 - h)], o_lo[out_buf(b, 1 - h)])
                        if ul == UNITS - 2 and which != "last":
                            split_qk(g + 1)
                        if left >= 1:
                            masked_max(i + 4, 0, nb, links + 3)
                        normalise(i + 3, 3, b, links + (4 if left >= 1 else 3))
                        turned_low(i + 1, 1)
                        if h == 0:
                            dve.wait_ge(M.proj_hi, this_v(pair).n + 1)
                            dve.sem_inc(M.proj_ready, 1)
                        if has_output and h == 1:
                            add_x(pair - 1, ob, 2)
                        if left >= 1:
                            masked_max(i + 5, 1, nb, links + 5)
                            normalise(i + 4, 0, nb, links + 6)
                        turned_low(i + 2, 2)
                        if h == 0:
                            dve.wait_ge(M.v_hi, pair + 1)
                            dve.tensor_tensor(vl[:], psO[1][:], f32(vh[:]), ALU.subtract).then_inc(M.v_ready, 1)
                        if has_output:
                            add_x(pair - 1, ob, 3 if h else 0)
                        if ul == UNITS - 2 and which != "last":
                            split_v(g + 1)
                        if left >= 1:
                            masked_max(i + 6, 2, nb, links + 7)
                            normalise(i + 5, 1, nb, links + 8)
                        turned_low(i + 3, 3)
                        if left >= 2:
                            proj_low(next_q(pair, h), qh[h], ql[h])
                        if has_output and h == 0:
                            add_x(pair - 1, ob, 1)
                        if left >= 2 and h == 0:
                            proj_low(next_k(pair), kh[(b + 1) % 2], kl[(b + 1) % 2])
                        if ul == 1:
                            split_o(g)

                groups(dve, body)
                proj_low(FINAL_PV, o_hi[out_buf(B - 1, 1)], o_lo[out_buf(B - 1, 1)])
                for tt in range(TT):
                    add_x(GROUPS * B - 1, B - 1, tt)

            @block.tensor
            def _(pe):
                def wq(h, k):
                    c = slice(k * HPG * D + h * D, k * HPG * D + (h + 1) * D)
                    return qkvh[:, c], qkvl[:, c]

                def wkv(j, k):
                    c = slice(NQ + (j * KV + k) * D, NQ + (j * KV + k + 1) * D)
                    return qkvh[:, c], qkvl[:, c]

                def bank_free(at):
                    at_least(pe, M.proj_ready, at.n - 1)

                def query(at, b, h, ks):
                    for k in ks:
                        tok = slice(b * S, (b + 1) * S)
                        last = product(pe, psP[at.bank][:], wq(h, k), (R.xTh[:, k, tok], R.xTl[:, k, tok]),
                                       k == 0, k == KC - 1)
                        if k == KC - 1:
                            last.then_inc(M.proj_done, 1)

                def key(at):
                    for k in range(KV):
                        last = product(pe, psP[at.bank][:], wkv(0, k), (ctxh[:, k, :], ctxl[:, k, :]), k == 0, k == KV - 1)
                    last.then_inc(M.proj_done, 1)

                def value(at):
                    for k in range(KV):
                        last = product(pe, psP[at.bank][:], wkv(1, k), (ctxh[:, k, :], ctxl[:, k, :]), k == 0, k == KV - 1)
                    last.then_inc(M.proj_done, 1)

                def turn_value(at, pair):
                    pe.wait_ge(M.proj_hi, at.n + 1)
                    at_least(pe, M.x_added, (pair - 1) * TT)
                    for st in range(TT):
                        last = pe.transpose(psO[1][:, st * P:(st + 1) * P], vT[:, st * P:(st + 1) * P], ident)
                    last.then_inc(M.v_turned, 1)

                def scores(i, tt, q, k):
                    at_least(pe, M.max_ready, i - 1)
                    m = slice(tt * P, (tt + 1) * P)
                    product(pe, psS[tt % 2][:], (qh[q][:, m], ql[q][:, m]), (kh[k][:], kl[k][:]), True, True).then_inc(M.s_done, 1)

                def turn(i, tt):
                    pe.wait_ge(M.norm_ready, i + 1)
                    at_least(pe, M.pt_ready, i - 1)
                    for k in range(TT):
                        last = pe.transpose(psT[tt % 2][:, k * P:(k + 1) * P], prob[tt][:, k * P:(k + 1) * P], ident)
                    last.then_inc(M.p_turned, 1)

                def weighted(at, u):
                    pe.wait_ge(M.pt_ready, TT * (u + 1))
                    bank_free(at)
                    for st in range(TT):
                        s = slice(st * P, (st + 1) * P)
                        last = product(pe, psP[at.bank][:], (vh[:, s], vl[:, s]), (PTh[:, st, :], PTl[:, st, :]),
                                       st == 0, st == TT - 1)
                    last.then_inc(M.proj_done, 1)

                def output(pair, b, tt):
                    at_least(pe, M.x_added, pair * TT + tt - 1)
                    m = slice(tt * P, (tt + 1) * P)
                    for h in range(HPG):
                        o = out_buf(b, h)
                        last = product(pe, psO[tt % 2][:], (o_hi[o][:, m], o_lo[o][:, m]),
                                       (woh[:, h * C:(h + 1) * C], wol[:, h * C:(h + 1) * C]), h == 0, h == HPG - 1)
                    last.then_inc(M.o_done, 1)

                pe.wait_ge(M.wv_ready, 1)
                pe.wait_ge(M.ctx_ready, 1)
                key(FIRST_K)
                turn_x = ln_tensor(pe, R, ident, ln_bank)
                for t in range(NT):
                    if t >= 4:
                        pe.wait_ge(R.xT_ready, t - 3)
                    turn_x(t)
                    if t == EARLY - 1:
                        pe.wait_ge(R.xT_ready, TT)
                        query(FIRST_Q, 0, 0, range(KC))
                        bank_free(SECOND_Q)
                        query(SECOND_Q, 0, 1, range(KC))
                pe.wait_ge(R.xT_ready, NT)
                pe.wait_ge(M.proj_ready, SECOND_Q.n + 1)
                for t in range(3):
                    scores(t, t, 0, 0)

                def body(g, which):
                    for ul, b, h, pair, u, i, left in units(g, which):
                        nk = (ul + 1) // HPG % 2
                        has_pv = not (which == "first" and ul == 0)
                        has_output = not (which == "first" and ul < HPG)
                        ob = (b - 1) % B
                        qb = (b + 1) % B
                        nq = next_q(pair, h)
                        scores(i + 3, 3, h, b % 2)
                        turn(i, 0)
                        if has_pv:
                            if h == 1:
                                pe.wait_ge(M.v_ready, pair + 1)
                            weighted(last_pv(pair, h, left < 2), u - 1)
                        if left >= 1:
                            pe.wait_ge(M.proj_ready, (next_k(pair) if h == 1 else next_q(pair - 1, 1)).n + 1)
                            scores(i + 4, 0, 1 - h, nk)
                        turn(i + 1, 1)
                        if h == 0:
                            bank_free(this_v(pair))
                            value(this_v(pair))
                        if has_output and h == 1:
                            output(pair - 1, ob, 2)
                        if left >= 1:
                            scores(i + 5, 1, 1 - h, nk)
                        turn(i + 2, 2)
                        if left >= 2:
                            if ul == UNITS - 2:
                                pe.wait_ge(M.qk_ready, g + 2)
                            bank_free(nq)
                            query(nq, qb, h, range(0, KC // 2))
                        if has_output and h == 0:
                            pe.wait_ge(M.proj_ready, last_pv(pair, h, left < 2).n + 1)
                            if ul == HPG:
                                pe.wait_ge(M.wo_ready, g + 2)
                            output(pair - 1, ob, 0)
                        if h == 0:
                            turn_value(this_v(pair), pair)
                        if has_output and h == 1:
                            output(pair - 1, ob, 3)
                        if left >= 1:
                            scores(i + 6, 2, 1 - h, nk)
                        turn(i + 3, 3)
                        if left >= 2:
                            query(nq, qb, h, range(KC // 2, KC))
                        if has_output and h == 0:
                            pe.wait_ge(M.v_ready, pair + 1)
                            output(pair - 1, ob, 1)
                        if left >= 2 and h == 0:
                            pe.wait_ge(M.ctx_ready, pair + 2)
                            bank_free(next_k(pair))
                            key(next_k(pair))
                            if ul == UNITS - 2:
                                pe.wait_ge(M.wv_ready, g + 2)

                groups(pe, body)
                weighted(FINAL_PV, LASTU)
                pe.wait_ge(M.proj_ready, FINAL_PV.n + 1)
                for tt in range(TT):
                    output(GROUPS * B - 1, B - 1, tt)


def kernel(**inputs):
    import concourse.bacc as bacc
    from concourse.bass_utils import run_bass_kernel_spmd

    a = {k: np.asarray(v) for k, v in inputs.items()}

    def chunks_T(w):
        n = w.shape[0] // P
        return w.reshape(n, P, -1, P).transpose(0, 3, 2, 1).reshape(n, P, -1)

    shared_w = np.concatenate([
        chunks_T(a["L0_ffn_shared_fc1"]), chunks_T(a["L0_ffn_shared_fc2"]),
        a["L0_ffn_shared_proj"].T.reshape(F_SHARED // P, P, C)], axis=2)

    def expert_in(w):
        return w.reshape(E, F_MOE, KC, P).transpose(0, 3, 2, 1).reshape(E, P, KC * F_MOE)

    down = np.concatenate([a["L0_ffn_expert_proj"].transpose(0, 2, 1), np.zeros((E, FCH * P - F_MOE, C), np.float32)], axis=1)
    expert_w = np.concatenate([
        expert_in(a["L0_ffn_expert_fc1"]), expert_in(a["L0_ffn_expert_fc2"]),
        down.reshape(E, FCH, P, C).transpose(0, 2, 1, 3).reshape(E, P, FCH * C)], axis=2)
    router = np.concatenate([a["L0_ffn_gate_w"], a["L0_ffn_shared_gate_w"], np.zeros((1, C), np.float32)])

    def rows(w, per_group):
        return w.reshape(-1, P, GROUPS, per_group).transpose(2, 1, 0, 3).reshape(GROUPS, P, -1)

    h = np.ones((1, 1), np.float32)
    while h.shape[0] < P:
        h = np.block([[h, h], [h, -h]]).astype(np.float32)
    wsc = a["L1_ffn_Wscale_ug"].reshape(2, NF, P)
    arrays = {
        "x": a["x"],
        "ctxT": a["ctx_1024"].reshape(B, S, KV, P).transpose(0, 3, 2, 1),
        "mask": a["mask_BxS2_bf1"].view(np.uint8).reshape(B * S),
        "ident": np.eye(P, dtype=np.float32),
        "h128": h,
        "sums": np.stack([np.triu(np.ones((P, P), np.float32), 1), np.ones((P, P), np.float32)], axis=1),
        "route_consts": np.concatenate([np.tril(np.ones((E, E)), -1).ravel(), np.arange(E) * SLOTS,
                                        np.arange(TILES)]).astype(np.float32),
        "ca_w": np.stack([chunks_T(a["L0_xattn_Wq"])[0], chunks_T(a["L0_xattn_Wk"])[0]], axis=1).reshape(P, 2, KV, D),
        "ca_b": np.stack([a["L0_xattn_bq"], a["L0_xattn_bk"]], axis=1),
        "shared_w": shared_w,
        "expert_w": expert_w,
        "router": router.reshape(RG, KC, P).transpose(2, 1, 0),
        "xa_w": np.concatenate([
            rows(a["L1_xattn_Wq"], HPG * D), rows(a["L1_xattn_Wk"], D), rows(a["L1_xattn_Wv"], D),
            a["L1_xattn_Wo"].reshape(GROUPS, HPG, D, C).transpose(0, 2, 1, 3).reshape(GROUPS, D, HPG * C)], axis=2),
        "ffn_w": np.concatenate([chunks_T(a["L1_ffn_W_gate"]), chunks_T(a["L1_ffn_W_up"])], axis=2),
        "wdT": a["L1_ffn_W_down"].T.reshape(NF, P, C),
        "wscale_dp": a["L1_ffn_Wscale_dp"],
        "su_ug": a["L1_ffn_SU_ug"],
        "ffn_tables": np.stack([wsc[0].T, wsc[1].T, a["L1_ffn_SU_dp"].reshape(NF, P).T], axis=1),
    }
    arrays = {f"in_{k}": np.ascontiguousarray(v) for k, v in arrays.items()}
    nc = bacc.Bacc("TRN2", target_bir_lowering=False, num_devices=1)
    io = {k[3:]: nc.dram_tensor(k, v.shape, mybir.dt.from_np(v.dtype), kind="ExternalInput").ap() for k, v in arrays.items()}
    io["out"] = nc.dram_tensor("out", (B, S, C), F32, kind="ExternalOutput").ap()
    program(nc, io)
    result = run_bass_kernel_spmd(nc, [arrays], core_ids=[0])
    return result.results[0]["out"]
```
